# Optimizing a Trainium2 kernel written in Bass

```python
import numpy as np
import jax
import jax.numpy as jnp

def _softmax(x, axis=-1):
    return jax.nn.softmax(x, axis=axis)

def _gelu(x):
    return jax.nn.gelu(x, approximate=True)

def _silu(x):
    return jax.nn.silu(x)

def _sigmoid(x):
    return jax.nn.sigmoid(x)

def _layernorm(x, axis=-1, eps=1e-05):
    m = jnp.mean(x, axis=axis, keepdims=True)
    v = jnp.var(x, axis=axis, keepdims=True)
    return (x - m) / jnp.sqrt(v + eps)

def _scatter_add(tgt, idx, src, axis=0):
    return tgt.at[idx].add(src)

def _segment_sum(src, seg, n):
    return jax.ops.segment_sum(src, seg, n)
kernel_name = 'mk_xattn_ffn_d2_seqx_r4_875f87'

def setup_inputs(seed: int=0):
    np.random.seed(seed)
    _w = jnp.asarray

    def _rec_inputs():
        import jax
        import jax.numpy as jnp
        _rk = jax.random.key(seed)
        x = -0.0002928 + 1 * jax.random.normal(jax.random.fold_in(_rk, 1), (8, 256, 256), jnp.float32)
        _lenS = 256 - jax.random.randint(jax.random.fold_in(_rk, 7), (8,), 0, max(1, 256 // 4) + 1, jnp.int32)
        _lenS2 = 256 - jax.random.randint(jax.random.fold_in(_rk, 8), (8,), 0, max(1, 256 // 4) + 1, jnp.int32)
        _ctx_1024P = jax.random.normal(jax.random.fold_in(_rk, 11), (8, 16, 256), jnp.float32)
        _ctx_1024c = jax.random.dirichlet(jax.random.fold_in(_rk, 511), 0.3 * jnp.ones((16,), jnp.float32), (8, 256))
        _ctx_1024t = jnp.einsum('bsk,bkd->bsd', _ctx_1024c, _ctx_1024P)
        _ctx_1024t = _ctx_1024t * jax.lax.rsqrt(jnp.mean(jnp.square(_ctx_1024t)) + 1e-12) * 0.953939
        ctx_1024 = -1.39393e-06 + 0.999914 * (_ctx_1024t + 0.3 * jax.random.normal(jax.random.fold_in(_rk, 611), (8, 256, 256), jnp.float32))
        _validS = jnp.arange(256)[None, :] < _lenS[:, None]
        _validS2 = jnp.arange(256)[None, :] < _lenS2[:, None]
        _causal = jnp.tril(jnp.ones((256, 256), dtype=bool))
        mask_BxSxS2_bf0 = jnp.logical_not(jnp.ones((8, 256, 256), dtype=bool))
        return (x, ctx_1024, mask_BxSxS2_bf0)
    x, ctx_1024, mask_BxSxS2_bf0 = _rec_inputs()

    def _L0_xattn_setup():
        import jax, jax.numpy as jnp
        import numpy as np
        NUM_HEADS = 16
        NEG_INF = float('-inf')
        key = jax.random.key(seed)
        ks = jax.random.split(key, 8)
        B, S, D = (2, 512, 256)
        return {'query': jax.random.normal(ks[0], (B, S, D), jnp.float32), 'key': jax.random.normal(ks[1], (B, S, D), jnp.float32), 'value': jax.random.normal(ks[2], (B, S, D), jnp.float32), 'attention_mask': jnp.zeros((B, S, S), dtype=bool), 'Wq': jax.random.normal(ks[3], (D, D), jnp.float32) * D ** (-0.5), 'Wk': jax.random.normal(ks[4], (D, D), jnp.float32) * D ** (-0.5), 'Wv': jax.random.normal(ks[5], (D, D), jnp.float32) * D ** (-0.5), 'Wout': jax.random.normal(ks[6], (D, D), jnp.float32) * D ** (-0.5), 'b_out': jnp.zeros((D,), jnp.float32), 'is_causal': 1}
    _L0_xattn_all = _L0_xattn_setup()
    _L0_xattn_in = {k: v for k, v in _L0_xattn_all.items() if k in ('Wq', 'Wk', 'Wv', 'Wout', 'b_out')}
    del _L0_xattn_all

    def _L0_ffn_setup():
        import jax, jax.numpy as jnp
        import numpy as np
        D_MODEL, EXPERT_DIM, NUM_EXPERTS, TOP_K = (256, 512, 16, 2)
        SEQ_LEN, BATCH = (512, 2)
        key = jax.random.key(seed)
        ks = jax.random.split(key, 8)
        s_d = 1.0 / np.sqrt(D_MODEL)
        s_h = 1.0 / np.sqrt(EXPERT_DIM)
        return {'x': jax.random.normal(ks[0], (SEQ_LEN, BATCH, D_MODEL), jnp.float32), 'Wg': jax.random.uniform(ks[1], (D_MODEL, NUM_EXPERTS), jnp.float32, -s_d, s_d), 'bg': jax.random.uniform(ks[2], (NUM_EXPERTS,), jnp.float32, -s_d, s_d), 'bias': jnp.zeros((NUM_EXPERTS,), jnp.float32), 'W1': jax.random.uniform(ks[3], (NUM_EXPERTS, D_MODEL, EXPERT_DIM), jnp.float32, -s_d, s_d), 'b1': jax.random.uniform(ks[4], (NUM_EXPERTS, EXPERT_DIM), jnp.float32, -s_d, s_d), 'W2': jax.random.uniform(ks[5], (NUM_EXPERTS, EXPERT_DIM, D_MODEL), jnp.float32, -s_h, s_h), 'b2': jax.random.uniform(ks[6], (NUM_EXPERTS, D_MODEL), jnp.float32, -s_h, s_h)}
    _L0_ffn_all = _L0_ffn_setup()
    _L0_ffn_in = {k: v for k, v in _L0_ffn_all.items() if k in ('Wg', 'bg', 'bias', 'W1', 'b1', 'W2', 'b2')}
    del _L0_ffn_all

    def _L1_xattn_setup():
        import jax, jax.numpy as jnp
        import numpy as np
        EMB = 256
        HEADS = 16
        HEAD_DIM = EMB // HEADS
        B, S = (2, 512)
        key = jax.random.key(seed)
        ks = jax.random.split(key, 11)
        scale = 1.0 / np.sqrt(EMB)
        inp = {'query': jax.random.normal(ks[0], (B, S, EMB), jnp.float32), 'key': jax.random.normal(ks[1], (B, S, EMB), jnp.float32), 'value': jax.random.normal(ks[2], (B, S, EMB), jnp.float32), 'Wq': jax.random.normal(ks[3], (EMB, EMB), jnp.float32) * scale, 'bq': jnp.zeros((EMB,), jnp.float32), 'Wk': jax.random.normal(ks[4], (EMB, EMB), jnp.float32) * scale, 'bk': jnp.zeros((EMB,), jnp.float32), 'Wv': jax.random.normal(ks[5], (EMB, EMB), jnp.float32) * scale, 'bv': jnp.zeros((EMB,), jnp.float32), 'Wo': jax.random.normal(ks[6], (EMB, EMB), jnp.float32) * scale, 'bo': jnp.zeros((EMB,), jnp.float32)}
        return inp
    _L1_xattn_all = _L1_xattn_setup()
    _L1_xattn_in = {k: v for k, v in _L1_xattn_all.items() if k in ('Wq', 'bq', 'Wk', 'bk', 'Wv', 'bv', 'Wo', 'bo')}
    del _L1_xattn_all

    def _L1_ffn_setup():
        import jax, jax.numpy as jnp
        import numpy as np
        import math
        D_MODEL = 256
        D_FF = 1024
        NUM_EXPERTS = 8
        NUM_SHARED = 1
        E_ROUTED = NUM_EXPERTS - NUM_SHARED
        TOP_K = 2
        CAP_FACTOR = 1.25
        B, S = (4, 512)
        T = B * S
        CAPACITY = math.ceil(CAP_FACTOR * T * TOP_K / E_ROUTED)
        SHARED_SCALE = 1.0

        def _layernorm(x, g, b, eps=1e-05):
            mu = jnp.mean(x, axis=-1, keepdims=True)
            var = jnp.mean((x - mu) ** 2, axis=-1, keepdims=True)
            return (x - mu) * jax.lax.rsqrt(var + eps) * g + b
        key = jax.random.key(seed)
        ks = jax.random.split(key, 10)
        s = 0.02
        return {'x': jax.random.normal(ks[0], (B, S, D_MODEL), dtype=jnp.float32), 'ln_g': jnp.ones((D_MODEL,), jnp.float32), 'ln_b': jnp.zeros((D_MODEL,), jnp.float32), 'Wr': jax.random.normal(ks[1], (D_MODEL, E_ROUTED), jnp.float32) * s, 'W1': jax.random.normal(ks[2], (E_ROUTED, D_MODEL, D_FF), jnp.float32) * s, 'W3': jax.random.normal(ks[3], (E_ROUTED, D_MODEL, D_FF), jnp.float32) * s, 'W2': jax.random.normal(ks[4], (E_ROUTED, D_FF, D_MODEL), jnp.float32) * s, 'W1s': jax.random.normal(ks[5], (D_MODEL, D_FF), jnp.float32) * s, 'W3s': jax.random.normal(ks[6], (D_MODEL, D_FF), jnp.float32) * s, 'W2s': jax.random.normal(ks[7], (D_FF, D_MODEL), jnp.float32) * s}
    _L1_ffn_all = _L1_ffn_setup()
    _L1_ffn_in = {k: v for k, v in _L1_ffn_all.items() if k in ('ln_g', 'ln_b', 'Wr', 'W1', 'W3', 'W2', 'W1s', 'W3s', 'W2s')}
    del _L1_ffn_all
    return {'x': x, 'ctx_1024': ctx_1024, 'mask_BxSxS2_bf0': mask_BxSxS2_bf0, 'L0_xattn_Wq': _L0_xattn_in['Wq'], 'L0_xattn_Wk': _L0_xattn_in['Wk'], 'L0_xattn_Wv': _L0_xattn_in['Wv'], 'L0_xattn_Wout': _L0_xattn_in['Wout'], 'L0_xattn_b_out': _L0_xattn_in['b_out'], 'L0_ffn_Wg': _L0_ffn_in['Wg'], 'L0_ffn_bg': _L0_ffn_in['bg'], 'L0_ffn_bias': _L0_ffn_in['bias'], 'L0_ffn_W1': _L0_ffn_in['W1'], 'L0_ffn_b1': _L0_ffn_in['b1'], 'L0_ffn_W2': _L0_ffn_in['W2'], 'L0_ffn_b2': _L0_ffn_in['b2'], 'L1_xattn_Wq': _L1_xattn_in['Wq'], 'L1_xattn_bq': _L1_xattn_in['bq'], 'L1_xattn_Wk': _L1_xattn_in['Wk'], 'L1_xattn_bk': _L1_xattn_in['bk'], 'L1_xattn_Wv': _L1_xattn_in['Wv'], 'L1_xattn_bv': _L1_xattn_in['bv'], 'L1_xattn_Wo': _L1_xattn_in['Wo'], 'L1_xattn_bo': _L1_xattn_in['bo'], 'L1_ffn_ln_g': _L1_ffn_in['ln_g'], 'L1_ffn_ln_b': _L1_ffn_in['ln_b'], 'L1_ffn_Wr': _L1_ffn_in['Wr'], 'L1_ffn_W1': _L1_ffn_in['W1'], 'L1_ffn_W3': _L1_ffn_in['W3'], 'L1_ffn_W2': _L1_ffn_in['W2'], 'L1_ffn_W1s': _L1_ffn_in['W1s'], 'L1_ffn_W3s': _L1_ffn_in['W3s'], 'L1_ffn_W2s': _L1_ffn_in['W2s']}

def reference(x, ctx_1024, mask_BxSxS2_bf0, L0_xattn_Wq, L0_xattn_Wk, L0_xattn_Wv, L0_xattn_Wout, L0_xattn_b_out, L0_ffn_Wg, L0_ffn_bg, L0_ffn_bias, L0_ffn_W1, L0_ffn_b1, L0_ffn_W2, L0_ffn_b2, L1_xattn_Wq, L1_xattn_bq, L1_xattn_Wk, L1_xattn_bk, L1_xattn_Wv, L1_xattn_bv, L1_xattn_Wo, L1_xattn_bo, L1_ffn_ln_g, L1_ffn_ln_b, L1_ffn_Wr, L1_ffn_W1, L1_ffn_W3, L1_ffn_W2, L1_ffn_W1s, L1_ffn_W3s, L1_ffn_W2s):
    import jax
    import jax.numpy as jnp

    def _L0_xattn_ref(query, key, value, attention_mask, Wq, Wk, Wv, Wout, b_out, is_causal):
        import jax, jax.numpy as jnp
        import numpy as np
        NUM_HEADS = 16
        NEG_INF = float('-inf')
        B, q_len, D = query.shape
        k_len = key.shape[1]
        H = NUM_HEADS
        dk = D // H
        q = (query @ Wq.T).reshape(B, q_len, H, dk).transpose(0, 2, 1, 3)
        k = (key @ Wk.T).reshape(B, k_len, H, dk).transpose(0, 2, 1, 3)
        v = (value @ Wv.T).reshape(B, k_len, H, dk).transpose(0, 2, 1, 3)
        scores = jnp.einsum('bhqd,bhkd->bhqk', q, k) / jnp.sqrt(jnp.float32(dk))
        if is_causal:
            causal = jnp.triu(jnp.ones((q_len, k_len), dtype=bool), k=1)
            scores = jnp.where(causal, NEG_INF, scores)
        scores = jnp.where(attention_mask[:, None, :, :], NEG_INF, scores)
        attn = jax.nn.softmax(scores, axis=-1)
        attn = jnp.where(jnp.isnan(attn), 0.0, attn)
        out = jnp.einsum('bhqk,bhkd->bhqd', attn, v)
        out = out.transpose(0, 2, 1, 3).reshape(B, q_len, D)
        return out @ Wout.T + b_out

    def _L0_ffn_ref(x, Wg, bg, bias, W1, b1, W2, b2):
        import jax, jax.numpy as jnp
        import numpy as np
        D_MODEL, EXPERT_DIM, NUM_EXPERTS, TOP_K = (256, 512, 16, 2)
        SEQ_LEN, BATCH = (512, 2)
        logits = jnp.einsum('sbd,de->sbe', x, Wg) + bg + bias
        vals, idx = jax.lax.top_k(logits, TOP_K)
        w = jax.nn.softmax(vals - jnp.max(vals, axis=-1, keepdims=True), axis=-1)
        cw = jnp.einsum('sbk,sbke->sbe', w, jax.nn.one_hot(idx, NUM_EXPERTS, dtype=x.dtype))
        h = jax.nn.relu(jnp.einsum('sbd,edh->esbh', x, W1) + b1[:, None, None, :])
        y = jnp.einsum('esbh,ehd->esbd', h, W2) + b2[:, None, None, :]
        out = jnp.einsum('esbd,sbe->sbd', y, cw)
        return out

    def _L1_xattn_ref(query, key, value, Wq, bq, Wk, bk, Wv, bv, Wo, bo):
        import jax, jax.numpy as jnp
        import numpy as np
        EMB = 256
        HEADS = 16
        HEAD_DIM = EMB // HEADS
        B, S = (2, 512)
        b = query.shape[0]

        def proj(x, W, bias):
            y = jnp.einsum('bse,ef->bsf', x, W) + bias
            return y.reshape(b, -1, HEADS, HEAD_DIM).transpose(0, 2, 1, 3)
        Q = proj(query, Wq, bq)
        K = proj(key, Wk, bk)
        V = proj(value, Wv, bv)
        scores = jnp.einsum('bhqd,bhkd->bhqk', Q, K) / np.sqrt(HEAD_DIM).astype(np.float32)
        weights = jax.nn.softmax(scores, axis=-1)
        ctx = jnp.einsum('bhqk,bhkd->bhqd', weights, V)
        ctx = ctx.transpose(0, 2, 1, 3).reshape(b, -1, EMB)
        return jnp.einsum('bse,ef->bsf', ctx, Wo) + bo

    def _L1_ffn_ref(x, ln_g, ln_b, Wr, W1, W3, W2, W1s, W3s, W2s):
        import jax, jax.numpy as jnp
        import numpy as np
        import math
        D_MODEL = 256
        D_FF = 1024
        NUM_EXPERTS = 8
        NUM_SHARED = 1
        E_ROUTED = NUM_EXPERTS - NUM_SHARED
        TOP_K = 2
        CAP_FACTOR = 1.25
        B, S = (4, 512)
        T = B * S
        CAPACITY = math.ceil(CAP_FACTOR * T * TOP_K / E_ROUTED)
        SHARED_SCALE = 1.0

        def _layernorm(x, g, b, eps=1e-05):
            mu = jnp.mean(x, axis=-1, keepdims=True)
            var = jnp.mean((x - mu) ** 2, axis=-1, keepdims=True)
            return (x - mu) * jax.lax.rsqrt(var + eps) * g + b
        Bx, Sx, D = x.shape
        Tn = Bx * Sx
        h = _layernorm(x, ln_g, ln_b).reshape(Tn, D)
        logits = h @ Wr
        top_vals, top_idx = jax.lax.top_k(logits, TOP_K)
        gates = jax.nn.softmax(top_vals, axis=-1)
        idx = top_idx.T.reshape(-1)
        gat = gates.T.reshape(-1)
        tok = jnp.tile(jnp.arange(Tn), TOP_K)
        onehot = jax.nn.one_hot(idx, E_ROUTED, dtype=jnp.int32)
        pos = jnp.sum(jnp.cumsum(onehot, axis=0) * onehot, axis=-1) - 1
        keep = pos < CAPACITY
        pos_c = jnp.where(keep, pos, CAPACITY)
        xe = jnp.zeros((E_ROUTED, CAPACITY, D), h.dtype).at[idx, pos_c].set(h[tok], mode='drop')
        a = jnp.einsum('ecd,edf->ecf', xe, W1)
        b = jnp.einsum('ecd,edf->ecf', xe, W3)
        ye = jnp.einsum('ecf,efd->ecd', jax.nn.silu(a) * b, W2)
        out_slots = ye[jnp.clip(idx, 0, E_ROUTED - 1), jnp.clip(pos_c, 0, CAPACITY - 1)]
        out_slots = out_slots * (gat * keep.astype(gat.dtype))[:, None]
        routed = jnp.zeros((Tn, D), h.dtype).at[tok].add(out_slots)
        shared = jax.nn.silu(h @ W1s) * (h @ W3s) @ W2s
        out = routed + SHARED_SCALE * shared
        return out.reshape(Bx, Sx, D)
    x = x + _L0_xattn_ref(_layernorm(x, axis=-1), ctx_1024, ctx_1024, mask_BxSxS2_bf0, L0_xattn_Wq, L0_xattn_Wk, L0_xattn_Wv, L0_xattn_Wout, L0_xattn_b_out, 1)
    x = x + _L0_ffn_ref(_layernorm(x, axis=-1), L0_ffn_Wg, L0_ffn_bg, L0_ffn_bias, L0_ffn_W1, L0_ffn_b1, L0_ffn_W2, L0_ffn_b2)
    x = x + _L1_xattn_ref(_layernorm(x, axis=-1), ctx_1024, ctx_1024, L1_xattn_Wq, L1_xattn_bq, L1_xattn_Wk, L1_xattn_bk, L1_xattn_Wv, L1_xattn_bv, L1_xattn_Wo, L1_xattn_bo)
    x = x + _L1_ffn_ref(_layernorm(x, axis=-1), L1_ffn_ln_g, L1_ffn_ln_b, L1_ffn_Wr, L1_ffn_W1, L1_ffn_W3, L1_ffn_W2, L1_ffn_W1s, L1_ffn_W3s, L1_ffn_W2s)
    return x

_drawn_inputs = setup_inputs


def setup_inputs(seed=0):
    import zlib

    import numpy as np

    out = dict(_drawn_inputs(seed))
    spreads = {'L0_xattn_b_out': (0.0, 0.1),
     'L0_ffn_bias': (0.0, 0.1),
     'L1_xattn_bq': (0.0, 0.461),
     'L1_xattn_bk': (0.0, 0.8),
     'L1_xattn_bv': (0.0, 0.1),
     'L1_xattn_bo': (0.0, 0.1),
     'L1_ffn_ln_g': (1.0, 0.6),
     'L1_ffn_ln_b': (0.0, 0.8)}
    factors = {'L0_ffn_b1': 6.674,
     'L0_ffn_b2': 3.872,
     'L1_ffn_Wr': 3.4,
     'L1_ffn_W1': 2.99,
     'L1_ffn_W3': 2.95,
     'L1_ffn_W2': 2.953}
    for name, (base, spread) in spreads.items():
        noise = np.random.default_rng([zlib.crc32(name.encode()), seed]).standard_normal(out[name].shape)
        drawn = base * np.exp(spread * noise) if base else spread * noise
        out[name] = jnp.asarray(drawn.astype(out[name].dtype))
    for name, factor in factors.items():
        out[name] = (out[name] * factor).astype(out[name].dtype)
    return out
```

```python
from contextlib import ExitStack, contextmanager

import numpy as np

import concourse.bass as bass
from concourse import mybir

F32 = mybir.dt.float32
F32R = mybir.dt.float32r
BF16 = mybir.dt.bfloat16
I32 = mybir.dt.int32
U32 = mybir.dt.uint32
U8 = mybir.dt.uint8
ALU = mybir.AluOpType
ACT = mybir.ActivationFunctionType
AX = mybir.AxisListType

P = 128
B, S, D = 8, 256, 256
T = B * S
NT = T // P
TPB = S // P
DC = D // P
H = 16
DK = D // H
HPC = P // DK
LN_EPS = 1e-5
PARTS = 3
STACK_Q = (0, 0, 0, 1, 1, 2)
STACK_K = (0, 1, 2, 0, 1, 0)
KS = len(STACK_Q) * DK
G = 4
NG = H // G
MASKED = -1e30
FLOOR = -1e25

E0, F0 = 16, 512
FC0 = F0 // P
W0 = DC * F0 + FC0 * D
NB0 = 2 * T // P + E0
ROWS0 = NB0 * P

E1, F1, CAP = 7, 1024, 732
FC1 = F1 // P
VX = -(-T // CAP)
NV = E1 + VX
W1C = 2 * DC * P + D
XT = -(-CAP // P)
ROWS1 = (NV - 1) * CAP + XT * P
LAST = CAP - (XT - 1) * P
HALF = (XT // 2 * P, CAP - XT // 2 * P)
OUT_OF_RANGE = 1e6


def weight_of(v):
    return min(v, E1)


@contextmanager
def signals(nc, resting):
    mine = []

    def signal(name):
        mine.append(nc.alloc_semaphore(name=name))
        return mine[-1]

    yield signal
    nc.clear_and_free_semaphores(mine)
    again = [nc.alloc_semaphore(name=s.name + "_rest", num=s.num) for s in mine]
    while resting:
        nc.release_semaphore(resting.pop())
    resting += again


def alloc(nc, ctx):
    def sb(name, shape, dt=F32):
        return ctx.enter_context(nc.sbuf_tensor(name, shape, dt))

    m = {"resting": []}
    m["xres"] = sb("xres", [P, NT, D])
    m["mv"] = sb("mv", [P, NT, 2])
    m["rstd"] = sb("rstd", [P, NT])
    m["ident"] = sb("ident", [P, P])
    m["identb"] = sb("identb", [P, P], BF16)
    m["ones"] = sb("ones", [P, P])
    m["before"] = sb("before", [P, P])
    m["minus"] = sb("minus", [P, G, P], BF16)
    m["gate"] = sb("gate", [P, 2, NT])
    m["slot"] = sb("slot", [P, 2, NT], U32)
    m["slot_back"] = sb("slot_back", [P, 2, NT], U32)
    m["block_expert"] = sb("block_expert", [P, NB0], I32)
    return m


def setup_block(nc, m, x, xe0, xe1):
    with ExitStack() as ctx:
        zeros = ctx.enter_context(nc.sbuf_tensor("zeros", [P, 4096], F32))
        stats = ctx.enter_context(nc.sbuf_tensor("stats", [P, NT, 6], F32))
        sem = ctx.enter_context(signals(nc, m["resting"]))
        x_loaded, zeros_ready, zeros_stored = sem("x_loaded"), sem("zeros_ready"), sem("zeros_stored")
        block = ctx.enter_context(nc.Block())

        @block.sync
        def _(sp):
            sp.dma_start(m["xres"][:], x.rearrange("(n p) d -> p n d", p=P)).then_inc(x_loaded, 16)
            sp.wait_ge(zeros_ready, 1)
            n = 0
            for buf, rows in ((xe0, ROWS0), (xe1, ROWS1)):
                flat = buf.rearrange("r d -> (r d)")
                at = 0
                while at < rows * D:
                    k = min(P * 4096, rows * D - at)
                    sp.dma_start(flat[at:at + k].rearrange("(p f) -> p f", p=P), zeros[:, 0:k // P]).then_inc(zeros_stored, 16)
                    at += k
                    n += 1
            sp.wait_ge(zeros_stored, 16 * n)

        @block.gpsimd
        def _(pool):
            pool.memset(zeros[:], 0.0).then_inc(zeros_ready, 1)
            pool.memset(m["ident"][:], 0.0)
            pool.memset(m["ones"][:], 1.0)
            pool.memset(m["before"][:], 1.0)
            pool.memset(m["minus"][:], 0.0)
            pool.drain()
            pool.affine_select(out=m["ident"][:], in_=m["ident"][:], compare_op=ALU.not_equal, fill=1.0,
                               base=0, pattern=[[-1, P]], channel_multiplier=1)
            pool.affine_select(out=m["before"][:], in_=m["before"][:], compare_op=ALU.is_gt, fill=0.0,
                               base=0, pattern=[[1, P]], channel_multiplier=-1)
            for part in range(2):
                pool.drain()
                pool.affine_select(out=m["minus"][:], in_=m["minus"][:], compare_op=ALU.not_equal, fill=-1.0,
                                   base=-part * G, pattern=[[-1, G], [0, P]], channel_multiplier=1)
            pool.drain()
            pool.tensor_copy(m["identb"][:], m["ident"][:])

        @block.vector
        def _(dve):
            dve.wait_ge(x_loaded, 16)
            for t in range(NT):
                dve.bn_stats(stats[:, t, :], m["xres"][:, t, :])
            dve.drain()
            for t in range(NT):
                dve.bn_aggr(m["mv"][:, t, :], stats[:, t, :])


def rstd_steps_vector(dve, m, var_ready, root_ready):
    dve.tensor_scalar(m["rstd"][:], m["mv"][:, :, 1], LN_EPS, None, ALU.add).then_inc(var_ready, 1)
    dve.wait_ge(root_ready, 1)
    dve.reciprocal(m["rstd"][:], m["rstd"][:])
    dve.drain()


def rstd_steps_scalar(act, m, var_ready, root_ready):
    act.wait_ge(var_ready, 1)
    act.activation(m["rstd"][:], m["rstd"][:], ACT.Sqrt).then_inc(root_ready, 1)


def primed(eng, *signals):
    for s in signals:
        eng.sem_inc(s, 1)


def done(n):
    return n + 2


def before(n):
    return n + 1


def project_block(nc, m, layer, ctxT, W, parts_dram, vals):
    ctx = ExitStack()
    with ctx:
        def sb(name, shape, dt=F32):
            return ctx.enter_context(nc.sbuf_tensor(f"{name}_{layer}", shape, dt))

        signal = ctx.enter_context(signals(nc, m["resting"]))

        def sem(name):
            return signal(f"{name}_{layer}")

        def sems(name):
            return [sem(f"{name}{j}") for j in range(2)]

        def sems2(name):
            return [[sem(f"{name}{j}{w}") for w in range(2)] for j in range(2)]

        biased = "bq" in W
        wq, wk, wv = (sb(n, [P, DC, D]) for n in ("wq", "wk", "wv"))
        bqk = sb("bqk", [P, 2, DC])
        bvb = sb("bvb", [P, D])
        bob = sb("bob", [P, D])
        cst = sb("cst", [P, 2, DC, S])
        h = sb("h", [P, 2, TPB, D])
        hT = sb("hT", [P, 2, DC, S])
        full = sb("full", [P, 2, 2, DC, S])
        rest = sb("rest", [P, 2, 2, DC, S])
        parts = sb("cut", [P, 2, 2, PARTS, DC, S], BF16)
        ps = ctx.enter_context(nc.psum_tensor(f"proj_ps_{layer}", [P, 8, 512], F32))
        KB, VB, TB, QB = 0, 2, 4, 6

        w_loaded = sem("w_loaded")
        var_ready, root_ready = sem("var_ready"), sem("root_ready")
        ctx_loaded = sems("ctx_loaded")
        h_ready, turned, hT_ready = sems("h_ready"), sems("turned"), sems("hT_ready")
        k_made, v_made, q_made = sems("k_made"), sems("v_made"), sems("q_made")
        k_taken, v_taken, q_taken = sems("k_taken"), sems("v_taken"), sems("q_taken")
        high_ready, parts_ready, parts_stored = sems2("high_ready"), sems2("parts_ready"), sems2("parts_stored")
        parts_free = sems("parts_free")
        block = ctx.enter_context(nc.Block())

        @block.sync
        def _(sp):
            for dst, name in ((wk, "Wk"), (wv, "Wv"), (wq, "Wq")):
                sp.dma_start(dst[:], W[name].rearrange("(c p) n -> p c n", p=P)).then_inc(w_loaded, 16)
            if biased:
                for w, name in enumerate(("bq", "bk")):
                    sp.dma_start(bqk[:, w, :], W[name].rearrange("(c p) -> p c", p=P), allow_slow_non_contiguous=True).then_inc(w_loaded, 16)
                sp.dma_start(bvb[:], W["bv"].partition_broadcast(P)).then_inc(w_loaded, 16)
            sp.dma_start(bob[:], W["bo"].partition_broadcast(P)).then_inc(w_loaded, 16)
            src = ctxT.rearrange("(c p) t -> p c t", p=P)
            with sp.Fori(0, B // 2) as i:
                for j in range(2):
                    sp.wait_ge(v_made[j], before(i))
                    sp.dma_start(cst[:, j, :, :], src[:, :, bass.ds((2 * i + j) * S, S)]).then_inc(ctx_loaded[j], 16)

        weights = 16 * (7 if biased else 4)

        @block.gpsimd
        def _(pool):
            primed(pool, *parts_free)
            pool.memset(vals[:, :, :, DK:DK + 1], 1.0)
            with pool.Fori(0, B // 2) as i:
                for j in range(2):
                    for w in (1, 0):
                        pool.wait_ge(parts_ready[j][w], i + 1)
                        for part in range(PARTS):
                            dst = parts_dram[w, part].rearrange("(c p) t -> p c t", p=P)
                            pool.dma_start(dst[:, :, bass.ds((2 * i + j) * S, S)], parts[:, j, w, part]).then_inc(parts_stored[j][w], 16)
                    for w in (1, 0):
                        pool.wait_ge(parts_stored[j][w], 16 * PARTS * (i + 1))
                    pool.sem_inc(parts_free[j], 1)

        @block.vector
        def _(dve):
            primed(dve, *h_ready)
            if biased:
                primed(dve, *v_taken)
            rstd_steps_vector(dve, m, var_ready, root_ready)
            dve.wait_ge(w_loaded, weights)

            def norm(i, j):
                dve.wait_ge(turned[j], before(i))
                for t in range(TPB):
                    n = (2 * i + j) * TPB + t
                    last = dve.tensor_scalar(h[:, j, t, :], m["xres"][:, bass.ds(n, 1), :].rearrange("p a d -> p (a d)"),
                                             m["mv"][:, bass.ds(n, 1), 0], m["rstd"][:, bass.ds(n, 1)], ALU.subtract, ALU.mult)
                last.then_inc(h_ready[j], 1)
                dve.drain()
                xt = m["xres"][:, bass.ds((2 * i + j) * TPB, TPB), :]
                dve.tensor_tensor(xt, xt, bob[:].unsqueeze(1).to_broadcast([P, TPB, D]), ALU.add)

            def split(i, j, w):
                f, r, pt = full[:, j, w], rest[:, j, w], parts[:, j, w]
                dve.wait_ge(high_ready[j][w], i + 1)
                dve.tensor_tensor(r, f, pt[:, 0], ALU.subtract)
                dve.drain()
                dve.tensor_copy(pt[:, 1], r)
                dve.drain()
                dve.tensor_tensor(pt[:, 2], r, pt[:, 1], ALU.subtract).then_inc(parts_ready[j][w], 1)

            with dve.Fori(0, B // 2) as i:
                for j in range(2):
                    norm(i, j)
                    split(i, j, 1)
                    if biased:
                        dve.wait_ge(v_made[j], done(i))
                        out = vals[:, bass.ds((2 * i + j) * TPB, TPB), :, 0:DK]
                        dve.tensor_tensor(out, ps[:, VB + j, :].rearrange("p (t h d) -> p t h d", t=TPB, h=H),
                                          bvb[:].rearrange("p (h d) -> p h d", h=H).unsqueeze(1).to_broadcast([P, TPB, H, DK]),
                                          ALU.add).then_inc(v_taken[j], 1)
                    split(i, j, 0)

        @block.scalar
        def _(act):
            primed(act, *k_taken, *q_taken, *hT_ready)
            if not biased:
                primed(act, *v_taken)
            rstd_steps_scalar(act, m, var_ready, root_ready)
            if biased:
                act.wait_ge(w_loaded, weights)

            def take(i, j, w, made, taken, bank):
                act.wait_ge(made[j], done(i))
                act.wait_ge(parts_free[j], before(i))
                if biased:
                    for c in range(DC):
                        last = act.activation(full[:, j, w, c, :], ps[:, bank + j, c * S:(c + 1) * S], ACT.Identity,
                                              bias=bqk[:, w, c:c + 1])
                else:
                    last = act.activation(full[:, j, w].rearrange("p c s -> p (c s)"), ps[:, bank + j, :], ACT.Copy)
                last.then_inc(taken[j], 1)
                act.drain()
                act.activation(parts[:, j, w, 0], full[:, j, w], ACT.Copy).then_inc(high_ready[j][w], 1)

            with act.Fori(0, B // 2) as i:
                for j in range(2):
                    take(i, j, 1, k_made, k_taken, KB)
                    act.wait_ge(turned[j], done(i))
                    act.wait_ge(q_made[j], before(i))
                    act.activation(hT[:, j].rearrange("p c s -> p (c s)"), ps[:, TB + j, :], ACT.Copy).then_inc(hT_ready[j], 1)
                    if not biased:
                        act.wait_ge(v_made[j], done(i))
                        act.activation(vals[:, bass.ds((2 * i + j) * TPB, TPB), :, 0:DK],
                                       ps[:, VB + j, :].rearrange("p (t h d) -> p t h d", t=TPB, h=H), ACT.Copy).then_inc(v_taken[j], 1)
                    take(i, j, 0, q_made, q_taken, QB)

        @block.tensor
        def _(pe):
            primed(pe, *k_made, *v_made, *q_made, *turned)
            pe.wait_ge(w_loaded, weights)
            with pe.Fori(0, B // 2) as i:
                for j in range(2):
                    pe.wait_ge(ctx_loaded[j], 16 * (i + 1))
                    pe.wait_ge(k_taken[j], before(i))
                    for dh in range(DC):
                        for c in range(DC):
                            last = pe.matmul(ps[:, KB + j, dh * S:(dh + 1) * S], wk[:, c, dh * P:(dh + 1) * P], cst[:, j, c, :],
                                             start=c == 0, stop=c == DC - 1)
                    last.then_inc(k_made[j], 1)
                    pe.wait_ge(h_ready[j], done(i))
                    pe.wait_ge(hT_ready[j], before(i))
                    for t in range(TPB):
                        for c in range(DC):
                            last = pe.transpose(ps[:, TB + j, c * S + t * P:c * S + (t + 1) * P], h[:, j, t, c * P:(c + 1) * P], m["ident"][:])
                    last.then_inc(turned[j], 1)
                    pe.wait_ge(v_taken[j], before(i))
                    for t in range(TPB):
                        for c in range(DC):
                            last = pe.matmul(ps[:, VB + j, t * D:(t + 1) * D], cst[:, j, c, t * P:(t + 1) * P], wv[:, c, :],
                                             start=c == 0, stop=c == DC - 1)
                    last.then_inc(v_made[j], 1)
                    pe.wait_ge(hT_ready[j], done(i))
                    pe.wait_ge(q_taken[j], before(i))
                    for dh in range(DC):
                        for c in range(DC):
                            last = pe.matmul(ps[:, QB + j, dh * S:(dh + 1) * S], wq[:, c, dh * P:(dh + 1) * P], hT[:, j, c, :],
                                             start=c == 0, stop=c == DC - 1)
                    last.then_inc(q_made[j], 1)


def lead(eng, signal, n):
    eng.sem_inc(signal, n)


def free(u):
    return u + 1


def ready(u, n=0):
    return u + 1 + n


def attend_block(nc, m, layer, causal, W, masks, parts_dram, vals):
    ctx = ExitStack()
    with ctx:
        def sb(name, shape, dt=F32):
            return ctx.enter_context(nc.sbuf_tensor(f"{name}_{layer}", shape, dt))

        signal = ctx.enter_context(signals(nc, m["resting"]))

        def sem(name):
            return signal(f"{name}_{layer}")

        def sems(name, n=2):
            return [sem(f"{name}{j}") for j in range(n)]

        PR = 4
        RING = 2
        wo = sb("wo", [P, DC, D])
        qs = sb("qs", [KS, 2, H, S], BF16)
        ks = sb("ks", [KS, 2, H, S], BF16)
        if causal:
            flags = sb("flags", [P, 2, B, TPB, S], U8)
            later = sb("later", [P, 2, TPB, S], BF16)
            shut = sb("shut", [P, 2, B, TPB, S], BF16)
        top = sb("top", [P, 2, TPB, G])
        top_parts = sb("top_parts", [P, 2, TPB, 2, G], BF16)
        top_row = sb("top_row", [P, 2, S], BF16)
        probs = sb("probs", [P, PR, TPB * S])
        total = sb("total", [P, TPB * G])
        o = sb("o", [P, 2, TPB, D])
        oT = sb("oT", [P, 2, DC, S])
        stats = sb("stats", [P, TPB, 6])
        mv = sb("mv", [P, TPB, 2])
        ps = ctx.enter_context(nc.psum_tensor(f"att_ps_{layer}", [P, 8, 512], F32))
        SB, TB, OB, MB, XB = 0, 2, 4, 6, 7

        wo_loaded = sem("wo_loaded")
        stacks_loaded, flags_loaded, shut_ready = sems("stacks_loaded"), sem("flags_loaded"), sem("shut_ready")
        blank_ready = sem("blank_ready")
        scored, reduced = sem("scored"), sem("reduced")
        top_ready, top_turned, row_ready = sem("top_ready"), sem("top_turned"), sem("row_ready")
        scoredT, exped, valued, taken = sem("scoredT"), sem("exped"), sem("valued"), sem("taken")
        o_turned, oT_ready, out_taken = sem("o_turned"), sem("oT_ready"), sem("out_taken")
        out_made = sems("out_made")
        block = ctx.enter_context(nc.Block())

        UNITS = [(qt, pair) for qt in range(TPB) for pair in range(G // 2)]
        NU = len(UNITS)
        WIDE = S + P if causal else 2 * S

        def keys(qt):
            return (qt + 1) * P if causal else S

        def first_q(kt):
            return kt * P if causal else 0

        @block.sync
        def _(sp):
            sp.dma_start(wo[:], W["Wo"].rearrange("(c p) n -> p c n", p=P)).then_inc(wo_loaded, 16)
            if causal:
                for w in range(2):
                    sp.dma_start(flags[:, w], masks[w].rearrange("b (t p) k -> p b t k", p=P)).then_inc(flags_loaded, 16)
            with sp.Fori(0, B // 2) as i:
                for j in range(2):
                    n = 2 * i + j
                    sp.wait_ge(out_made[j], before(i))
                    for stack, order, w in ((qs, STACK_Q, 0), (ks, STACK_K, 1)):
                        for r, part in enumerate(order):
                            src = parts_dram[w, part].rearrange("(h d) t -> d h t", d=DK)[:, :, bass.ds(n * S, S)]
                            sp.dma_start(stack[r * DK:(r + 1) * DK, j], src).then_inc(stacks_loaded[j], 16)

        @block.gpsimd
        def _(pool):
            pool.memset(top_row[:], 0.0).then_inc(blank_ready, 1)
            if causal:
                pool.memset(later[:], 0.0)
                pool.drain()
                for t in range(TPB):
                    pool.affine_select(out=later[:, 0, t], in_=later[:, 0, t], compare_op=ALU.is_ge, fill=MASKED,
                                       base=t * P, pattern=[[-1, S]], channel_multiplier=1)
                    pool.affine_select(out=later[:, 1, t], in_=later[:, 1, t], compare_op=ALU.is_ge, fill=MASKED,
                                       base=-t * P, pattern=[[1, S]], channel_multiplier=-1)
                pool.wait_ge(flags_loaded, 32)
                pool.drain()
                for n in range(B):
                    pool.tensor_scalar(shut[:, :, n], flags[:, :, n], MASKED, None, ALU.mult)
                    pool.drain()
                    pool.tensor_tensor(shut[:, :, n], shut[:, :, n], later[:], ALU.add).then_inc(shut_ready, 1)

        @block.vector
        def _(dve):
            lead(dve, reduced, RING)
            lead(dve, taken, RING)
            primed(dve, out_taken)
            dve.wait_ge(blank_ready, 1)

            def reduce(n, g, u):
                qt, pair = UNITS[u]
                s = (n * NG + g) * NU + u
                dve.wait_ge(scored, ready(s))
                src = ps[:, SB + u % RING, :].rearrange("p (h k) -> p h k", h=2)[:, :, 0:keys(qt)]
                dve.tensor_reduce(top[:, g % 2, qt, 2 * pair:2 * pair + 2], src, AX.X, ALU.max).then_inc(reduced, 1)

            def tops(n, g):
                dve.drain()
                tp, pt = top[:, g % 2], top_parts[:, g % 2]
                if causal:
                    dve.tensor_scalar(tp, tp, FLOOR, None, ALU.max)
                    dve.drain()
                dve.tensor_copy(pt[:, :, 0], tp)
                dve.drain()
                dve.tensor_tensor(pt[:, :, 1], tp, pt[:, :, 0], ALU.subtract).then_inc(top_ready, 1)
                dve.wait_ge(top_turned, ready(n * NG + g))
                dve.tensor_copy(top_row[0:2 * G, g % 2, :], ps[0:2 * G, MB, 0:S]).then_inc(row_ready, 1)

            def normalize(n, g, j):
                dve.drain()
                dve.wait_ge(valued, ready(n * H + g * G + G - 1, PR))
                src = ps[:, OB + g % 2, 0:TPB * G * (DK + 1)].rearrange("p (t h d) -> p t h d", t=TPB, h=G)
                tt = total[:].rearrange("p (t h) -> p t h", t=TPB)
                if causal:
                    dve.tensor_scalar(tt, src[:, :, :, DK], 1e-30, None, ALU.max)
                    dve.drain()
                    dve.reciprocal(tt, tt)
                else:
                    dve.reciprocal(tt, src[:, :, :, DK])
                dve.drain()
                out = o[:, j].rearrange("p t (h d) -> p t h d", h=H)
                for t in range(TPB):
                    last = dve.tensor_tensor(out[:, t, g * G:(g + 1) * G, :], src[:, t, :, 0:DK],
                                             tt[:, t, :].unsqueeze(2).to_broadcast([P, G, DK]), ALU.mult)
                last.then_inc(taken, 1)

            with dve.Fori(0, B // 2) as i:
                for j in range(2):
                    n = 2 * i + j
                    for g in range(NG):
                        for u in range(NU):
                            reduce(n, g, u)
                        tops(n, g)
                        if g:
                            normalize(n, g - 1, j)
                    normalize(n, NG - 1, j)
                    dve.wait_ge(out_made[j], done(i))
                    xt = m["xres"][:, bass.ds(n * TPB, TPB), :]
                    dve.tensor_tensor(xt, xt, ps[:, XB, :].rearrange("p (t d) -> p t d", t=TPB), ALU.add).then_inc(out_taken, 1)
                    dve.drain()
                    for t in range(TPB):
                        dve.bn_stats(stats[:, t, :], m["xres"][:, bass.ds(n * TPB + t, 1), :].rearrange("p a d -> p (a d)"))
                    dve.drain()
                    for t in range(TPB):
                        dve.bn_aggr(mv[:, t, :], stats[:, t, :])
                    dve.drain()
                    dve.tensor_copy(m["mv"][:, bass.ds(n * TPB, TPB), :], mv[:])

        @block.scalar
        def _(act):
            lead(act, exped, RING)
            with act.Fori(0, B // 2) as i:
                for j in range(2):
                    n = 2 * i + j
                    for h in range(H):
                        act.wait_ge(scoredT, ready(n * H + h))
                        act.wait_ge(valued, free(n * H + h))
                        act.activation(probs[:, h % PR, 0:WIDE], ps[:, TB + h % RING, 0:WIDE], ACT.Exp, scale=DK ** -0.5).then_inc(exped, 1)
                    act.wait_ge(o_turned, ready(n))
                    act.activation(oT[:, j].rearrange("p c s -> p (c s)"), ps[:, XB, :], ACT.Copy).then_inc(oT_ready, 1)

        @block.tensor
        def _(pe):
            lead(pe, valued, PR)
            primed(pe, *out_made)
            pe.wait_ge(wo_loaded, 16)
            pe.wait_ge(blank_ready, 1)

            def score(n, j, g, u):
                qt, pair = UNITS[u]
                pe.wait_ge(reduced, free((n * NG + g) * NU + u))
                for x in range(2):
                    h = g * G + 2 * pair + x
                    out = ps[:, SB + u % RING, x * S:x * S + keys(qt)]
                    last = pe.matmul(out, qs[:, j, h, qt * P:(qt + 1) * P], ks[:, j, h, 0:keys(qt)], start=True, stop=not causal)
                    if causal:
                        last = pe.matmul(out, m["identb"][:], shut[:, 0, bass.ds(n, 1), qt, 0:keys(qt)].rearrange("p a k -> p (a k)"), start=False, stop=True)
                last.then_inc(scored, 1)

            def turn_tops(n, g):
                pe.wait_ge(top_ready, ready(n * NG + g))
                for t in range(TPB):
                    last = pe.matmul(ps[0:2 * G, MB, t * P:(t + 1) * P], top_parts[:, g % 2, t].rearrange("p a g -> p (a g)"),
                                     m["identb"][:], start=True, stop=True)
                last.then_inc(top_turned, 1)

            def scoreT(n, j, h):
                g = h // G
                if h % G == 0:
                    pe.wait_ge(row_ready, ready(n * NG + g))
                pe.wait_ge(exped, free(n * H + h))
                at = 0
                for kt in range(TPB):
                    q0 = first_q(kt)
                    out = ps[:, TB + h % RING, at:at + S - q0]
                    at += S - q0
                    pe.matmul(out, ks[:, j, h, kt * P:(kt + 1) * P], qs[:, j, h, q0:S], start=True, stop=False)
                    if causal:
                        pe.matmul(out, m["identb"][:], shut[:, 1, bass.ds(n, 1), kt, q0:S].rearrange("p a k -> p (a k)"), start=False, stop=False)
                    last = pe.matmul(out, m["minus"][:, h % G, :], top_row[:, g % 2, q0:S], start=False, stop=True)
                last.then_inc(scoredT, 1)

            def value(n, h):
                g = h // G
                if h % G == 0:
                    pe.wait_ge(taken, free(n * NG + g))
                pe.wait_ge(exped, ready(n * H + h, RING))
                for qt in range(TPB):
                    at = (qt * G + h % G) * (DK + 1)
                    kts = range(keys(qt) // P)
                    for kt in kts:
                        col = kt * S + qt * P - first_q(kt)
                        v = vals[:, bass.ds(n * TPB + kt, 1), h, :].rearrange("p a d -> p (a d)")
                        last = pe.matmul(ps[:, OB + g % 2, at:at + DK + 1], probs[:, h % PR, col:col + P], v,
                                         start=kt == 0, stop=kt == kts[-1])
                last.then_inc(valued, 1)

            with pe.Fori(0, B // 2) as i:
                for j in range(2):
                    n = 2 * i + j
                    pe.wait_ge(stacks_loaded[j], 16 * len(STACK_Q) * 2 * (i + 1))
                    if causal:
                        pe.wait_ge(shut_ready, n + 1)
                    for u in range(NU):
                        score(n, j, 0, u)
                    turn_tops(n, 0)
                    for g in range(NG):
                        plan = {0: (0, 1), 1: (2,), 2: (3,), 3: ()}
                        for x in range(G):
                            if g + 1 < NG:
                                for u in plan[x]:
                                    score(n, j, g + 1, u)
                            scoreT(n, j, g * G + x)
                            if g or x:
                                value(n, g * G + x - 1)
                        if g + 1 < NG:
                            turn_tops(n, g + 1)
                    value(n, H - 1)
                    pe.wait_ge(taken, ready(n * NG + NG - 1, RING))
                    pe.wait_ge(out_taken, before(n))
                    for t in range(TPB):
                        for c in range(DC):
                            last = pe.transpose(ps[:, XB, c * S + t * P:c * S + (t + 1) * P], o[:, j, t, c * P:(c + 1) * P], m["ident"][:])
                    last.then_inc(o_turned, 1)
                    pe.wait_ge(oT_ready, ready(n))
                    for t in range(TPB):
                        for c in range(DC):
                            last = pe.matmul(ps[:, XB, t * D:(t + 1) * D], oT[:, j, c, t * P:(t + 1) * P], wo[:, c, :],
                                             start=c == 0, stop=c == DC - 1)
                    last.then_inc(out_made[j], 1)


def route_block(nc, m, layer, E, a, xe):
    ctx = ExitStack()
    with ctx:
        def sb(name, shape, dt=F32):
            return ctx.enter_context(nc.sbuf_tensor(f"{name}_r{layer}", shape, dt))

        signal = ctx.enter_context(signals(nc, m["resting"]))

        def sem(name):
            return signal(f"{name}_r{layer}")

        def sems(name, n=2):
            return [sem(f"{name}{j}") for j in range(n)]

        capped = layer == 1
        N2 = 2 * NT
        wr = sb("wr", [P, DC, E])
        bias = sb("bias", [P, 2, E])
        lng = sb("lng", [P, 2, D])
        hall = sb("hall", [P, NT, D])
        hs = sb("hs", [P, 2, TPB, D])
        hn = sb("hn", [P, 2, TPB, D])
        hT = sb("hT", [P, 2, DC, S])
        logits = sb("logits", [P, NT, E])
        left = sb("left", [P, NT, E])
        fall = sb("fall", [P, E])
        rise = sb("rise", [P, E])
        steps = sb("steps", [P, NT])
        upto = sb("upto", [P, E, E])
        blocks = sb("blocks", [P, NB0])
        best = sb("best", [P, 2, NT])
        key = sb("key", [P, NT, E])
        keymax = sb("keymax", [P, NT])
        pick = sb("pick", [P, 2, NT, E])
        sums = sb("sums", [P, 2, N2, E])
        work = sb("work", [P, N2, E])
        load = sb("load", [P, E])
        full = sb("full", [P, E, NT])
        nblk = sb("nblk", [P, E])
        cum = sb("cum", [P, E, E])
        last_blk = sb("last_blk", [P, E])
        base = sb("base", [P, E])
        past = sb("past", [P, NB0, E])
        owner = sb("owner", [P, NB0])
        pos = sb("pos", [P, N2])
        home = sb("home", [P, N2])
        kept = sb("kept", [P, N2])
        slotf = sb("slotf", [P, N2])
        e2 = sb("e2", [P, NT])
        ps = ctx.enter_context(nc.psum_tensor(f"route_ps_{layer}", [P, 8, 512], F32))
        TB, LB, RB, CB = 0, 2, 4, 5

        w_loaded, const_ready = sem("w_loaded"), sem("const_ready")
        var_ready, root_ready = sem("var_ready"), sem("root_ready")
        h_ready, turned, hT_ready = sems("h_ready"), sems("turned"), sems("hT_ready")
        logits_made, logits_taken = sems("logits_made"), sems("logits_taken")
        kept_copy = sems("kept_copy")
        gap_ready, gap_exp = sem("gap_ready"), sem("gap_exp")
        sums_ready, ranks_made, slots_ready = sem("sums_ready"), sem("ranks_made"), sem("slots_ready")
        rows_stored = [sem(f"rows_stored{n}") for n in range(2)]
        shared_stored = sem("shared_stored")
        block = ctx.enter_context(nc.Block())

        loads = 16 * 3

        @block.sync
        def _(sp):
            sp.dma_start(wr[:], a["Wr" if capped else "Wg"].rearrange("(c p) e -> p c e", p=P)).then_inc(w_loaded, 16)
            for x, name in enumerate(("ln_g", "ln_b") if capped else ("bg", "bias")):
                dst = lng if capped else bias
                sp.dma_start(dst[:, x, :], a[name].partition_broadcast(P)).then_inc(w_loaded, 16)
            if capped:
                for j in range(2):
                    sp.wait_ge(kept_copy[j], before(B // 2))
                sp.dma_start(xe[E1 * CAP:E1 * CAP + T, :].rearrange("(n p) d -> p n d", p=P), hall[:]).then_inc(shared_stored, 16)
                sp.wait_ge(shared_stored, 16)

        @block.gpsimd
        def _(pool):
            def small(out, pattern, base=0, channel=0):
                return pool.iota(out, pattern=pattern, base=base, channel_multiplier=channel,
                                 allow_small_or_imprecise_dtypes=True)
            primed(pool, *kept_copy)
            small(fall[:], [[-1, E]], base=E)
            small(rise[:], [[1, E]])
            small(steps[:], [[P, NT]])
            small(blocks[:], [[1, NB0]])
            small(upto[:], [[-1, E], [1, E]])
            pool.drain()
            pool.tensor_scalar(upto[:], upto[:], 0.0, None, ALU.is_le).then_inc(const_ready, 1)
            with pool.Fori(0, B // 2) as i:
                for j in range(2):
                    pool.wait_ge(h_ready[j], done(i))
                    pool.tensor_copy(hall[:, bass.ds((2 * i + j) * TPB, TPB), :], hs[:, j]).then_inc(kept_copy[j], 1)
            pool.drain()
            pool.wait_ge(slots_ready, 1)
            for c in range(2):
                for t in range(NT):
                    pool.indirect_dma_start(xe, bass.IndirectOffsetOnAxis(ap=m["slot"][:, c, t:t + 1], axis=0),
                                            hall[:, t, :], None, bounds_check=xe.shape[0] - 1,
                                            oob_is_err=False).then_inc(rows_stored[c], 16)
            for c in range(2):
                pool.wait_ge(rows_stored[c], 16 * NT)

        @block.scalar
        def _(act):
            primed(act, *hT_ready)
            rstd_steps_scalar(act, m, var_ready, root_ready)
            with act.Fori(0, B // 2) as i:
                for j in range(2):
                    act.wait_ge(turned[j], done(i))
                    act.wait_ge(logits_made[j], before(i))
                    act.activation(hT[:, j].rearrange("p c s -> p (c s)"), ps[:, TB + j, :], ACT.Copy).then_inc(hT_ready[j], 1)
            act.wait_ge(gap_ready, 1)
            act.activation(e2[:], e2[:], ACT.Exp).then_inc(gap_exp, 1)

        @block.tensor
        def _(pe):
            primed(pe, *turned, *logits_made)
            pe.wait_ge(w_loaded, loads)
            with pe.Fori(0, B // 2) as i:
                for j in range(2):
                    pe.wait_ge(h_ready[j], done(i))
                    pe.wait_ge(hT_ready[j], before(i))
                    for t in range(TPB):
                        for c in range(DC):
                            last = pe.transpose(ps[:, TB + j, c * S + t * P:c * S + (t + 1) * P], hs[:, j, t, c * P:(c + 1) * P], m["ident"][:])
                    last.then_inc(turned[j], 1)
                    pe.wait_ge(hT_ready[j], done(i))
                    pe.wait_ge(logits_taken[j], before(i))
                    for t in range(TPB):
                        for c in range(DC):
                            last = pe.matmul(ps[:, LB + j, t * E:(t + 1) * E], hT[:, j, c, t * P:(t + 1) * P], wr[:, c, :],
                                             start=c == 0, stop=c == DC - 1)
                    last.then_inc(logits_made[j], 1)
            pe.wait_ge(sums_ready, 1)
            picks = pick[:].rearrange("p c t e -> p (c t e)")
            incl = sums[:, 0].rearrange("p n e -> p (n e)")
            pe.matmul(ps[:, RB, 0:N2 * E], m["before"][:], picks, start=True, stop=False, skip_group_check=True)
            pe.matmul(ps[:, RB, E:N2 * E], m["ones"][:], incl[:, 0:(N2 - 1) * E], start=False, stop=True, skip_group_check=True)
            pe.matmul(ps[:, CB, 0:E], m["ones"][:], incl[:, (N2 - 1) * E:N2 * E], start=True, stop=True).then_inc(ranks_made, 1)

        @block.vector
        def _(dve):
            primed(dve, *h_ready, *logits_taken)
            rstd_steps_vector(dve, m, var_ready, root_ready)
            dve.wait_ge(w_loaded, loads)
            dve.wait_ge(const_ready, 1)
            if not capped:
                dve.tensor_tensor(bias[:, 0], bias[:, 0], bias[:, 1], ALU.add)
                dve.drain()
            with dve.Fori(0, B // 2) as i:
                for j in range(2):
                    dve.wait_ge(turned[j], before(i))
                    dve.wait_ge(kept_copy[j], before(i))
                    dst = hn if capped else hs
                    for t in range(TPB):
                        n = (2 * i + j) * TPB + t
                        last = dve.tensor_scalar(dst[:, j, t, :], m["xres"][:, bass.ds(n, 1), :].rearrange("p a d -> p (a d)"),
                                                 m["mv"][:, bass.ds(n, 1), 0], m["rstd"][:, bass.ds(n, 1)], ALU.subtract, ALU.mult)
                    if capped:
                        dve.drain()
                        dve.tensor_tensor(hn[:, j], hn[:, j], lng[:, 0].unsqueeze(1).to_broadcast([P, TPB, D]), ALU.mult)
                        dve.drain()
                        last = dve.tensor_tensor(hs[:, j], hn[:, j], lng[:, 1].unsqueeze(1).to_broadcast([P, TPB, D]), ALU.add)
                    last.then_inc(h_ready[j], 1)
                    dve.wait_ge(logits_made[j], done(i))
                    dst = logits[:, bass.ds((2 * i + j) * TPB, TPB), :]
                    src = ps[:, LB + j, 0:TPB * E].rearrange("p (t e) -> p t e", t=TPB)
                    if capped:
                        last = dve.tensor_copy(dst, src)
                    else:
                        last = dve.tensor_tensor(dst, src, bias[:, 0].unsqueeze(1).to_broadcast([P, TPB, E]), ALU.add)
                    last.then_inc(logits_taken[j], 1)
            dve.drain()

            def then(ins):
                dve.drain()

            def over_tiles(ap):
                return ap.unsqueeze(1).to_broadcast([P, NT, E])

            src = logits
            for c in range(2):
                then(dve.tensor_reduce(best[:, c], src[:], AX.X, ALU.max))
                then(dve.tensor_tensor(key[:], src[:], best[:, c].unsqueeze(2).to_broadcast([P, NT, E]), ALU.is_equal))
                then(dve.tensor_tensor(key[:], key[:], over_tiles(fall[:]), ALU.mult))
                then(dve.tensor_reduce(keymax[:], key[:], AX.X, ALU.max))
                then(dve.tensor_tensor(pick[:, c], over_tiles(fall[:]), keymax[:].unsqueeze(2).to_broadcast([P, NT, E]), ALU.is_equal))
                if c == 0:
                    then(dve.scalar_tensor_tensor(out=left[:], in0=pick[:, 0], scalar=MASKED, in1=logits[:], op0=ALU.mult, op1=ALU.add))
                    src = left
            dve.tensor_tensor(e2[:], best[:, 1], best[:, 0], ALU.subtract).then_inc(gap_ready, 1)
            at = pick[:].rearrange("p c t e -> p (c t) e")
            reach, n = 1, 0
            while reach < N2:
                nxt = sums[:, n % 2]
                dve.tensor_copy(nxt[:, 0:reach], at[:, 0:reach])
                then(dve.tensor_tensor(nxt[:, reach:N2], at[:, reach:N2], at[:, 0:N2 - reach], ALU.add))
                at = nxt
                reach *= 2
                n += 1
            assert n % 2 == 1
            dve.sem_inc(sums_ready, 1)
            dve.wait_ge(gap_exp, 1)
            then(dve.tensor_scalar(m["gate"][:, 0], e2[:], 1.0, None, ALU.add))
            then(dve.reciprocal(m["gate"][:, 0], m["gate"][:, 0]))
            then(dve.tensor_tensor(m["gate"][:, 1], m["gate"][:, 0], e2[:], ALU.mult))

            dve.wait_ge(ranks_made, 1)
            ranks = ps[:, RB, 0:N2 * E].rearrange("p (n e) -> p n e", n=N2)
            picks = pick[:].rearrange("p c t e -> p (c t) e")

            def over_all(ap):
                return ap.unsqueeze(1).to_broadcast([P, N2, E])

            if capped:
                then(dve.tensor_tensor(work[:], ranks, picks, ALU.mult))
                then(dve.tensor_reduce(pos[:], work[:], AX.X, ALU.add))
                then(dve.tensor_tensor(work[:], over_all(rise[:]), picks, ALU.mult))
                then(dve.tensor_reduce(home[:], work[:], AX.X, ALU.add))
                then(dve.tensor_scalar(kept[:], pos[:], float(CAP), None, ALU.is_lt))
                then(dve.scalar_tensor_tensor(out=slotf[:], in0=home[:], scalar=float(CAP), in1=pos[:], op0=ALU.mult, op1=ALU.add))
                gates = m["gate"][:].rearrange("p c t -> p (c t)")
                then(dve.tensor_tensor(gates, gates, kept[:], ALU.mult))
                then(dve.tensor_tensor(home[:], slotf[:], kept[:], ALU.mult))
                dve.tensor_copy(m["slot_back"][:].rearrange("p c t -> p (c t)"), home[:])
                then(dve.tensor_scalar(kept[:], kept[:], -OUT_OF_RANGE, OUT_OF_RANGE, ALU.mult, ALU.add))
                then(dve.tensor_tensor(slotf[:], slotf[:], kept[:], ALU.add))
                dve.tensor_copy(m["slot"][:].rearrange("p c t -> p (c t)"), slotf[:]).then_inc(slots_ready, 1)
            else:
                then(dve.tensor_copy(load[:], ps[:, CB, 0:E]))
                then(dve.tensor_tensor(full[:], load[:].unsqueeze(2).to_broadcast([P, E, NT]), steps[:].unsqueeze(1).to_broadcast([P, E, NT]), ALU.is_gt))
                then(dve.tensor_reduce(nblk[:], full[:], AX.X, ALU.add))
                then(dve.tensor_tensor(cum[:], nblk[:].unsqueeze(1).to_broadcast([P, E, E]), upto[:], ALU.mult))
                then(dve.tensor_reduce(last_blk[:], cum[:], AX.X, ALU.add))
                then(dve.tensor_tensor(base[:], last_blk[:], nblk[:], ALU.subtract))
                then(dve.tensor_scalar(base[:], base[:], float(P), None, ALU.mult))
                then(dve.tensor_tensor(work[:], ranks, over_all(base[:]), ALU.add))
                then(dve.tensor_tensor(work[:], work[:], picks, ALU.mult))
                then(dve.tensor_reduce(pos[:], work[:], AX.X, ALU.add))
                dve.tensor_copy(m["slot_back"][:].rearrange("p c t -> p (c t)"), pos[:])
                dve.tensor_copy(m["slot"][:].rearrange("p c t -> p (c t)"), pos[:]).then_inc(slots_ready, 1)
                then(dve.tensor_tensor(past[:], last_blk[:].unsqueeze(1).to_broadcast([P, NB0, E]), blocks[:].unsqueeze(2).to_broadcast([P, NB0, E]), ALU.is_le))
                then(dve.tensor_reduce(owner[:], past[:], AX.X, ALU.add))
                then(dve.tensor_scalar(owner[:], owner[:], float(E - 1), None, ALU.min))
                dve.tensor_copy(m["block_expert"][:], owner[:])


def experts0_block(nc, m, a, xe, ye):
    ctx = ExitStack()
    with ctx:
        def sb(name, shape, dt=F32):
            return ctx.enter_context(nc.sbuf_tensor(f"{name}_e0", shape, dt))

        signal = ctx.enter_context(signals(nc, m["resting"]))

        def sem(name):
            return signal(f"{name}_e0")

        def sems(name, n=2):
            return [sem(f"{name}{j}") for j in range(n)]

        b1 = sb("b1", [P, E0, FC0])
        b2 = sb("b2", [P, E0, D])
        w = sb("w", [P, 2, W0])
        x = sb("x", [P, 2, D])
        xT = sb("xT", [P, 2, DC, P])
        hid = sb("hid", [P, 2, FC0, P])
        y = sb("y", [P, 2, D])
        ps = ctx.enter_context(nc.psum_tensor("e0_ps", [P, 8, 512], F32))
        XB, HB, YB = 0, 2, 4

        b_loaded = sem("b_loaded")
        w_loaded, x_loaded = sems("w_loaded"), sems("x_loaded")
        turned, xT_ready, hid_made, hid_ready = sems("turned"), sems("xT_ready"), sems("hid_made"), sems("hid_ready")
        y_made, y_ready, y_stored = sems("y_made"), sems("y_ready"), sems("y_stored")
        y_free = sems("y_free")
        block = ctx.enter_context(nc.Block())

        def w1(j, c, f):
            return w[:, j, c * F0 + f * P:c * F0 + (f + 1) * P]

        def w2(j, f):
            return w[:, j, DC * F0 + f * D:DC * F0 + (f + 1) * D]

        @block.sync
        def _(sp):
            sp.dma_start(b1[:], a["b1"]).then_inc(b_loaded, 16)
            sp.dma_start(b2[:].rearrange("p e d -> p (e d)"), a["b2"].rearrange("e d -> (e d)").partition_broadcast(P)).then_inc(b_loaded, 16)
            with sp.Fori(0, NB0 // 2) as i:
                for j in range(2):
                    n = 2 * i + j
                    e = sp.value_load(m["block_expert"][0:1, bass.ds(n, 1)], min_val=0, max_val=E0 - 1)
                    sp.wait_ge(turned[j], before(i))
                    sp.dma_start(x[:, j], xe[bass.ds(n * P, P), :]).then_inc(x_loaded[j], 16)
                    sp.wait_ge(y_made[j], before(i))
                    sp.dma_start(w[:, j], a["W_0"][bass.ds(e, 1)].rearrange("a p f -> p (a f)")).then_inc(w_loaded[j], 16)

        @block.gpsimd
        def _(pool):
            primed(pool, *y_free)
            with pool.Fori(0, NB0 // 2) as i:
                for j in range(2):
                    pool.wait_ge(y_ready[j], done(i))
                    pool.dma_start(ye[bass.ds((2 * i + j) * P, P), :], y[:, j]).then_inc(y_stored[j], 16)
                    pool.wait_ge(y_stored[j], 16 * (i + 1))
                    pool.sem_inc(y_free[j], 1)

        @block.scalar
        def _(act):
            primed(act, *xT_ready, *hid_ready)
            act.wait_ge(b_loaded, 32)
            with act.Fori(0, NB0 // 2) as i:
                for j in range(2):
                    e = act.value_load(m["block_expert"][0:1, bass.ds(2 * i + j, 1)], min_val=0, max_val=E0 - 1)
                    act.wait_ge(turned[j], done(i))
                    act.wait_ge(hid_made[j], before(i))
                    act.activation(xT[:, j].rearrange("p c s -> p (c s)"), ps[:, XB + j, 0:DC * P], ACT.Copy).then_inc(xT_ready[j], 1)
                    act.wait_ge(hid_made[j], done(i))
                    act.wait_ge(y_made[j], before(i))
                    for f in range(FC0):
                        last = act.activation(hid[:, j, f, :], ps[:, HB + j, f * P:(f + 1) * P], ACT.Relu,
                                              bias=b1[:, bass.ds(e, 1), f])
                    last.then_inc(hid_ready[j], 1)

        @block.vector
        def _(dve):
            primed(dve, *y_ready)
            dve.wait_ge(b_loaded, 32)
            with dve.Fori(0, NB0 // 2) as i:
                for j in range(2):
                    e = dve.value_load(m["block_expert"][0:1, bass.ds(2 * i + j, 1)], min_val=0, max_val=E0 - 1)
                    dve.wait_ge(y_made[j], done(i))
                    dve.wait_ge(y_free[j], before(i))
                    dve.tensor_tensor(y[:, j], ps[:, YB + j, 0:D], b2[:, bass.ds(e, 1), :].rearrange("p a d -> p (a d)"),
                                      ALU.add).then_inc(y_ready[j], 1)

        @block.tensor
        def _(pe):
            primed(pe, *turned, *hid_made, *y_made)

            def first(i, j):
                pe.wait_ge(x_loaded[j], 16 * (i + 1))
                pe.wait_ge(xT_ready[j], before(i))
                for c in range(DC):
                    last = pe.transpose(ps[:, XB + j, c * P:(c + 1) * P], x[:, j, c * P:(c + 1) * P], m["ident"][:])
                last.then_inc(turned[j], 1)
                pe.wait_ge(w_loaded[j], 16 * (i + 1))
                pe.wait_ge(xT_ready[j], done(i))
                pe.wait_ge(hid_ready[j], before(i))
                for f in range(FC0):
                    for c in range(DC):
                        last = pe.matmul(ps[:, HB + j, f * P:(f + 1) * P], w1(j, c, f), xT[:, j, c, :], start=c == 0, stop=c == DC - 1)
                last.then_inc(hid_made[j], 1)

            def second(i, j):
                pe.wait_ge(hid_ready[j], done(i))
                pe.wait_ge(y_ready[j], before(i))
                for f in range(FC0):
                    last = pe.matmul(ps[:, YB + j, 0:D], hid[:, j, f, :], w2(j, f), start=f == 0, stop=f == FC0 - 1)
                last.then_inc(y_made[j], 1)

            first(0, 0)
            with pe.Fori(0, NB0 // 2 - 1) as i:
                first(i, 1)
                second(i, 0)
                first(i + 1, 0)
                second(i, 1)
            first(NB0 // 2 - 1, 1)
            second(NB0 // 2 - 1, 0)
            second(NB0 // 2 - 1, 1)


def experts1_block(nc, m, a, xe, ye):
    ctx = ExitStack()
    with ctx:
        def sb(name, shape, dt=F32):
            return ctx.enter_context(nc.sbuf_tensor(f"{name}_e1", shape, dt))

        signal = ctx.enter_context(signals(nc, m["resting"]))

        def sem(name):
            return signal(f"{name}_e1")

        def sems(name, n=2):
            return [sem(f"{name}{j}") for j in range(n)]

        ROUNDS = XT // 2
        UN = 2 * FC1
        w = sb("w", [P, 2, W1C])
        wp = sb("wp", [P, 2, 2, W1C], F32R)
        x = sb("x", [P, XT, D])
        xT = sb("xT", [P, 2, DC, XT * P], F32R)
        act_a = sb("act_a", [P, 2, HALF[0]])
        hid = sb("hid", [P, 2, HALF[0]])
        hidp = sb("hidp", [P, 2, 2, HALF[0]], F32R)
        y = sb("y", [P, XT, D])
        ps = ctx.enter_context(nc.psum_tensor("e1_ps", [P, 8, 512], F32))
        AB, BB, YB, XB = 0, 2, 4, 7

        w_loaded = sems("w_loaded")
        w_high, w_cut = sem("w_high"), sem("w_cut")
        x_loaded, x_turned, x_high, x_cut = sem("x_loaded"), sem("x_turned"), sem("x_high"), sem("x_cut")
        first_done, silu_ready, mixed = sem("first_done"), sem("silu_ready"), sem("mixed")
        hid_high, hid_cut, second_done = sem("hid_high"), sem("hid_cut"), sem("second_done")
        y_taken, y_stored, y_free = sem("y_taken"), sem("y_stored"), sem("y_free")
        block = ctx.enter_context(nc.Block())

        chunks = a["W_1"].rearrange("e f p n -> (e f) p n")

        def lots(eng, body):
            with eng.Fori(0, E1) as v:
                body(v, lambda c: v * FC1 + c)
            with eng.Fori(E1, NV) as v:
                body(v, lambda c: E1 * FC1 + c % FC1)

        @block.sync
        def _(sp):
            def load(n, c, row):
                sp.wait_ge(w_cut, free(n + c))
                sp.dma_start(w[:, c % 2], chunks[bass.ds(row, 1)].rearrange("a p n -> p (a n)")).then_inc(w_loaded[c % 2], 16)

            load(0, 0, 0)

            def body(v, row):
                sp.wait_ge(x_turned, free(v * ROUNDS))
                sp.dma_start(x[:], xe[bass.ds(v * CAP, XT * P), :].rearrange("(n p) d -> p n d", p=P)).then_inc(x_loaded, 16)
                for c in range(FC1):
                    load(v * FC1, c + 1, row(c + 1))

            lots(sp, body)

        @block.gpsimd
        def _(pool):
            primed(pool, y_free)

            def body(v, row):
                pool.wait_ge(y_taken, done(v))
                full = (XT - 1) * P
                pool.dma_start(ye[bass.ds(v * CAP, full), :].rearrange("(n p) d -> p n d", p=P), y[:, 0:XT - 1]).then_inc(y_stored, 16)
                pool.dma_start(ye[bass.ds(v * CAP + full, LAST), :], y[0:LAST, XT - 1]).then_inc(y_stored, 16)
                pool.wait_ge(y_stored, 32 * (v + 1))
                pool.sem_inc(y_free, 1)

            lots(pool, body)

        @block.scalar
        def _(act):
            primed(act, y_taken)

            def weights_high(n, c):
                act.wait_ge(w_loaded[c % 2], 16 * ((n + c - c % 2) // 2 + 1) if isinstance(n, int) else 16 * (n // 2 + c // 2 + 1))
                act.wait_ge(second_done, (n + c) * 2 + 2)
                act.activation(wp[:, c % 2, 0], w[:, c % 2], ACT.Copy).then_inc(w_high, 1)

            weights_high(0, 0)

            def body(v, row):
                for r in range(ROUNDS):
                    act.wait_ge(x_turned, ready(v * ROUNDS + r, 1))
                    if r == 0:
                        act.wait_ge(first_done, v * UN + 1)
                    act.activation(xT[:, 0, :, r * 2 * P:(r + 1) * 2 * P], ps[:, XB, :].rearrange("p (c t) -> p c t", c=DC),
                                   ACT.Copy).then_inc(x_high, 1)
                for u in range(UN):
                    k, n = v * UN + u, HALF[u % 2]
                    act.wait_ge(first_done, ready(k, 1))
                    act.wait_ge(mixed, free(k))
                    act.activation(act_a[:, u % 2, 0:n], ps[:, AB + u % 2, 0:n], ACT.Silu).then_inc(silu_ready, 1)
                    act.wait_ge(mixed, ready(k, 2))
                    act.wait_ge(second_done, k + 3)
                    act.activation(hidp[:, u % 2, 0, 0:n], hid[:, u % 2, 0:n], ACT.Copy).then_inc(hid_high, 1)
                    if u % 2 == 0:
                        weights_high(v * FC1, u // 2 + 1)
                act.wait_ge(second_done, ready(v * UN + UN - 1, 4))
                act.wait_ge(y_free, before(v))
                act.activation(y[:, 0:XT - 1].rearrange("p n d -> p (n d)"), ps[:, YB:YB + 3].rearrange("p b f -> p (b f)")[:, 0:(XT - 1) * D], ACT.Copy)
                act.activation(y[0:LAST, XT - 1], ps[0:LAST, YB + 2, D:2 * D], ACT.Copy).then_inc(y_taken, 1)

            lots(act, body)

        @block.vector
        def _(dve):
            lead(dve, w_cut, 2)
            lead(dve, mixed, 2)
            lead(dve, x_cut, 1)

            def weights_rest(n, c):
                dve.wait_ge(w_high, ready(n + c))
                dve.tensor_tensor(wp[:, c % 2, 1], w[:, c % 2], wp[:, c % 2, 0].bitcast(F32), ALU.subtract).then_inc(w_cut, 1)

            weights_rest(0, 0)

            def body(v, row):
                for r in range(ROUNDS):
                    dve.wait_ge(x_high, ready(v * ROUNDS + r))
                    dve.tensor_tensor(xT[:, 1, :, r * 2 * P:(r + 1) * 2 * P], ps[:, XB, :].rearrange("p (c t) -> p c t", c=DC),
                                      xT[:, 0, :, r * 2 * P:(r + 1) * 2 * P].bitcast(F32), ALU.subtract).then_inc(x_cut, 1)
                for u in range(UN):
                    k, n = v * UN + u, HALF[u % 2]
                    dve.drain()
                    dve.wait_ge(silu_ready, ready(k))
                    dve.tensor_tensor(hid[:, u % 2, 0:n], act_a[:, u % 2, 0:n], ps[:, BB + u % 2, 0:n], ALU.mult).then_inc(mixed, 1)
                    dve.wait_ge(hid_high, ready(k))
                    dve.tensor_tensor(hidp[:, u % 2, 1, 0:n], hid[:, u % 2, 0:n], hidp[:, u % 2, 0, 0:n].bitcast(F32),
                                      ALU.subtract).then_inc(hid_cut, 1)
                    if u % 2 == 0:
                        weights_rest(v * FC1, u // 2 + 1)

            lots(dve, body)

        PASSES = ((0, 0), (0, 1), (1, 0))

        @block.tensor
        def _(pe):
            lead(pe, x_turned, 1)
            lead(pe, first_done, 1)
            lead(pe, second_done, 4)

            def first(v, u):
                c, half = u // 2, u % 2
                t0, n = half * HALF[0], HALF[half]
                if half == 0:
                    pe.wait_ge(w_cut, ready(v * FC1 + c, 2))
                pe.wait_ge(mixed, free(v * UN + u))
                for b, bank in enumerate((AB, BB)):
                    for d in range(DC):
                        for q, (pw, px) in enumerate(PASSES):
                            last = pe.matmul(ps[:, bank + u % 2, 0:n], wp[:, c % 2, pw, (b * DC + d) * P:(b * DC + d + 1) * P],
                                             xT[:, px, d, t0:t0 + n], start=d == 0 and q == 0, stop=d == DC - 1 and q == len(PASSES) - 1)
                last.then_inc(first_done, 1)

            def second(v, u):
                c, half = u // 2, u % 2
                pe.wait_ge(hid_cut, ready(v * UN + u))
                if u == 0:
                    pe.wait_ge(y_taken, before(v))
                for t in range(XT // 2):
                    tile = half * (XT // 2) + t
                    rows = LAST if tile == XT - 1 else P
                    out = ps[0:rows, YB + tile // 2, tile % 2 * D:(tile % 2 + 1) * D]
                    for q, (pw, px) in enumerate(PASSES):
                        last = pe.matmul(out, hidp[:, u % 2, px, t * P:t * P + rows], wp[:, c % 2, pw, 2 * DC * P:],
                                         start=c == 0 and q == 0 and tile % 2 == 0, stop=c == FC1 - 1 and q == len(PASSES) - 1,
                                         skip_group_check=True)
                last.then_inc(second_done, 1)

            def body(v, row):
                pe.wait_ge(x_loaded, 16 * (v + 1))
                for r in range(ROUNDS):
                    pe.wait_ge(x_cut, free(v * ROUNDS + r))
                    for c in range(DC):
                        for t in range(2):
                            last = pe.transpose(ps[:, XB, (2 * c + t) * P:(2 * c + t + 1) * P], x[:, 2 * r + t, c * P:(c + 1) * P], m["ident"][:])
                    last.then_inc(x_turned, 1)
                pe.wait_ge(x_cut, ready(v * ROUNDS + ROUNDS - 1, 1))
                for u in range(UN):
                    first(v, u)
                    if u:
                        second(v, u - 1)
                second(v, UN - 1)

            lots(pe, body)


def combine_block(nc, m, layer, ye, last_one):
    ctx = ExitStack()
    with ctx:
        def sb(name, shape, dt=F32):
            return ctx.enter_context(nc.sbuf_tensor(f"{name}_c{layer}", shape, dt))

        signal = ctx.enter_context(signals(nc, m["resting"]))

        def sem(name):
            return signal(f"{name}_c{layer}")

        RING = 4
        shared = layer == 1
        rows = sb("rows", [P, RING, 2, D])
        own = sb("own", [P, NT, D])
        stats = sb("stats", [P, NT, 6])
        own_loaded = sem("own_loaded")
        rows_loaded = [sem(f"rows_loaded{r}") for r in range(RING)]
        joined = sem("joined")
        block = ctx.enter_context(nc.Block())

        if shared:
            @block.sync
            def _(sp):
                sp.dma_start(own[:], ye[E1 * CAP:E1 * CAP + T, :].rearrange("(n p) d -> p n d", p=P)).then_inc(own_loaded, 16)

        @block.gpsimd
        def _(pool):
            for t in range(NT):
                if t >= RING:
                    pool.wait_ge(joined, t - RING + 1)
                for c in range(2):
                    pool.indirect_dma_start(rows[:, t % RING, c], None, ye,
                                            bass.IndirectOffsetOnAxis(ap=m["slot_back"][:, c, t:t + 1], axis=0)).then_inc(rows_loaded[t % RING], 16)

        @block.vector
        def _(dve):
            if shared:
                dve.wait_ge(own_loaded, 16)
                dve.tensor_tensor(m["xres"][:], m["xres"][:], own[:], ALU.add)
                dve.drain()
            for t in range(NT):
                dve.wait_ge(rows_loaded[t % RING], 32 * (t // RING + 1))
                xt = m["xres"][:, t]
                for c in range(2):
                    last = dve.scalar_tensor_tensor(out=xt, in0=rows[:, t % RING, c], scalar=m["gate"][:, c, t:t + 1], in1=xt,
                                                    op0=ALU.mult, op1=ALU.add)
                    if c == 0:
                        dve.drain()
                last.then_inc(joined, 1)
            if not last_one:
                dve.drain()
                for t in range(NT):
                    dve.bn_stats(stats[:, t, :], m["xres"][:, t, :])
                dve.drain()
                for t in range(NT):
                    dve.bn_aggr(m["mv"][:, t, :], stats[:, t, :])


def two_layers(nc, a, out, stop=99):
    with ExitStack() as ctx:
        m = alloc(nc, ctx)
        xe0 = nc.dram_tensor("rows0", (ROWS0, D), F32, kind="Internal").ap()
        xe1 = nc.dram_tensor("rows1", (ROWS1, D), F32, kind="Internal").ap()
        setup_block(nc, m, a["x"], xe0, xe1)
        step = 1
        for layer in range(2):
            W = {n: a[f"{n}_{layer}"] for n in ("Wq", "Wk", "Wv", "Wo", "bq", "bk", "bv", "bo") if f"{n}_{layer}" in a}
            parts = nc.dram_tensor(f"parts_{layer}", (2, PARTS, D, T), BF16, kind="Internal").ap()
            if step < stop:
                with nc.sbuf_tensor(f"vals_{layer}", [P, NT, H, DK + 1], F32) as vals:
                    project_block(nc, m, layer, a["ctxT"], W, parts, vals)
                    step += 1
                    if step < stop:
                        attend_block(nc, m, layer, layer == 0, W, (a.get("mask"), a.get("maskT")), parts, vals)
                    step += 1
            ye = nc.dram_tensor(f"done{layer}", (ROWS0 if layer == 0 else NV * CAP, D), F32, kind="Internal").ap()
            if step < stop:
                route_block(nc, m, layer, (E0, E1)[layer], a, (xe0, xe1)[layer])
                (experts0_block, experts1_block)[layer](nc, m, a, (xe0, xe1)[layer], ye)
                combine_block(nc, m, layer, ye, layer == 1)
            step += 1
        store_block(nc, m, out)


def store_block(nc, m, out):
    with ExitStack() as ctx:
        out_stored = ctx.enter_context(signals(nc, m["resting"]))("out_stored")
        block = ctx.enter_context(nc.Block())

        @block.sync
        def _(sp):
            sp.dma_start(out.rearrange("(n p) d -> p n d", p=P), m["xres"][:]).then_inc(out_stored, 16)
            sp.wait_ge(out_stored, 16)


def lay_out(i):
    c = np.ascontiguousarray
    mask = i["mask_BxSxS2_bf0"]
    a = {
        "x": i["x"].reshape(T, D),
        "ctxT": c(i["ctx_1024"].reshape(T, D).T),
        "mask": mask,
        "maskT": c(mask.transpose(0, 2, 1)),
        "Wq_0": c(i["L0_xattn_Wq"].T), "Wk_0": c(i["L0_xattn_Wk"].T), "Wv_0": c(i["L0_xattn_Wv"].T),
        "Wo_0": c(i["L0_xattn_Wout"].T), "bo_0": i["L0_xattn_b_out"],
        "Wq_1": i["L1_xattn_Wq"], "Wk_1": i["L1_xattn_Wk"], "Wv_1": i["L1_xattn_Wv"], "Wo_1": i["L1_xattn_Wo"],
        "bq_1": i["L1_xattn_bq"], "bk_1": i["L1_xattn_bk"], "bv_1": i["L1_xattn_bv"], "bo_1": i["L1_xattn_bo"],
        "Wg": i["L0_ffn_Wg"], "bg": i["L0_ffn_bg"], "bias": i["L0_ffn_bias"],
        "W_0": c(np.concatenate([
            i["L0_ffn_W1"].reshape(E0, DC, P, F0).transpose(0, 2, 1, 3).reshape(E0, P, DC * F0),
            i["L0_ffn_W2"].reshape(E0, FC0, P, D).transpose(0, 2, 1, 3).reshape(E0, P, FC0 * D)], axis=2)),
        "b1": c(i["L0_ffn_b1"].reshape(E0, FC0, P).transpose(2, 0, 1)),
        "b2": i["L0_ffn_b2"],
        "ln_g": i["L1_ffn_ln_g"], "ln_b": i["L1_ffn_ln_b"], "Wr": i["L1_ffn_Wr"],
    }
    w1, w3, w2 = (np.concatenate([i[f"L1_ffn_W{n}"], i[f"L1_ffn_W{n}s"][None]]) for n in (1, 3, 2))
    w1, w3 = (w.reshape(E1 + 1, DC, P, FC1, P).transpose(0, 3, 2, 1, 4).reshape(E1 + 1, FC1, P, DC * P) for w in (w1, w3))
    a["W_1"] = c(np.concatenate([w1, w3, w2.reshape(E1 + 1, FC1, P, D)], axis=3))
    return {k: c(v) for k, v in a.items()}


def kernel(**inputs):
    from concourse import bacc
    from concourse.bass_utils import run_bass_kernel_spmd

    nc = bacc.Bacc("TRN2", target_bir_lowering=False, num_devices=1)
    arrays = lay_out({k: np.asarray(v) for k, v in inputs.items()})
    args = {k: nc.dram_tensor(f"in_{k}", v.shape, mybir.dt.from_np(v.dtype), kind="ExternalInput").ap() for k, v in arrays.items()}
    out = nc.dram_tensor("out", (T, D), F32, kind="ExternalOutput").ap()
    two_layers(nc, args, out)
    r = run_bass_kernel_spmd(nc, [{f"in_{k}": v for k, v in arrays.items()}], core_ids=[0])
    return r.results[0]["out"].reshape(B, S, D)
```

```python
from contextlib import ExitStack, contextmanager

import numpy as np

import concourse.bass as bass
from concourse import mybir

F32 = mybir.dt.float32
F32R = mybir.dt.float32r
BF16 = mybir.dt.bfloat16
I32 = mybir.dt.int32
U32 = mybir.dt.uint32
U8 = mybir.dt.uint8
ALU = mybir.AluOpType
ACT = mybir.ActivationFunctionType
AX = mybir.AxisListType

P = 128
B, S, D = 8, 256, 256
T = B * S
NT = T // P
TPB = S // P
DC = D // P
H = 16
DK = D // H
HPC = P // DK
LN_EPS = 1e-5
PARTS = 3
STACK_Q = (0, 0, 0, 1, 1, 2)
STACK_K = (0, 1, 2, 0, 1, 0)
KS = len(STACK_Q) * DK
G = 4
NG = H // G
ROWS = P // G
MASKED = -1e30
FLOOR = -1e25

E0, F0 = 16, 512
FC0 = F0 // P
W0 = DC * F0 + FC0 * D
NB0 = 2 * T // P + E0
ROWS0 = NB0 * P

E1, F1, CAP = 7, 1024, 732
FC1 = F1 // P
VX = -(-T // CAP)
NV = E1 + VX
W1C = 2 * DC * P + D
XT = -(-CAP // P)
ROWS1 = (NV - 1) * CAP + XT * P
LAST = CAP - (XT - 1) * P
HALF = (XT // 2 * P, CAP - XT // 2 * P)
OUT_OF_RANGE = 1e6


def weight_of(v):
    return min(v, E1)


@contextmanager
def signals(nc, resting):
    mine = []

    def signal(name):
        mine.append(nc.alloc_semaphore(name=name))
        return mine[-1]

    yield signal
    nc.clear_and_free_semaphores(mine)
    again = [nc.alloc_semaphore(name=s.name + "_rest", num=s.num) for s in mine]
    while resting:
        nc.release_semaphore(resting.pop())
    resting += again


def alloc(nc, ctx):
    def sb(name, shape, dt=F32):
        return ctx.enter_context(nc.sbuf_tensor(name, shape, dt))

    m = {"resting": []}
    m["xres"] = sb("xres", [P, NT, D])
    m["mv"] = sb("mv", [P, NT, 2])
    m["rstd"] = sb("rstd", [P, NT])
    m["ident"] = sb("ident", [P, P])
    m["identb"] = sb("identb", [P, P], BF16)
    m["ones"] = sb("ones", [P, P])
    m["before"] = sb("before", [P, P])
    m["minus"] = sb("minus", [P, G, P], BF16)
    m["sum_row"] = sb("sum_row", [P, G])
    m["gate"] = sb("gate", [P, 2, NT])
    m["slot"] = sb("slot", [P, 2, NT], U32)
    m["slot_back"] = sb("slot_back", [P, 2, NT], U32)
    m["block_expert"] = sb("block_expert", [P, NB0], I32)
    return m


def setup_block(nc, m, x, xe0, xe1):
    with ExitStack() as ctx:
        zeros = ctx.enter_context(nc.sbuf_tensor("zeros", [P, 4096], F32))
        stats = ctx.enter_context(nc.sbuf_tensor("stats", [P, NT, 6], F32))
        sem = ctx.enter_context(signals(nc, m["resting"]))
        x_loaded, zeros_ready, zeros_stored = sem("x_loaded"), sem("zeros_ready"), sem("zeros_stored")
        block = ctx.enter_context(nc.Block())

        @block.sync
        def _(sp):
            sp.dma_start(m["xres"][:], x.rearrange("(n p) d -> p n d", p=P)).then_inc(x_loaded, 16)
            sp.wait_ge(zeros_ready, 1)
            n = 0
            for buf, rows in ((xe0, ROWS0), (xe1, ROWS1)):
                flat = buf.rearrange("r d -> (r d)")
                at = 0
                while at < rows * D:
                    k = min(P * 4096, rows * D - at)
                    sp.dma_start(flat[at:at + k].rearrange("(p f) -> p f", p=P), zeros[:, 0:k // P]).then_inc(zeros_stored, 16)
                    at += k
                    n += 1
            sp.wait_ge(zeros_stored, 16 * n)

        @block.gpsimd
        def _(pool):
            pool.memset(zeros[:], 0.0).then_inc(zeros_ready, 1)
            pool.memset(m["ident"][:], 0.0)
            pool.memset(m["ones"][:], 1.0)
            pool.memset(m["before"][:], 1.0)
            pool.memset(m["minus"][:], 0.0)
            pool.memset(m["sum_row"][:], 0.0)
            pool.drain()
            pool.affine_select(out=m["ident"][:], in_=m["ident"][:], compare_op=ALU.not_equal, fill=1.0,
                               base=0, pattern=[[-1, P]], channel_multiplier=1)
            pool.affine_select(out=m["before"][:], in_=m["before"][:], compare_op=ALU.is_gt, fill=0.0,
                               base=0, pattern=[[1, P]], channel_multiplier=-1)
            pool.affine_select(out=m["sum_row"][:], in_=m["sum_row"][:], compare_op=ALU.not_equal, fill=1.0,
                               base=-DK, pattern=[[-ROWS, G]], channel_multiplier=1)
            for part in range(2):
                pool.drain()
                pool.affine_select(out=m["minus"][:], in_=m["minus"][:], compare_op=ALU.not_equal, fill=-1.0,
                                   base=-part * G, pattern=[[-1, G], [0, P]], channel_multiplier=1)
            pool.drain()
            pool.tensor_copy(m["identb"][:], m["ident"][:])

        @block.vector
        def _(dve):
            dve.wait_ge(x_loaded, 16)
            for t in range(NT):
                dve.bn_stats(stats[:, t, :], m["xres"][:, t, :])
            dve.drain()
            for t in range(NT):
                dve.bn_aggr(m["mv"][:, t, :], stats[:, t, :])


def rstd_steps_vector(dve, m, var_ready, root_ready):
    dve.tensor_scalar(m["rstd"][:], m["mv"][:, :, 1], LN_EPS, None, ALU.add).then_inc(var_ready, 1)
    dve.wait_ge(root_ready, 1)
    dve.reciprocal(m["rstd"][:], m["rstd"][:])
    dve.drain()


def rstd_steps_scalar(act, m, var_ready, root_ready):
    act.wait_ge(var_ready, 1)
    act.activation(m["rstd"][:], m["rstd"][:], ACT.Sqrt).then_inc(root_ready, 1)


def primed(eng, *signals):
    for s in signals:
        eng.sem_inc(s, 1)


def done(n):
    return n + 2


def before(n):
    return n + 1


def project_block(nc, m, layer, ctxT, W, parts_dram, vals):
    ctx = ExitStack()
    with ctx:
        def sb(name, shape, dt=F32):
            return ctx.enter_context(nc.sbuf_tensor(f"{name}_{layer}", shape, dt))

        signal = ctx.enter_context(signals(nc, m["resting"]))

        def sem(name):
            return signal(f"{name}_{layer}")

        def sems(name):
            return [sem(f"{name}{j}") for j in range(2)]

        def sems2(name):
            return [[sem(f"{name}{j}{w}") for w in range(2)] for j in range(2)]

        biased = "bq" in W
        wq, wk, wv = (sb(n, [P, DC, D]) for n in ("wq", "wk", "wv"))
        bqk = sb("bqk", [P, 2, DC])
        bvb = sb("bvb", [P, D])
        bob = sb("bob", [P, D])
        cst = sb("cst", [P, 2, DC, S])
        h = sb("h", [P, 2, TPB, D])
        hT = sb("hT", [P, 2, DC, S])
        full = sb("full", [P, 2, 2, DC, S])
        rest = sb("rest", [P, 2, 2, DC, S])
        parts = sb("cut", [P, 2, 2, PARTS, DC, S], BF16)
        ps = ctx.enter_context(nc.psum_tensor(f"proj_ps_{layer}", [P, 8, 512], F32))
        KB, VB, TB, QB = 0, 2, 4, 6

        w_loaded = sem("w_loaded")
        var_ready, root_ready = sem("var_ready"), sem("root_ready")
        ctx_loaded = sems("ctx_loaded")
        h_ready, turned, hT_ready = sems("h_ready"), sems("turned"), sems("hT_ready")
        k_made, v_made, q_made = sems("k_made"), sems("v_made"), sems("q_made")
        k_taken, v_taken, q_taken = sems("k_taken"), sems("v_taken"), sems("q_taken")
        high_ready, parts_ready, parts_stored = sems2("high_ready"), sems2("parts_ready"), sems2("parts_stored")
        parts_free = sems("parts_free")
        block = ctx.enter_context(nc.Block())

        @block.sync
        def _(sp):
            for dst, name in ((wk, "Wk"), (wv, "Wv"), (wq, "Wq")):
                sp.dma_start(dst[:], W[name].rearrange("(c p) n -> p c n", p=P)).then_inc(w_loaded, 16)
            if biased:
                for w, name in enumerate(("bq", "bk")):
                    sp.dma_start(bqk[:, w, :], W[name].rearrange("(c p) -> p c", p=P), allow_slow_non_contiguous=True).then_inc(w_loaded, 16)
                sp.dma_start(bvb[:], W["bv"].partition_broadcast(P)).then_inc(w_loaded, 16)
            sp.dma_start(bob[:], W["bo"].partition_broadcast(P)).then_inc(w_loaded, 16)
            src = ctxT.rearrange("(c p) t -> p c t", p=P)
            with sp.Fori(0, B // 2) as i:
                for j in range(2):
                    sp.wait_ge(v_made[j], before(i))
                    sp.dma_start(cst[:, j, :, :], src[:, :, bass.ds((2 * i + j) * S, S)]).then_inc(ctx_loaded[j], 16)

        weights = 16 * (7 if biased else 4)

        @block.gpsimd
        def _(pool):
            primed(pool, *parts_free)
            with pool.Fori(0, B // 2) as i:
                for j in range(2):
                    for w in (1, 0):
                        pool.wait_ge(parts_ready[j][w], i + 1)
                        for part in range(PARTS):
                            dst = parts_dram[w, part].rearrange("(c p) t -> p c t", p=P)
                            pool.dma_start(dst[:, :, bass.ds((2 * i + j) * S, S)], parts[:, j, w, part]).then_inc(parts_stored[j][w], 16)
                    for w in (1, 0):
                        pool.wait_ge(parts_stored[j][w], 16 * PARTS * (i + 1))
                    pool.sem_inc(parts_free[j], 1)

        @block.vector
        def _(dve):
            primed(dve, *h_ready)
            if biased:
                primed(dve, *v_taken)
            rstd_steps_vector(dve, m, var_ready, root_ready)
            dve.wait_ge(w_loaded, weights)

            def norm(i, j):
                dve.wait_ge(turned[j], before(i))
                for t in range(TPB):
                    n = (2 * i + j) * TPB + t
                    last = dve.tensor_scalar(h[:, j, t, :], m["xres"][:, bass.ds(n, 1), :].rearrange("p a d -> p (a d)"),
                                             m["mv"][:, bass.ds(n, 1), 0], m["rstd"][:, bass.ds(n, 1)], ALU.subtract, ALU.mult)
                last.then_inc(h_ready[j], 1)
                dve.drain()
                xt = m["xres"][:, bass.ds((2 * i + j) * TPB, TPB), :]
                dve.tensor_tensor(xt, xt, bob[:].unsqueeze(1).to_broadcast([P, TPB, D]), ALU.add)

            def split(i, j, w):
                f, r, pt = full[:, j, w], rest[:, j, w], parts[:, j, w]
                dve.wait_ge(high_ready[j][w], i + 1)
                dve.tensor_tensor(r, f, pt[:, 0], ALU.subtract)
                dve.drain()
                dve.tensor_copy(pt[:, 1], r)
                dve.drain()
                dve.tensor_tensor(pt[:, 2], r, pt[:, 1], ALU.subtract).then_inc(parts_ready[j][w], 1)

            with dve.Fori(0, B // 2) as i:
                for j in range(2):
                    norm(i, j)
                    split(i, j, 1)
                    if biased:
                        dve.wait_ge(v_made[j], done(i))
                        out = vals[:, bass.ds((2 * i + j) * TPB, TPB), :, :]
                        dve.tensor_tensor(out, ps[:, VB + j, :].rearrange("p (t h d) -> p t h d", t=TPB, h=H),
                                          bvb[:].rearrange("p (h d) -> p h d", h=H).unsqueeze(1).to_broadcast([P, TPB, H, DK]),
                                          ALU.add).then_inc(v_taken[j], 1)
                    split(i, j, 0)

        @block.scalar
        def _(act):
            primed(act, *k_taken, *q_taken, *hT_ready)
            if not biased:
                primed(act, *v_taken)
            rstd_steps_scalar(act, m, var_ready, root_ready)
            if biased:
                act.wait_ge(w_loaded, weights)

            def take(i, j, w, made, taken, bank):
                act.wait_ge(made[j], done(i))
                act.wait_ge(parts_free[j], before(i))
                if biased:
                    for c in range(DC):
                        last = act.activation(full[:, j, w, c, :], ps[:, bank + j, c * S:(c + 1) * S], ACT.Identity,
                                              bias=bqk[:, w, c:c + 1])
                else:
                    last = act.activation(full[:, j, w].rearrange("p c s -> p (c s)"), ps[:, bank + j, :], ACT.Copy)
                last.then_inc(taken[j], 1)
                act.drain()
                act.activation(parts[:, j, w, 0], full[:, j, w], ACT.Copy).then_inc(high_ready[j][w], 1)

            with act.Fori(0, B // 2) as i:
                for j in range(2):
                    take(i, j, 1, k_made, k_taken, KB)
                    act.wait_ge(turned[j], done(i))
                    act.wait_ge(q_made[j], before(i))
                    act.activation(hT[:, j].rearrange("p c s -> p (c s)"), ps[:, TB + j, :], ACT.Copy).then_inc(hT_ready[j], 1)
                    if not biased:
                        act.wait_ge(v_made[j], done(i))
                        act.activation(vals[:, bass.ds((2 * i + j) * TPB, TPB), :, :],
                                       ps[:, VB + j, :].rearrange("p (t h d) -> p t h d", t=TPB, h=H), ACT.Copy).then_inc(v_taken[j], 1)
                    take(i, j, 0, q_made, q_taken, QB)

        @block.tensor
        def _(pe):
            primed(pe, *k_made, *v_made, *q_made, *turned)
            pe.wait_ge(w_loaded, weights)
            with pe.Fori(0, B // 2) as i:
                for j in range(2):
                    pe.wait_ge(ctx_loaded[j], 16 * (i + 1))
                    pe.wait_ge(k_taken[j], before(i))
                    for dh in range(DC):
                        for c in range(DC):
                            last = pe.matmul(ps[:, KB + j, dh * S:(dh + 1) * S], wk[:, c, dh * P:(dh + 1) * P], cst[:, j, c, :],
                                             start=c == 0, stop=c == DC - 1)
                    last.then_inc(k_made[j], 1)
                    pe.wait_ge(h_ready[j], done(i))
                    pe.wait_ge(hT_ready[j], before(i))
                    for t in range(TPB):
                        for c in range(DC):
                            last = pe.transpose(ps[:, TB + j, c * S + t * P:c * S + (t + 1) * P], h[:, j, t, c * P:(c + 1) * P], m["ident"][:])
                    last.then_inc(turned[j], 1)
                    pe.wait_ge(v_taken[j], before(i))
                    for t in range(TPB):
                        for c in range(DC):
                            last = pe.matmul(ps[:, VB + j, t * D:(t + 1) * D], cst[:, j, c, t * P:(t + 1) * P], wv[:, c, :],
                                             start=c == 0, stop=c == DC - 1)
                    last.then_inc(v_made[j], 1)
                    pe.wait_ge(hT_ready[j], done(i))
                    pe.wait_ge(q_taken[j], before(i))
                    for dh in range(DC):
                        for c in range(DC):
                            last = pe.matmul(ps[:, QB + j, dh * S:(dh + 1) * S], wq[:, c, dh * P:(dh + 1) * P], hT[:, j, c, :],
                                             start=c == 0, stop=c == DC - 1)
                    last.then_inc(q_made[j], 1)


def lead(eng, signal, n):
    eng.sem_inc(signal, n)


def free(u):
    return u + 1


def ready(u, n=0):
    return u + 1 + n


def attend_block(nc, m, layer, causal, W, masks, parts_dram, vals):
    ctx = ExitStack()
    with ctx:
        def sb(name, shape, dt=F32):
            return ctx.enter_context(nc.sbuf_tensor(f"{name}_{layer}", shape, dt))

        signal = ctx.enter_context(signals(nc, m["resting"]))

        def sem(name):
            return signal(f"{name}_{layer}")

        def sems(name, n=2):
            return [sem(f"{name}{j}") for j in range(n)]

        RING = 2
        wo = sb("wo", [P, NG, D])
        qs = sb("qs", [KS, 2, H, S], BF16)
        ks = sb("ks", [KS, 2, H, S], BF16)
        if causal:
            flags = sb("flags", [P, 2, B, TPB, S], U8)
            later = sb("later", [P, 2, TPB, S], BF16)
            shut = sb("shut", [P, 2, B, TPB, S], BF16)
        top = sb("top", [P, 2, TPB, G])
        top_parts = sb("top_parts", [P, 2, TPB, 2, G], BF16)
        top_row = sb("top_row", [P, 2, S], BF16)
        probs = sb("probs", [P, 2, G, TPB * S])
        v = sb("v", [P, 2, TPB, H, ROWS])
        o = sb("o", [P, 2, S])
        share = sb("share", [P, 2, TPB, G])
        oT = sb("oT", [P, 2, NG, S])
        stats = sb("stats", [P, TPB, 6])
        mv = sb("mv", [P, TPB, 2])
        ps = ctx.enter_context(nc.psum_tensor(f"att_ps_{layer}", [P, 8, 512], F32))
        SB, TB, OB, MB, XB = 0, 2, 4, 6, 7
        sums = ps[:, MB, S:S + TPB * G]

        wo_blank, wo_loaded = sem("wo_blank"), sem("wo_loaded")
        stacks_loaded, flags_loaded, shut_ready = sems("stacks_loaded"), sem("flags_loaded"), sem("shut_ready")
        blank_ready, v_ready = sem("blank_ready"), sem("v_ready")
        scored, reduced = sem("scored"), sem("reduced")
        top_ready, top_turned, row_ready = sem("top_ready"), sem("top_turned"), sem("row_ready")
        scoredT, exped, valued, o_ready = sem("scoredT"), sem("exped"), sem("valued"), sem("o_ready")
        summed, share_ready, spread, normed = sem("summed"), sem("share_ready"), sem("spread"), sem("normed")
        out_made, out_taken = sem("out_made"), sem("out_taken")
        block = ctx.enter_context(nc.Block())

        AHEAD = 2 * H

        UNITS = [(0, 0, 4), (1, 0, 2), (1, 2, 2)] if causal else [(t, x, 2) for t in range(TPB) for x in (0, 2)]
        NU = len(UNITS)
        WIDE = S + P if causal else 2 * S

        def keys(qt):
            return (qt + 1) * P if causal else S

        def first_q(kt):
            return kt * P if causal else 0

        def after(at):
            n, j, r, g = at
            return (n, j, r, g + 1) if g + 1 < NG else (n + 1, 1 - j, r + j, 0)

        def prior(at):
            n, j, r, g = at
            return (n, j, r, g - 1) if g else (n - 1, 1 - j, None, NG - 1)

        def group(at):
            return at[0] * NG + at[3]

        def unit_bank(at, u):
            return SB + (at[3] * NU + u) % RING

        def batches(eng, batch):
            batch(0, 0, 0, True, False)
            with eng.Fori(0, B // 2 - 1) as i:
                batch(2 * i + 1, 1, i, False, False)
                batch(2 * i + 2, 0, i + 1, False, False)
            batch(B - 1, 1, B // 2 - 1, False, True)

        @block.sync
        def _(sp):
            sp.wait_ge(wo_blank, 1)
            for x in range(G):
                src = W["Wo"].rearrange("(g x d) n -> x d g n", x=G, d=DK)[x]
                sp.dma_start(wo[x * ROWS:x * ROWS + DK], src).then_inc(wo_loaded, 16)
            if causal:
                for w in range(2):
                    sp.dma_start(flags[:, w], masks[w].rearrange("b (t p) k -> p b t k", p=P)).then_inc(flags_loaded, 16)
            with sp.Fori(0, B // 2) as i:
                for j in range(2):
                    n = 2 * i + j
                    sp.wait_ge(scoredT, (n + 1) * H)
                    for stack, order, w in ((qs, STACK_Q, 0), (ks, STACK_K, 1)):
                        for r, part in enumerate(order):
                            src = parts_dram[w, part].rearrange("(h d) t -> d h t", d=DK)[:, :, bass.ds(n * S, S)]
                            sp.dma_start(stack[r * DK:(r + 1) * DK, j], src).then_inc(stacks_loaded[j], 16)

        @block.gpsimd
        def _(pool):
            pool.memset(wo[:], 0.0).then_inc(wo_blank, 1)
            pool.memset(v[:, :, :, :, DK + 1:ROWS], 0.0)
            pool.memset(v[:, :, :, :, DK:DK + 1], 1.0)
            pool.memset(top_row[:], 0.0)
            pool.drain()
            pool.sem_inc(blank_ready, 1)
            if causal:
                pool.memset(later[:], 0.0)
                pool.drain()
                for t in range(TPB):
                    pool.affine_select(out=later[:, 0, t], in_=later[:, 0, t], compare_op=ALU.is_ge, fill=MASKED,
                                       base=t * P, pattern=[[-1, S]], channel_multiplier=1)
                    pool.affine_select(out=later[:, 1, t], in_=later[:, 1, t], compare_op=ALU.is_ge, fill=MASKED,
                                       base=-t * P, pattern=[[1, S]], channel_multiplier=-1)
                pool.wait_ge(flags_loaded, 32)
                pool.drain()
                for n in range(B):
                    pool.tensor_scalar(shut[:, :, n], flags[:, :, n], MASKED, None, ALU.mult)
                    pool.drain()
                    pool.tensor_tensor(shut[:, :, n], shut[:, :, n], later[:], ALU.add).then_inc(shut_ready, 1)

        @block.vector
        def _(dve):
            lead(dve, reduced, RING)
            lead(dve, normed, 2)
            lead(dve, out_taken, 1)

            def reduce(at, u):
                qt, x, heads = UNITS[u]
                dve.wait_ge(scored, ready(group(at) * NU + u))
                src = ps[:, unit_bank(at, u), :].rearrange("p (h k) -> p h k", h=heads)[:, :, 0:keys(qt)]
                dve.tensor_reduce(top[:, at[3] % 2, qt, x:x + heads], src, AX.X, ALU.max).then_inc(reduced, 1)

            def tops(at):
                g = at[3]
                tp, pt = top[:, g % 2], top_parts[:, g % 2]
                dve.drain()
                if causal:
                    dve.tensor_scalar(tp, tp, FLOOR, None, ALU.max)
                    dve.drain()
                dve.tensor_copy(pt[:, :, 0], tp)
                dve.drain()
                dve.tensor_tensor(pt[:, :, 1], tp, pt[:, :, 0], ALU.subtract).then_inc(top_ready, 1)

            def values(n, j):
                dve.tensor_copy(v[:, j, :, :, 0:DK], vals[:, bass.ds(n * TPB, TPB), :, :] if not isinstance(n, int)
                                else vals[:, n * TPB:(n + 1) * TPB, :, :]).then_inc(v_ready, 1)

            def invert(at):
                g = at[3]
                dve.wait_ge(summed, ready(group(at)))
                dst = share[:, g % 2].rearrange("p t x -> p (t x)")
                if causal:
                    dve.tensor_scalar(dst, sums, 1e-30, None, ALU.max)
                    dve.drain()
                    dve.reciprocal(dst, dst).then_inc(share_ready, 1)
                else:
                    dve.reciprocal(dst, sums).then_inc(share_ready, 1)

            def normalize(at):
                g = at[3]
                dve.wait_ge(spread, ready(group(at)))
                dve.tensor_tensor(oT[:, at[1], g], o[:, g % 2], ps[:, OB + g % 2, S:2 * S], ALU.mult).then_inc(normed, 1)

            def residual(n):
                dve.wait_ge(out_made, ready(n))
                xt = m["xres"][:, bass.ds(n * TPB, TPB), :]
                dve.tensor_tensor(xt, xt, ps[:, XB, :].rearrange("p (t d) -> p t d", t=TPB), ALU.add).then_inc(out_taken, 1)
                dve.drain()
                for t in range(TPB):
                    dve.bn_stats(stats[:, t, :], m["xres"][:, bass.ds(n * TPB + t, 1), :].rearrange("p a d -> p (a d)"))
                dve.drain()
                for t in range(TPB):
                    dve.bn_aggr(mv[:, t, :], stats[:, t, :])
                dve.drain()
                dve.tensor_copy(m["mv"][:, bass.ds(n * TPB, TPB), :], mv[:])

            def batch(n, j, r, first, last):
                for g in range(NG):
                    at = (n, j, r, g)
                    more, started = not (last and g == NG - 1), not (first and g == 0)
                    for u in range(4):
                        if u == 3 and started:
                            invert(prior(at))
                        if more and u < NU:
                            reduce(after(at), u)
                    if more:
                        tops(after(at))
                    if started:
                        normalize(prior(at))
                    if g == 0 and started:
                        residual(n - 1)
                    if g == 1 and not last:
                        values(n + 1, 1 - j)

            dve.wait_ge(blank_ready, 1)
            values(0, 0)
            for u in range(NU):
                reduce((0, 0, 0, 0), u)
            tops((0, 0, 0, 0))
            batches(dve, batch)
            invert((B - 1, 1, None, NG - 1))
            normalize((B - 1, 1, None, NG - 1))
            residual(B - 1)

        @block.scalar
        def _(act):
            lead(act, exped, RING)

            def take(at):
                g = at[3]
                act.wait_ge(valued, ready(group(at), 2))
                act.wait_ge(normed, free(group(at)))
                act.activation(o[:, g % 2], ps[:, OB + g % 2, 0:S], ACT.Copy).then_inc(o_ready, 1)

            def batch(n, j, r, first, last):
                for g in range(NG):
                    at = (n, j, r, g)
                    act.wait_ge(top_turned, ready(group(at)))
                    act.activation(top_row[0:2 * G, g % 2, :], ps[0:2 * G, MB, 0:S], ACT.Copy).then_inc(row_ready, 1)
                    if not (first and g == 0):
                        take(prior(at))
                    act.wait_ge(valued, free(group(at)))
                    for x in range(G):
                        act.wait_ge(scoredT, ready(n * H + g * G + x, AHEAD))
                        act.activation(probs[:, g % 2, x, 0:WIDE], ps[:, TB + x % RING, 0:WIDE], ACT.Exp, scale=DK ** -0.5).then_inc(exped, 1)

            batches(act, batch)
            take((B - 1, 1, None, NG - 1))

        @block.tensor
        def _(pe):
            lead(pe, valued, 2)
            lead(pe, scoredT, AHEAD)
            pe.wait_ge(blank_ready, 1)

            def score(at, u):
                n, j, r, g = at
                qt, x0, heads = UNITS[u]
                if g == 0 and u == 0:
                    pe.wait_ge(stacks_loaded[j], 16 * len(STACK_Q) * 2 * (r + 1))
                    if causal:
                        pe.wait_ge(shut_ready, n + 1)
                pe.wait_ge(reduced, free(group(at) * NU + u))
                for x in range(heads):
                    h = g * G + x0 + x
                    out = ps[:, unit_bank(at, u), x * 512 // heads:x * 512 // heads + keys(qt)]
                    last = pe.matmul(out, qs[:, j, h, qt * P:(qt + 1) * P], ks[:, j, h, 0:keys(qt)], start=True, stop=not causal)
                    if causal:
                        last = pe.matmul(out, m["identb"][:], closed(n, 0, qt, 0, keys(qt)), start=False, stop=True)
                last.then_inc(scored, 1)

            def closed(n, w, t, lo, hi):
                return shut[:, w, bass.ds(n, 1), t, lo:hi].rearrange("p a k -> p (a k)")

            def turn_tops(at):
                g = at[3]
                pe.wait_ge(top_ready, ready(group(at)))
                for t in range(TPB):
                    last = pe.matmul(ps[0:2 * G, MB, t * P:(t + 1) * P], top_parts[:, g % 2, t].rearrange("p a g -> p (a g)"),
                                     m["identb"][:], start=True, stop=True)
                last.then_inc(top_turned, 1)

            def scoreT(at, x):
                n, j, r, g = at
                h = g * G + x
                if x == 0:
                    pe.wait_ge(row_ready, ready(group(at)))
                pe.wait_ge(exped, free(n * H + h))
                col = 0
                for kt in range(TPB):
                    q0 = first_q(kt)
                    out = ps[:, TB + x % RING, col:col + S - q0]
                    col += S - q0
                    pe.matmul(out, ks[:, j, h, kt * P:(kt + 1) * P], qs[:, j, h, q0:S], start=True, stop=False)
                    if causal:
                        pe.matmul(out, m["identb"][:], closed(n, 1, kt, q0, S), start=False, stop=False)
                    last = pe.matmul(out, m["minus"][:, x, :], top_row[:, g % 2, q0:S], start=False, stop=True)
                last.then_inc(scoredT, 1)

            def value(at):
                n, j, r, g = at
                if g == 0:
                    pe.wait_ge(v_ready, n + 1)
                pe.wait_ge(normed, free(group(at)))
                pe.wait_ge(exped, ready(n * H + g * G + G - 1, RING))
                for kt in range(TPB):
                    q0 = first_q(kt)
                    for x in range(G):
                        last = pe.matmul(ps[x * ROWS:(x + 1) * ROWS, OB + g % 2, q0:S], v[:, j, kt, g * G + x, :],
                                         probs[:, g % 2, x, kt * S:kt * S + S - q0], start=kt == 0, stop=kt == TPB - 1,
                                         tile_position=(0, x * ROWS))
                last.then_inc(valued, 1)

            def turn_sums(at):
                g = at[3]
                pe.wait_ge(o_ready, ready(group(at)))
                for t in range(TPB):
                    last = pe.matmul(sums[:, t * G:(t + 1) * G], o[:, g % 2, t * P:(t + 1) * P], m["sum_row"][:], start=True, stop=True)
                last.then_inc(summed, 1)

            def spread_shares(at):
                g = at[3]
                pe.wait_ge(share_ready, ready(group(at)))
                for t in range(TPB):
                    for x in range(G):
                        last = pe.matmul(ps[x * ROWS:(x + 1) * ROWS, OB + g % 2, S + t * P:S + (t + 1) * P],
                                         share[:, g % 2, t, x:x + 1].to_broadcast([P, ROWS]), m["ident"][:], start=True, stop=True,
                                         tile_position=(0, x * ROWS))
                last.then_inc(spread, 1)

            def project(n, j):
                pe.wait_ge(normed, ready(n * NG + NG - 1, 2))
                pe.wait_ge(out_taken, free(n))
                for t in range(TPB):
                    for g in range(NG):
                        last = pe.matmul(ps[:, XB, t * D:(t + 1) * D], oT[:, j, g, t * P:(t + 1) * P], wo[:, g, :],
                                         start=g == 0, stop=g == NG - 1)
                last.then_inc(out_made, 1)

            def batch(n, j, r, first, last):
                for g in range(NG):
                    at = (n, j, r, g)
                    more, started = not (last and g == NG - 1), not (first and g == 0)

                    def score_next(u):
                        if more and u < NU:
                            score(after(at), u)

                    turn_tops(at)
                    score_next(0)
                    if started:
                        value(prior(at))
                    score_next(1)
                    scoreT(at, 0)
                    score_next(2)
                    scoreT(at, 1)
                    if started:
                        turn_sums(prior(at))
                    score_next(3)
                    scoreT(at, 2)
                    if started:
                        spread_shares(prior(at))
                    scoreT(at, 3)
                    if g == 0 and started:
                        project(n - 1, 1 - j)

            for u in range(NU):
                score((0, 0, 0, 0), u)
            pe.wait_ge(wo_loaded, 16 * G)
            batches(pe, batch)
            ended = (B - 1, 1, None, NG - 1)
            value(ended)
            turn_sums(ended)
            spread_shares(ended)
            project(B - 1, 1)


def route_block(nc, m, layer, E, a, xe):
    ctx = ExitStack()
    with ctx:
        def sb(name, shape, dt=F32):
            return ctx.enter_context(nc.sbuf_tensor(f"{name}_r{layer}", shape, dt))

        signal = ctx.enter_context(signals(nc, m["resting"]))

        def sem(name):
            return signal(f"{name}_r{layer}")

        def sems(name, n=2):
            return [sem(f"{name}{j}") for j in range(n)]

        capped = layer == 1
        N2 = 2 * NT
        wr = sb("wr", [P, DC, E])
        bias = sb("bias", [P, 2, E])
        lng = sb("lng", [P, 2, D])
        hall = sb("hall", [P, NT, D])
        hs = sb("hs", [P, 2, TPB, D])
        hn = sb("hn", [P, 2, TPB, D])
        hT = sb("hT", [P, 2, DC, S])
        logits = sb("logits", [P, NT, E])
        left = sb("left", [P, NT, E])
        fall = sb("fall", [P, E])
        rise = sb("rise", [P, E])
        steps = sb("steps", [P, NT])
        upto = sb("upto", [P, E, E])
        blocks = sb("blocks", [P, NB0])
        best = sb("best", [P, 2, NT])
        key = sb("key", [P, NT, E])
        keymax = sb("keymax", [P, NT])
        pick = sb("pick", [P, 2, NT, E])
        sums = sb("sums", [P, 2, N2, E])
        work = sb("work", [P, N2, E])
        load = sb("load", [P, E])
        full = sb("full", [P, E, NT])
        nblk = sb("nblk", [P, E])
        cum = sb("cum", [P, E, E])
        last_blk = sb("last_blk", [P, E])
        base = sb("base", [P, E])
        past = sb("past", [P, NB0, E])
        owner = sb("owner", [P, NB0])
        pos = sb("pos", [P, N2])
        home = sb("home", [P, N2])
        kept = sb("kept", [P, N2])
        slotf = sb("slotf", [P, N2])
        e2 = sb("e2", [P, NT])
        ps = ctx.enter_context(nc.psum_tensor(f"route_ps_{layer}", [P, 8, 512], F32))
        TB, LB, RB, CB = 0, 2, 4, 5

        w_loaded, const_ready = sem("w_loaded"), sem("const_ready")
        var_ready, root_ready = sem("var_ready"), sem("root_ready")
        h_ready, turned, hT_ready = sems("h_ready"), sems("turned"), sems("hT_ready")
        logits_made, logits_taken = sems("logits_made"), sems("logits_taken")
        kept_copy = sems("kept_copy")
        gap_ready, gap_exp = sem("gap_ready"), sem("gap_exp")
        sums_ready, ranks_made, slots_ready = sem("sums_ready"), sem("ranks_made"), sem("slots_ready")
        rows_stored = [sem(f"rows_stored{n}") for n in range(2)]
        shared_stored = sem("shared_stored")
        block = ctx.enter_context(nc.Block())

        loads = 16 * 3

        @block.sync
        def _(sp):
            sp.dma_start(wr[:], a["Wr" if capped else "Wg"].rearrange("(c p) e -> p c e", p=P)).then_inc(w_loaded, 16)
            for x, name in enumerate(("ln_g", "ln_b") if capped else ("bg", "bias")):
                dst = lng if capped else bias
                sp.dma_start(dst[:, x, :], a[name].partition_broadcast(P)).then_inc(w_loaded, 16)
            if capped:
                for j in range(2):
                    sp.wait_ge(kept_copy[j], before(B // 2))
                sp.dma_start(xe[E1 * CAP:E1 * CAP + T, :].rearrange("(n p) d -> p n d", p=P), hall[:]).then_inc(shared_stored, 16)
                sp.wait_ge(shared_stored, 16)

        @block.gpsimd
        def _(pool):
            def small(out, pattern, base=0, channel=0):
                return pool.iota(out, pattern=pattern, base=base, channel_multiplier=channel,
                                 allow_small_or_imprecise_dtypes=True)
            primed(pool, *kept_copy)
            small(fall[:], [[-1, E]], base=E)
            small(rise[:], [[1, E]])
            small(steps[:], [[P, NT]])
            small(blocks[:], [[1, NB0]])
            small(upto[:], [[-1, E], [1, E]])
            pool.drain()
            pool.tensor_scalar(upto[:], upto[:], 0.0, None, ALU.is_le).then_inc(const_ready, 1)
            with pool.Fori(0, B // 2) as i:
                for j in range(2):
                    pool.wait_ge(h_ready[j], done(i))
                    pool.tensor_copy(hall[:, bass.ds((2 * i + j) * TPB, TPB), :], hs[:, j]).then_inc(kept_copy[j], 1)
            pool.drain()
            pool.wait_ge(slots_ready, 1)
            for c in range(2):
                for t in range(NT):
                    pool.indirect_dma_start(xe, bass.IndirectOffsetOnAxis(ap=m["slot"][:, c, t:t + 1], axis=0),
                                            hall[:, t, :], None, bounds_check=xe.shape[0] - 1,
                                            oob_is_err=False).then_inc(rows_stored[c], 16)
            for c in range(2):
                pool.wait_ge(rows_stored[c], 16 * NT)

        @block.scalar
        def _(act):
            primed(act, *hT_ready)
            rstd_steps_scalar(act, m, var_ready, root_ready)
            with act.Fori(0, B // 2) as i:
                for j in range(2):
                    act.wait_ge(turned[j], done(i))
                    act.wait_ge(logits_made[j], before(i))
                    act.activation(hT[:, j].rearrange("p c s -> p (c s)"), ps[:, TB + j, :], ACT.Copy).then_inc(hT_ready[j], 1)
            act.wait_ge(gap_ready, 1)
            act.activation(e2[:], e2[:], ACT.Exp).then_inc(gap_exp, 1)

        @block.tensor
        def _(pe):
            primed(pe, *turned, *logits_made)
            pe.wait_ge(w_loaded, loads)
            with pe.Fori(0, B // 2) as i:
                for j in range(2):
                    pe.wait_ge(h_ready[j], done(i))
                    pe.wait_ge(hT_ready[j], before(i))
                    for t in range(TPB):
                        for c in range(DC):
                            last = pe.transpose(ps[:, TB + j, c * S + t * P:c * S + (t + 1) * P], hs[:, j, t, c * P:(c + 1) * P], m["ident"][:])
                    last.then_inc(turned[j], 1)
                    pe.wait_ge(hT_ready[j], done(i))
                    pe.wait_ge(logits_taken[j], before(i))
                    for t in range(TPB):
                        for c in range(DC):
                            last = pe.matmul(ps[:, LB + j, t * E:(t + 1) * E], hT[:, j, c, t * P:(t + 1) * P], wr[:, c, :],
                                             start=c == 0, stop=c == DC - 1)
                    last.then_inc(logits_made[j], 1)
            pe.wait_ge(sums_ready, 1)
            picks = pick[:].rearrange("p c t e -> p (c t e)")
            incl = sums[:, 0].rearrange("p n e -> p (n e)")
            pe.matmul(ps[:, RB, 0:N2 * E], m["before"][:], picks, start=True, stop=False, skip_group_check=True)
            pe.matmul(ps[:, RB, E:N2 * E], m["ones"][:], incl[:, 0:(N2 - 1) * E], start=False, stop=True, skip_group_check=True)
            pe.matmul(ps[:, CB, 0:E], m["ones"][:], incl[:, (N2 - 1) * E:N2 * E], start=True, stop=True).then_inc(ranks_made, 1)

        @block.vector
        def _(dve):
            primed(dve, *h_ready, *logits_taken)
            rstd_steps_vector(dve, m, var_ready, root_ready)
            dve.wait_ge(w_loaded, loads)
            dve.wait_ge(const_ready, 1)
            if not capped:
                dve.tensor_tensor(bias[:, 0], bias[:, 0], bias[:, 1], ALU.add)
                dve.drain()
            with dve.Fori(0, B // 2) as i:
                for j in range(2):
                    dve.wait_ge(turned[j], before(i))
                    dve.wait_ge(kept_copy[j], before(i))
                    dst = hn if capped else hs
                    for t in range(TPB):
                        n = (2 * i + j) * TPB + t
                        last = dve.tensor_scalar(dst[:, j, t, :], m["xres"][:, bass.ds(n, 1), :].rearrange("p a d -> p (a d)"),
                                                 m["mv"][:, bass.ds(n, 1), 0], m["rstd"][:, bass.ds(n, 1)], ALU.subtract, ALU.mult)
                    if capped:
                        dve.drain()
                        dve.tensor_tensor(hn[:, j], hn[:, j], lng[:, 0].unsqueeze(1).to_broadcast([P, TPB, D]), ALU.mult)
                        dve.drain()
                        last = dve.tensor_tensor(hs[:, j], hn[:, j], lng[:, 1].unsqueeze(1).to_broadcast([P, TPB, D]), ALU.add)
                    last.then_inc(h_ready[j], 1)
                    dve.wait_ge(logits_made[j], done(i))
                    dst = logits[:, bass.ds((2 * i + j) * TPB, TPB), :]
                    src = ps[:, LB + j, 0:TPB * E].rearrange("p (t e) -> p t e", t=TPB)
                    if capped:
                        last = dve.tensor_copy(dst, src)
                    else:
                        last = dve.tensor_tensor(dst, src, bias[:, 0].unsqueeze(1).to_broadcast([P, TPB, E]), ALU.add)
                    last.then_inc(logits_taken[j], 1)
            dve.drain()

            def then(ins):
                dve.drain()

            def over_tiles(ap):
                return ap.unsqueeze(1).to_broadcast([P, NT, E])

            src = logits
            for c in range(2):
                then(dve.tensor_reduce(best[:, c], src[:], AX.X, ALU.max))
                then(dve.tensor_tensor(key[:], src[:], best[:, c].unsqueeze(2).to_broadcast([P, NT, E]), ALU.is_equal))
                then(dve.tensor_tensor(key[:], key[:], over_tiles(fall[:]), ALU.mult))
                then(dve.tensor_reduce(keymax[:], key[:], AX.X, ALU.max))
                then(dve.tensor_tensor(pick[:, c], over_tiles(fall[:]), keymax[:].unsqueeze(2).to_broadcast([P, NT, E]), ALU.is_equal))
                if c == 0:
                    then(dve.scalar_tensor_tensor(out=left[:], in0=pick[:, 0], scalar=MASKED, in1=logits[:], op0=ALU.mult, op1=ALU.add))
                    src = left
            dve.tensor_tensor(e2[:], best[:, 1], best[:, 0], ALU.subtract).then_inc(gap_ready, 1)
            at = pick[:].rearrange("p c t e -> p (c t) e")
            reach, n = 1, 0
            while reach < N2:
                nxt = sums[:, n % 2]
                dve.tensor_copy(nxt[:, 0:reach], at[:, 0:reach])
                then(dve.tensor_tensor(nxt[:, reach:N2], at[:, reach:N2], at[:, 0:N2 - reach], ALU.add))
                at = nxt
                reach *= 2
                n += 1
            assert n % 2 == 1
            dve.sem_inc(sums_ready, 1)
            dve.wait_ge(gap_exp, 1)
            then(dve.tensor_scalar(m["gate"][:, 0], e2[:], 1.0, None, ALU.add))
            then(dve.reciprocal(m["gate"][:, 0], m["gate"][:, 0]))
            then(dve.tensor_tensor(m["gate"][:, 1], m["gate"][:, 0], e2[:], ALU.mult))

            dve.wait_ge(ranks_made, 1)
            ranks = ps[:, RB, 0:N2 * E].rearrange("p (n e) -> p n e", n=N2)
            picks = pick[:].rearrange("p c t e -> p (c t) e")

            def over_all(ap):
                return ap.unsqueeze(1).to_broadcast([P, N2, E])

            if capped:
                then(dve.tensor_tensor(work[:], ranks, picks, ALU.mult))
                then(dve.tensor_reduce(pos[:], work[:], AX.X, ALU.add))
                then(dve.tensor_tensor(work[:], over_all(rise[:]), picks, ALU.mult))
                then(dve.tensor_reduce(home[:], work[:], AX.X, ALU.add))
                then(dve.tensor_scalar(kept[:], pos[:], float(CAP), None, ALU.is_lt))
                then(dve.scalar_tensor_tensor(out=slotf[:], in0=home[:], scalar=float(CAP), in1=pos[:], op0=ALU.mult, op1=ALU.add))
                gates = m["gate"][:].rearrange("p c t -> p (c t)")
                then(dve.tensor_tensor(gates, gates, kept[:], ALU.mult))
                then(dve.tensor_tensor(home[:], slotf[:], kept[:], ALU.mult))
                dve.tensor_copy(m["slot_back"][:].rearrange("p c t -> p (c t)"), home[:])
                then(dve.tensor_scalar(kept[:], kept[:], -OUT_OF_RANGE, OUT_OF_RANGE, ALU.mult, ALU.add))
                then(dve.tensor_tensor(slotf[:], slotf[:], kept[:], ALU.add))
                dve.tensor_copy(m["slot"][:].rearrange("p c t -> p (c t)"), slotf[:]).then_inc(slots_ready, 1)
            else:
                then(dve.tensor_copy(load[:], ps[:, CB, 0:E]))
                then(dve.tensor_tensor(full[:], load[:].unsqueeze(2).to_broadcast([P, E, NT]), steps[:].unsqueeze(1).to_broadcast([P, E, NT]), ALU.is_gt))
                then(dve.tensor_reduce(nblk[:], full[:], AX.X, ALU.add))
                then(dve.tensor_tensor(cum[:], nblk[:].unsqueeze(1).to_broadcast([P, E, E]), upto[:], ALU.mult))
                then(dve.tensor_reduce(last_blk[:], cum[:], AX.X, ALU.add))
                then(dve.tensor_tensor(base[:], last_blk[:], nblk[:], ALU.subtract))
                then(dve.tensor_scalar(base[:], base[:], float(P), None, ALU.mult))
                then(dve.tensor_tensor(work[:], ranks, over_all(base[:]), ALU.add))
                then(dve.tensor_tensor(work[:], work[:], picks, ALU.mult))
                then(dve.tensor_reduce(pos[:], work[:], AX.X, ALU.add))
                dve.tensor_copy(m["slot_back"][:].rearrange("p c t -> p (c t)"), pos[:])
                dve.tensor_copy(m["slot"][:].rearrange("p c t -> p (c t)"), pos[:]).then_inc(slots_ready, 1)
                then(dve.tensor_tensor(past[:], last_blk[:].unsqueeze(1).to_broadcast([P, NB0, E]), blocks[:].unsqueeze(2).to_broadcast([P, NB0, E]), ALU.is_le))
                then(dve.tensor_reduce(owner[:], past[:], AX.X, ALU.add))
                then(dve.tensor_scalar(owner[:], owner[:], float(E - 1), None, ALU.min))
                dve.tensor_copy(m["block_expert"][:], owner[:])


def experts0_block(nc, m, a, xe, ye):
    ctx = ExitStack()
    with ctx:
        def sb(name, shape, dt=F32):
            return ctx.enter_context(nc.sbuf_tensor(f"{name}_e0", shape, dt))

        signal = ctx.enter_context(signals(nc, m["resting"]))

        def sem(name):
            return signal(f"{name}_e0")

        def sems(name, n):
            return [sem(f"{name}{j}") for j in range(n)]

        RING = 4
        b1 = sb("b1", [P, E0, FC0])
        b2 = sb("b2", [P, E0, D])
        w = sb("w", [P, RING, W0])
        x = sb("x", [P, RING, D])
        xT = sb("xT", [P, 2, DC, P])
        hid = sb("hid", [P, 2, FC0, P])
        y = sb("y", [P, RING, D])
        ps = ctx.enter_context(nc.psum_tensor("e0_ps", [P, 8, 512], F32))
        XB, HB, YB = 0, 2, 4

        b_loaded = sem("b_loaded")
        w_loaded, x_loaded, y_stored = sems("w_loaded", RING), sems("x_loaded", RING), sems("y_stored", RING)
        turned, xT_ready, hid_made, hid_ready = sem("turned"), sem("xT_ready"), sem("hid_made"), sem("hid_ready")
        y_made, y_ready, y_free = sem("y_made"), sem("y_ready"), sem("y_free")
        block = ctx.enter_context(nc.Block())

        TURNED, MADE, Y_MADE = RING, 2, RING

        def at(i, j):
            return (i, j) if j < RING else (i + 1, j - RING)

        def w1(j, c, f):
            return w[:, j, c * F0 + f * P:c * F0 + (f + 1) * P]

        def w2(j, f):
            return w[:, j, DC * F0 + f * D:DC * F0 + (f + 1) * D]

        @block.sync
        def _(sp):
            sp.dma_start(b1[:], a["b1"]).then_inc(b_loaded, 16)
            sp.dma_start(b2[:].rearrange("p e d -> p (e d)"), a["b2"].rearrange("e d -> (e d)").partition_broadcast(P)).then_inc(b_loaded, 16)
            with sp.Fori(0, NB0 // RING) as i:
                for j in range(RING):
                    n = RING * i + j
                    e = sp.value_load(m["block_expert"][0:1, bass.ds(n, 1)], min_val=0, max_val=E0 - 1)
                    sp.wait_ge(turned, free(n))
                    sp.dma_start(x[:, j], xe[bass.ds(n * P, P), :]).then_inc(x_loaded[j], 16)
                    sp.wait_ge(y_made, free(n))
                    sp.dma_start(w[:, j], a["W_0"][bass.ds(e, 1)].rearrange("a p f -> p (a f)")).then_inc(w_loaded[j], 16)

        @block.gpsimd
        def _(pool):
            lead(pool, y_free, RING)
            with pool.Fori(0, NB0 // RING) as i:
                for j in range(RING):
                    n = RING * i + j
                    pool.wait_ge(y_ready, ready(n, 2))
                    pool.dma_start(ye[bass.ds(n * P, P), :], y[:, j]).then_inc(y_stored[j], 16)
                    pool.wait_ge(y_stored[j], 16 * (i + 1))
                    pool.sem_inc(y_free, 1)

        @block.scalar
        def _(act):
            lead(act, hid_ready, 2)
            act.wait_ge(b_loaded, 32)
            with act.Fori(0, NB0 // RING) as i:
                for j in range(RING):
                    n = RING * i + j
                    e = act.value_load(m["block_expert"][0:1, bass.ds(n, 1)], min_val=0, max_val=E0 - 1)
                    act.wait_ge(hid_made, ready(n, MADE))
                    act.wait_ge(y_made, free(n) + Y_MADE - 2)
                    for f in range(FC0):
                        last = act.activation(hid[:, j % 2, f, :], ps[:, HB + j % 2, f * P:(f + 1) * P], ACT.Relu,
                                              bias=b1[:, bass.ds(e, 1), f])
                    last.then_inc(hid_ready, 1)

        @block.vector
        def _(dve):
            lead(dve, y_ready, 2)
            lead(dve, xT_ready, 2)
            dve.wait_ge(b_loaded, 32)

            def take_rows(i, j):
                n = RING * i + j
                dve.wait_ge(turned, ready(n, TURNED))
                dve.wait_ge(hid_made, free(n))
                dve.tensor_copy(xT[:, j % 2].rearrange("p c s -> p (c s)"), ps[:, XB + j % 2, 0:DC * P]).then_inc(xT_ready, 1)

            def take_sums(i, j):
                n = RING * i + j
                e = dve.value_load(m["block_expert"][0:1, bass.ds(n, 1)], min_val=0, max_val=E0 - 1)
                dve.wait_ge(y_made, ready(n, Y_MADE))
                dve.wait_ge(y_free, free(n))
                dve.tensor_tensor(y[:, j], ps[:, YB + j % 2, 0:D], b2[:, bass.ds(e, 1), :].rearrange("p a d -> p (a d)"),
                                  ALU.add).then_inc(y_ready, 1)

            def round_of(i, more):
                for j in range(RING):
                    if j + 2 < RING or more:
                        take_rows(*at(i, j + 2))
                    take_sums(i, j)

            take_rows(0, 0)
            take_rows(0, 1)
            with dve.Fori(0, NB0 // RING - 1) as i:
                round_of(i, True)
            round_of(NB0 // RING - 1, False)

        @block.tensor
        def _(pe):
            lead(pe, turned, TURNED)
            lead(pe, hid_made, MADE)
            lead(pe, y_made, Y_MADE)

            def turn(i, j):
                n = RING * i + j
                pe.wait_ge(x_loaded[j], 16 * (i + 1))
                pe.wait_ge(xT_ready, free(n))
                for c in range(DC):
                    last = pe.transpose(ps[:, XB + j % 2, c * P:(c + 1) * P], x[:, j, c * P:(c + 1) * P], m["ident"][:])
                last.then_inc(turned, 1)

            def first(i, j):
                n = RING * i + j
                pe.wait_ge(w_loaded[j], 16 * (i + 1))
                pe.wait_ge(xT_ready, ready(n, 2))
                pe.wait_ge(hid_ready, free(n))
                for f in range(FC0):
                    for c in range(DC):
                        last = pe.matmul(ps[:, HB + j % 2, f * P:(f + 1) * P], w1(j, c, f), xT[:, j % 2, c, :], start=c == 0, stop=c == DC - 1)
                last.then_inc(hid_made, 1)

            def second(i, j):
                n = RING * i + j
                pe.wait_ge(hid_ready, ready(n, 2))
                pe.wait_ge(y_ready, free(n))
                for f in range(FC0):
                    last = pe.matmul(ps[:, YB + j % 2, 0:D], hid[:, j % 2, f, :], w2(j, f), start=f == 0, stop=f == FC0 - 1)
                last.then_inc(y_made, 1)

            def round_of(i, more):
                for j in range(RING):
                    if j + 1 < RING or more:
                        first(*at(i, j + 1))
                    if j + 2 < RING or more:
                        turn(*at(i, j + 2))
                    second(i, j)

            turn(0, 0)
            turn(0, 1)
            first(0, 0)
            with pe.Fori(0, NB0 // RING - 1) as i:
                round_of(i, True)
            round_of(NB0 // RING - 1, False)


def experts1_block(nc, m, a, xe, ye):
    ctx = ExitStack()
    with ctx:
        def sb(name, shape, dt=F32):
            return ctx.enter_context(nc.sbuf_tensor(f"{name}_e1", shape, dt))

        signal = ctx.enter_context(signals(nc, m["resting"]))

        def sem(name):
            return signal(f"{name}_e1")

        def sems(name, n=2):
            return [sem(f"{name}{j}") for j in range(n)]

        ROUNDS = XT // 2
        UN = 2 * FC1
        w = sb("w", [P, 2, W1C])
        wp = sb("wp", [P, 2, 2, W1C], F32R)
        x = sb("x", [P, XT, D])
        xT = sb("xT", [P, 2, DC, XT * P], F32R)
        act_a = sb("act_a", [P, 2, HALF[0]])
        hid = sb("hid", [P, 2, HALF[0]])
        hidp = sb("hidp", [P, 2, 2, HALF[0]], F32R)
        y = sb("y", [P, XT, D])
        ps = ctx.enter_context(nc.psum_tensor("e1_ps", [P, 8, 512], F32))
        AB, BB, YB, XB = 0, 2, 4, 7

        w_loaded = sems("w_loaded")
        w_high, w_cut = sem("w_high"), sem("w_cut")
        x_loaded, x_turned, x_high, x_cut = sem("x_loaded"), sem("x_turned"), sem("x_high"), sem("x_cut")
        first_done, silu_ready, mixed = sem("first_done"), sem("silu_ready"), sem("mixed")
        hid_high, hid_cut, second_done = sem("hid_high"), sem("hid_cut"), sem("second_done")
        y_taken, y_stored, y_free = sem("y_taken"), sem("y_stored"), sem("y_free")
        block = ctx.enter_context(nc.Block())

        chunks = a["W_1"].rearrange("e f p n -> (e f) p n")

        def lots(eng, body):
            with eng.Fori(0, E1) as v:
                body(v, lambda c: v * FC1 + c)
            with eng.Fori(E1, NV) as v:
                body(v, lambda c: E1 * FC1 + c % FC1)

        @block.sync
        def _(sp):
            def load(n, c, row):
                sp.wait_ge(w_cut, free(n + c))
                sp.dma_start(w[:, c % 2], chunks[bass.ds(row, 1)].rearrange("a p n -> p (a n)")).then_inc(w_loaded[c % 2], 16)

            load(0, 0, 0)

            def body(v, row):
                sp.wait_ge(x_turned, free(v * ROUNDS))
                sp.dma_start(x[:], xe[bass.ds(v * CAP, XT * P), :].rearrange("(n p) d -> p n d", p=P)).then_inc(x_loaded, 16)
                for c in range(FC1):
                    load(v * FC1, c + 1, row(c + 1))

            lots(sp, body)

        @block.gpsimd
        def _(pool):
            primed(pool, y_free)

            def body(v, row):
                pool.wait_ge(y_taken, done(v))
                full = (XT - 1) * P
                pool.dma_start(ye[bass.ds(v * CAP, full), :].rearrange("(n p) d -> p n d", p=P), y[:, 0:XT - 1]).then_inc(y_stored, 16)
                pool.dma_start(ye[bass.ds(v * CAP + full, LAST), :], y[0:LAST, XT - 1]).then_inc(y_stored, 16)
                pool.wait_ge(y_stored, 32 * (v + 1))
                pool.sem_inc(y_free, 1)

            lots(pool, body)

        @block.scalar
        def _(act):
            primed(act, y_taken)

            def weights_high(n, c):
                act.wait_ge(w_loaded[c % 2], 16 * ((n + c - c % 2) // 2 + 1) if isinstance(n, int) else 16 * (n // 2 + c // 2 + 1))
                act.wait_ge(second_done, (n + c) * 2 + 2)
                act.activation(wp[:, c % 2, 0], w[:, c % 2], ACT.Copy).then_inc(w_high, 1)

            weights_high(0, 0)

            def body(v, row):
                for r in range(ROUNDS):
                    act.wait_ge(x_turned, ready(v * ROUNDS + r, 1))
                    if r == 0:
                        act.wait_ge(first_done, v * UN + 1)
                    act.activation(xT[:, 0, :, r * 2 * P:(r + 1) * 2 * P], ps[:, XB, :].rearrange("p (c t) -> p c t", c=DC),
                                   ACT.Copy).then_inc(x_high, 1)
                for u in range(UN):
                    k, n = v * UN + u, HALF[u % 2]
                    act.wait_ge(first_done, ready(k, 1))
                    act.wait_ge(mixed, free(k))
                    act.activation(act_a[:, u % 2, 0:n], ps[:, AB + u % 2, 0:n], ACT.Silu).then_inc(silu_ready, 1)
                    act.wait_ge(mixed, ready(k, 2))
                    act.wait_ge(second_done, k + 3)
                    act.activation(hidp[:, u % 2, 0, 0:n], hid[:, u % 2, 0:n], ACT.Copy).then_inc(hid_high, 1)
                    if u % 2 == 0:
                        weights_high(v * FC1, u // 2 + 1)
                act.wait_ge(second_done, ready(v * UN + UN - 1, 4))
                act.wait_ge(y_free, before(v))
                act.activation(y[:, 0:XT - 1].rearrange("p n d -> p (n d)"), ps[:, YB:YB + 3].rearrange("p b f -> p (b f)")[:, 0:(XT - 1) * D], ACT.Copy)
                act.activation(y[0:LAST, XT - 1], ps[0:LAST, YB + 2, D:2 * D], ACT.Copy).then_inc(y_taken, 1)

            lots(act, body)

        @block.vector
        def _(dve):
            lead(dve, w_cut, 2)
            lead(dve, mixed, 2)
            lead(dve, x_cut, 1)

            def weights_rest(n, c):
                dve.wait_ge(w_high, ready(n + c))
                dve.tensor_tensor(wp[:, c % 2, 1], w[:, c % 2], wp[:, c % 2, 0].bitcast(F32), ALU.subtract).then_inc(w_cut, 1)

            weights_rest(0, 0)

            def body(v, row):
                for r in range(ROUNDS):
                    dve.wait_ge(x_high, ready(v * ROUNDS + r))
                    dve.tensor_tensor(xT[:, 1, :, r * 2 * P:(r + 1) * 2 * P], ps[:, XB, :].rearrange("p (c t) -> p c t", c=DC),
                                      xT[:, 0, :, r * 2 * P:(r + 1) * 2 * P].bitcast(F32), ALU.subtract).then_inc(x_cut, 1)
                for u in range(UN):
                    k, n = v * UN + u, HALF[u % 2]
                    dve.drain()
                    dve.wait_ge(silu_ready, ready(k))
                    dve.tensor_tensor(hid[:, u % 2, 0:n], act_a[:, u % 2, 0:n], ps[:, BB + u % 2, 0:n], ALU.mult).then_inc(mixed, 1)
                    dve.wait_ge(hid_high, ready(k))
                    dve.tensor_tensor(hidp[:, u % 2, 1, 0:n], hid[:, u % 2, 0:n], hidp[:, u % 2, 0, 0:n].bitcast(F32),
                                      ALU.subtract).then_inc(hid_cut, 1)
                    if u % 2 == 0:
                        weights_rest(v * FC1, u // 2 + 1)

            lots(dve, body)

        PASSES = ((0, 0), (0, 1), (1, 0))

        @block.tensor
        def _(pe):
            lead(pe, x_turned, 1)
            lead(pe, first_done, 1)
            lead(pe, second_done, 4)

            def first(v, u):
                c, half = u // 2, u % 2
                t0, n = half * HALF[0], HALF[half]
                if half == 0:
                    pe.wait_ge(w_cut, ready(v * FC1 + c, 2))
                pe.wait_ge(mixed, free(v * UN + u))
                for b, bank in enumerate((AB, BB)):
                    for d in range(DC):
                        for q, (pw, px) in enumerate(PASSES):
                            last = pe.matmul(ps[:, bank + u % 2, 0:n], wp[:, c % 2, pw, (b * DC + d) * P:(b * DC + d + 1) * P],
                                             xT[:, px, d, t0:t0 + n], start=d == 0 and q == 0, stop=d == DC - 1 and q == len(PASSES) - 1)
                last.then_inc(first_done, 1)

            def second(v, u):
                c, half = u // 2, u % 2
                pe.wait_ge(hid_cut, ready(v * UN + u))
                if u == 0:
                    pe.wait_ge(y_taken, before(v))
                for t in range(XT // 2):
                    tile = half * (XT // 2) + t
                    rows = LAST if tile == XT - 1 else P
                    out = ps[0:rows, YB + tile // 2, tile % 2 * D:(tile % 2 + 1) * D]
                    for q, (pw, px) in enumerate(PASSES):
                        last = pe.matmul(out, hidp[:, u % 2, px, t * P:t * P + rows], wp[:, c % 2, pw, 2 * DC * P:],
                                         start=c == 0 and q == 0 and tile % 2 == 0, stop=c == FC1 - 1 and q == len(PASSES) - 1,
                                         skip_group_check=True)
                last.then_inc(second_done, 1)

            def body(v, row):
                pe.wait_ge(x_loaded, 16 * (v + 1))
                for r in range(ROUNDS):
                    pe.wait_ge(x_cut, free(v * ROUNDS + r))
                    for c in range(DC):
                        for t in range(2):
                            last = pe.transpose(ps[:, XB, (2 * c + t) * P:(2 * c + t + 1) * P], x[:, 2 * r + t, c * P:(c + 1) * P], m["ident"][:])
                    last.then_inc(x_turned, 1)
                pe.wait_ge(x_cut, ready(v * ROUNDS + ROUNDS - 1, 1))
                for u in range(UN):
                    first(v, u)
                    if u:
                        second(v, u - 1)
                second(v, UN - 1)

            lots(pe, body)


def combine_block(nc, m, layer, ye, last_one):
    ctx = ExitStack()
    with ctx:
        def sb(name, shape, dt=F32):
            return ctx.enter_context(nc.sbuf_tensor(f"{name}_c{layer}", shape, dt))

        signal = ctx.enter_context(signals(nc, m["resting"]))

        def sem(name):
            return signal(f"{name}_c{layer}")

        RING = 4
        shared = layer == 1
        rows = sb("rows", [P, RING, 2, D])
        own = sb("own", [P, NT, D])
        stats = sb("stats", [P, NT, 6])
        own_loaded = sem("own_loaded")
        rows_loaded = [sem(f"rows_loaded{r}") for r in range(RING)]
        joined = sem("joined")
        block = ctx.enter_context(nc.Block())

        if shared:
            @block.sync
            def _(sp):
                sp.dma_start(own[:], ye[E1 * CAP:E1 * CAP + T, :].rearrange("(n p) d -> p n d", p=P)).then_inc(own_loaded, 16)

        @block.gpsimd
        def _(pool):
            for t in range(NT):
                if t >= RING:
                    pool.wait_ge(joined, t - RING + 1)
                for c in range(2):
                    pool.indirect_dma_start(rows[:, t % RING, c], None, ye,
                                            bass.IndirectOffsetOnAxis(ap=m["slot_back"][:, c, t:t + 1], axis=0)).then_inc(rows_loaded[t % RING], 16)

        @block.vector
        def _(dve):
            if shared:
                dve.wait_ge(own_loaded, 16)
                dve.tensor_tensor(m["xres"][:], m["xres"][:], own[:], ALU.add)
                dve.drain()
            for t in range(NT):
                dve.wait_ge(rows_loaded[t % RING], 32 * (t // RING + 1))
                xt = m["xres"][:, t]
                for c in range(2):
                    last = dve.scalar_tensor_tensor(out=xt, in0=rows[:, t % RING, c], scalar=m["gate"][:, c, t:t + 1], in1=xt,
                                                    op0=ALU.mult, op1=ALU.add)
                    if c == 0:
                        dve.drain()
                last.then_inc(joined, 1)
            if not last_one:
                dve.drain()
                for t in range(NT):
                    dve.bn_stats(stats[:, t, :], m["xres"][:, t, :])
                dve.drain()
                for t in range(NT):
                    dve.bn_aggr(m["mv"][:, t, :], stats[:, t, :])


def two_layers(nc, a, out, stop=99):
    with ExitStack() as ctx:
        m = alloc(nc, ctx)
        xe0 = nc.dram_tensor("rows0", (ROWS0, D), F32, kind="Internal").ap()
        xe1 = nc.dram_tensor("rows1", (ROWS1, D), F32, kind="Internal").ap()
        setup_block(nc, m, a["x"], xe0, xe1)
        step = 1
        for layer in range(2):
            W = {n: a[f"{n}_{layer}"] for n in ("Wq", "Wk", "Wv", "Wo", "bq", "bk", "bv", "bo") if f"{n}_{layer}" in a}
            parts = nc.dram_tensor(f"parts_{layer}", (2, PARTS, D, T), BF16, kind="Internal").ap()
            if step < stop:
                with nc.sbuf_tensor(f"vals_{layer}", [P, NT, H, DK], F32) as vals:
                    project_block(nc, m, layer, a["ctxT"], W, parts, vals)
                    step += 1
                    if step < stop:
                        attend_block(nc, m, layer, layer == 0, W, (a.get("mask"), a.get("maskT")), parts, vals)
                    step += 1
            ye = nc.dram_tensor(f"done{layer}", (ROWS0 if layer == 0 else NV * CAP, D), F32, kind="Internal").ap()
            if step < stop:
                route_block(nc, m, layer, (E0, E1)[layer], a, (xe0, xe1)[layer])
                (experts0_block, experts1_block)[layer](nc, m, a, (xe0, xe1)[layer], ye)
                combine_block(nc, m, layer, ye, layer == 1)
            step += 1
        store_block(nc, m, out)


def store_block(nc, m, out):
    with ExitStack() as ctx:
        out_stored = ctx.enter_context(signals(nc, m["resting"]))("out_stored")
        block = ctx.enter_context(nc.Block())

        @block.sync
        def _(sp):
            sp.dma_start(out.rearrange("(n p) d -> p n d", p=P), m["xres"][:]).then_inc(out_stored, 16)
            sp.wait_ge(out_stored, 16)


def lay_out(i):
    c = np.ascontiguousarray
    mask = i["mask_BxSxS2_bf0"]
    a = {
        "x": i["x"].reshape(T, D),
        "ctxT": c(i["ctx_1024"].reshape(T, D).T),
        "mask": mask,
        "maskT": c(mask.transpose(0, 2, 1)),
        "Wq_0": c(i["L0_xattn_Wq"].T), "Wk_0": c(i["L0_xattn_Wk"].T), "Wv_0": c(i["L0_xattn_Wv"].T),
        "Wo_0": c(i["L0_xattn_Wout"].T), "bo_0": i["L0_xattn_b_out"],
        "Wq_1": i["L1_xattn_Wq"], "Wk_1": i["L1_xattn_Wk"], "Wv_1": i["L1_xattn_Wv"], "Wo_1": i["L1_xattn_Wo"],
        "bq_1": i["L1_xattn_bq"], "bk_1": i["L1_xattn_bk"], "bv_1": i["L1_xattn_bv"], "bo_1": i["L1_xattn_bo"],
        "Wg": i["L0_ffn_Wg"], "bg": i["L0_ffn_bg"], "bias": i["L0_ffn_bias"],
        "W_0": c(np.concatenate([
            i["L0_ffn_W1"].reshape(E0, DC, P, F0).transpose(0, 2, 1, 3).reshape(E0, P, DC * F0),
            i["L0_ffn_W2"].reshape(E0, FC0, P, D).transpose(0, 2, 1, 3).reshape(E0, P, FC0 * D)], axis=2)),
        "b1": c(i["L0_ffn_b1"].reshape(E0, FC0, P).transpose(2, 0, 1)),
        "b2": i["L0_ffn_b2"],
        "ln_g": i["L1_ffn_ln_g"], "ln_b": i["L1_ffn_ln_b"], "Wr": i["L1_ffn_Wr"],
    }
    w1, w3, w2 = (np.concatenate([i[f"L1_ffn_W{n}"], i[f"L1_ffn_W{n}s"][None]]) for n in (1, 3, 2))
    w1, w3 = (w.reshape(E1 + 1, DC, P, FC1, P).transpose(0, 3, 2, 1, 4).reshape(E1 + 1, FC1, P, DC * P) for w in (w1, w3))
    a["W_1"] = c(np.concatenate([w1, w3, w2.reshape(E1 + 1, FC1, P, D)], axis=3))
    return {k: c(v) for k, v in a.items()}


def kernel(**inputs):
    from concourse import bacc
    from concourse.bass_utils import run_bass_kernel_spmd

    nc = bacc.Bacc("TRN2", target_bir_lowering=False, num_devices=1)
    arrays = lay_out({k: np.asarray(v) for k, v in inputs.items()})
    args = {k: nc.dram_tensor(f"in_{k}", v.shape, mybir.dt.from_np(v.dtype), kind="ExternalInput").ap() for k, v in arrays.items()}
    out = nc.dram_tensor("out", (T, D), F32, kind="ExternalOutput").ap()
    two_layers(nc, args, out)
    r = run_bass_kernel_spmd(nc, [{f"in_{k}": v for k, v in arrays.items()}], core_ids=[0])
    return r.results[0]["out"].reshape(B, S, D)
```

```python
from contextlib import ExitStack, contextmanager

import numpy as np

import concourse.bass as bass
from concourse import mybir

F32 = mybir.dt.float32
F32R = mybir.dt.float32r
BF16 = mybir.dt.bfloat16
I32 = mybir.dt.int32
U32 = mybir.dt.uint32
U8 = mybir.dt.uint8
ALU = mybir.AluOpType
ACT = mybir.ActivationFunctionType
AX = mybir.AxisListType

P = 128
B, S, D = 8, 256, 256
T = B * S
NT = T // P
TPB = S // P
DC = D // P
H = 16
DK = D // H
HPC = P // DK
LN_EPS = 1e-5
PARTS = 3
STACK_Q = (0, 0, 0, 1, 1, 2)
STACK_K = (0, 1, 2, 0, 1, 0)
KS = len(STACK_Q) * DK
G = 4
NG = H // G
ROWS = P // G
MASKED = -1e30
FLOOR = -1e25

E0, F0 = 16, 512
FC0 = F0 // P
W0 = DC * F0 + FC0 * D
NB0 = 2 * T // P + E0
ROWS0 = NB0 * P

E1, F1, CAP = 7, 1024, 732
FC1 = F1 // P
W1C = 2 * DC * P + D
XT = -(-CAP // P)
ROWS1 = E1 * CAP + XT * P
LAST = CAP - (XT - 1) * P
HALF = XT // 2 * P
OUT_OF_RANGE = 1e6


@contextmanager
def signals(nc, resting):
    mine = []

    def signal(name):
        mine.append(nc.alloc_semaphore(name=name))
        return mine[-1]

    yield signal
    nc.clear_and_free_semaphores(mine)
    again = [nc.alloc_semaphore(name=s.name + "_rest", num=s.num) for s in mine]
    while resting:
        nc.release_semaphore(resting.pop())
    resting += again


def alloc(nc, ctx):
    def sb(name, shape, dt=F32):
        return ctx.enter_context(nc.sbuf_tensor(name, shape, dt))

    m = {"resting": []}
    m["xres"] = sb("xres", [P, NT, D])
    m["mv"] = sb("mv", [P, NT, 2])
    m["rstd"] = sb("rstd", [P, NT])
    m["ident"] = sb("ident", [P, P])
    m["identb"] = sb("identb", [P, P], BF16)
    m["ones"] = sb("ones", [P, P])
    m["before"] = sb("before", [P, P])
    m["minus"] = sb("minus", [P, G, P], BF16)
    m["sum_row"] = sb("sum_row", [P, 2, G])
    m["gate"] = sb("gate", [P, 2, NT])
    m["slot"] = sb("slot", [P, 2, NT], U32)
    m["slot_back"] = sb("slot_back", [P, 2, NT], U32)
    m["block_expert"] = sb("block_expert", [P, NB0], I32)
    return m


def setup_block(nc, m):
    with nc.Block() as block:
        @block.gpsimd
        def _(pool):
            pool.memset(m["ident"][:], 0.0)
            pool.memset(m["ones"][:], 1.0)
            pool.memset(m["before"][:], 1.0)
            pool.memset(m["minus"][:], 0.0)
            pool.memset(m["sum_row"][:], 0.0)
            pool.drain()
            pool.affine_select(out=m["ident"][:], in_=m["ident"][:], compare_op=ALU.not_equal, fill=1.0,
                               base=0, pattern=[[-1, P]], channel_multiplier=1)
            pool.affine_select(out=m["before"][:], in_=m["before"][:], compare_op=ALU.is_gt, fill=0.0,
                               base=0, pattern=[[1, P]], channel_multiplier=-1)
            pool.affine_select(out=m["sum_row"][:], in_=m["sum_row"][:], compare_op=ALU.not_equal, fill=1.0,
                               base=-DK, pattern=[[DK, 2], [-ROWS, G]], channel_multiplier=1)
            for part in range(2):
                pool.drain()
                pool.affine_select(out=m["minus"][:], in_=m["minus"][:], compare_op=ALU.not_equal, fill=-1.0,
                                   base=-part * G, pattern=[[-1, G], [0, P]], channel_multiplier=1)
            pool.drain()
            pool.tensor_copy(m["identb"][:], m["ident"][:])


def rstd_steps_vector(dve, m, var_ready, root_ready):
    dve.tensor_scalar(m["rstd"][:], m["mv"][:, :, 1], LN_EPS, None, ALU.add).then_inc(var_ready, 1)
    dve.wait_ge(root_ready, 1)
    dve.reciprocal(m["rstd"][:], m["rstd"][:])
    dve.drain()


def rstd_steps_scalar(act, m, var_ready, root_ready):
    act.wait_ge(var_ready, 1)
    act.activation(m["rstd"][:], m["rstd"][:], ACT.Sqrt).then_inc(root_ready, 1)


def primed(eng, *signals):
    for s in signals:
        eng.sem_inc(s, 1)


def done(n):
    return n + 2


def before(n):
    return n + 1


def project_block(nc, m, layer, W, parts_dram, q_from=None, kv_from=None, vals=None, stacks=None, scatter=None, masks=None):
    x, ye = q_from or (None, None)
    kinds = ([1] if kv_from is not None else []) + ([0] if q_from else [])
    tag = f"{layer}" if len(kinds) == 2 else f"{layer}{'qk'[kinds[0]]}"
    ctx = ExitStack()
    with ctx:
        def sb(name, shape, dt=F32):
            return ctx.enter_context(nc.sbuf_tensor(f"{name}_{tag}", shape, dt))

        signal = ctx.enter_context(signals(nc, m["resting"]))

        def sem(name):
            return signal(f"{name}_{tag}")

        def sems(name):
            return [sem(f"{name}{j}") for j in range(2)]

        def sems2(name):
            return [[sem(f"{name}{j}{w}") for w in range(2)] for j in range(2)]

        biased = "bq" in W
        wq, wk, wv = (sb(n, [P, DC, D]) for n in ("wq", "wk", "wv"))
        bqk = sb("bqk", [P, 2, DC])
        bvb = sb("bvb", [P, D])
        cst = sb("cst", [P, 2, DC, S])
        h = sb("h", [P, 2, TPB, D])
        if ye is not None:
            back = sb("back", [P, B, TPB, 2, D])
        stats = sb("row_stats", [P, 2, TPB, 6])
        mean_var = sb("mean_var", [P, 2, TPB, 2])
        rstd = sb("rstd", [P, 2, TPB])
        hT = sb("hT", [P, 2, DC, S])
        full = sb("full", [P, 2, 2, DC, S])
        rest = sb("rest", [P, 2, 2, DC, S])
        parts = sb("cut", [P, 2, 2, PARTS, DC, S], BF16)
        ps = ctx.enter_context(nc.psum_tensor(f"proj_ps_{tag}", [P, 8, 512], F32))
        KB, VB, TB, QB = 0, 2, 4, 6

        w_loaded = sem("w_loaded")
        x_loaded, back_loaded, rows_here = sems("x_loaded"), [sem(f"back_loaded{n}") for n in range(B)], sem("rows_here")
        var_ready, root_ready = sem("var_ready"), sem("root_ready")
        ctx_loaded = sems("ctx_loaded")
        h_ready, turned, hT_ready = sems("h_ready"), sems("turned"), sems("hT_ready")
        k_made, v_made, q_made = sems("k_made"), sems("v_made"), sems("q_made")
        k_taken, v_taken, q_taken = sems("k_taken"), sems("v_taken"), sems("q_taken")
        high_ready, parts_ready, parts_stored = sems2("high_ready"), sems2("parts_ready"), sems2("parts_stored")
        parts_free = sems("parts_free")
        if masks:
            flags = sb("flags", [P, 2, B, TPB, S], U8)
            later = sb("later", [P, 2, TPB, S], BF16)
        slots_filled, stack_loaded, flags_loaded = sem("slots_filled"), sem("stack_loaded"), sem("flags_loaded")
        block = ctx.enter_context(nc.Block())

        matrices = ([(wk, "Wk"), (wv, "Wv")] if 1 in kinds else []) + ([(wq, "Wq")] if 0 in kinds else [])
        weights = 16 * (len(matrices) + (3 if biased else 0))

        def next_one(i, j):
            return (i, 1) if j == 0 else (i + 1, 0)


        @block.sync
        def _(sp):
            def load_ctx(i, j):
                src = kv_from.rearrange("(c p) t -> p c t", p=P)
                at = src[:, :, bass.ds((2 * i + j) * S, S)]
                sp.wait_ge(v_made[j], before(i))
                sp.dma_start(cst[:, j, :, :], at).then_inc(ctx_loaded[j], 16)

            def load_x(part):
                tiles = (slice(0, 2 * TPB), slice(2 * TPB, NT))[part]
                sp.dma_start(m["xres"][:, tiles], x.rearrange("(n p) d -> p n d", p=P)[:, tiles]).then_inc(x_loaded[part], 16)

            if 1 in kinds:
                load_ctx(0, 0)
            for q, (dst, name) in enumerate(matrices):
                sp.dma_start(dst[:], W[name].rearrange("(c p) n -> p c n", p=P)).then_inc(w_loaded, 16)
                if x is not None and q == 0:
                    load_x(0)
            if biased:
                for w, name in enumerate(("bq", "bk")):
                    sp.dma_start(bqk[:, w, :], W[name].rearrange("(c p) -> p c", p=P), allow_slow_non_contiguous=True).then_inc(w_loaded, 16)
                sp.dma_start(bvb[:], W["bv"].partition_broadcast(P)).then_inc(w_loaded, 16)
            if x is not None:
                load_x(1)
            primed(sp, *parts_free)

            def pair(i, more):
                for j in range(2):
                    if more and 1 in kinds:
                        load_ctx(i + 1, j)
                    for w in kinds:
                        sp.wait_ge(parts_ready[j][w], i + 1)
                    for w in kinds:
                        for c in range(DC):
                            dst = parts_dram[w].rearrange("a (c p) t -> c p a t", p=P)[c]
                            sp.dma_start(dst[:, :, bass.ds((2 * i + j) * S, S)], parts[:, j, w, :, c]).then_inc(parts_stored[j][w], 16)
                    for w in kinds:
                        sp.wait_ge(parts_stored[j][w], 16 * DC * (i + 1))
                    sp.sem_inc(parts_free[j], 1)
            if 1 in kinds:
                load_ctx(0, 1)
            with sp.Fori(0, B // 2 - 1) as i:
                pair(i, True)
            pair(B // 2 - 1, False)

        @block.gpsimd
        def _(pool):
            if masks:
                shut = masks[2]
                if x is not None:
                    pool.wait_ge(x_loaded[0], 16)
                for w in range(2):
                    pool.dma_start(flags[:, w], masks[w].rearrange("b (t p) k -> p b t k", p=P)).then_inc(flags_loaded, 16)
                pool.memset(later[:], 0.0)
                pool.drain()
                for t in range(TPB):
                    pool.affine_select(out=later[:, 0, t], in_=later[:, 0, t], compare_op=ALU.is_ge, fill=MASKED,
                                       base=t * P, pattern=[[-1, S]], channel_multiplier=1)
                    pool.affine_select(out=later[:, 1, t], in_=later[:, 1, t], compare_op=ALU.is_ge, fill=MASKED,
                                       base=-t * P, pattern=[[1, S]], channel_multiplier=-1)
                pool.wait_ge(flags_loaded, 32)
                for n in range(B):
                    pool.tensor_scalar(shut[:, :, n], flags[:, :, n], MASKED, None, ALU.mult)
                pool.drain()
                for n in range(B):
                    pool.tensor_tensor(shut[:, :, n], shut[:, :, n], later[:], ALU.add)
            if scatter:
                rows, to = scatter
                for c in range(2):
                    for t in range(NT):
                        pool.indirect_dma_start(to, bass.IndirectOffsetOnAxis(ap=m["slot"][:, c, t:t + 1], axis=0),
                                                rows[:, t, :], None, bounds_check=to.shape[0] - 1,
                                                oob_is_err=False).then_inc(slots_filled, 16)
                pool.wait_ge(slots_filled, 16 * 2 * NT)
            if ye is not None:
                for n in range(B):
                    for t in range(TPB):
                        for c in range(2):
                            at = m["slot_back"][:, c, n * TPB + t:n * TPB + t + 1]
                            pool.indirect_dma_start(back[:, n, t, c], None, ye, bass.IndirectOffsetOnAxis(ap=at, axis=0)).then_inc(back_loaded[n], 16)
                    if n:
                        pool.wait_ge(back_loaded[n - 1], 16 * 2 * TPB)
                        pool.sem_inc(rows_here, 1)
                pool.wait_ge(back_loaded[B - 1], 16 * 2 * TPB)
                pool.sem_inc(rows_here, 1)

        @block.vector
        def _(dve):
            primed(dve, *h_ready)
            if biased:
                primed(dve, *v_taken)
            def arrive(i, j):
                n = 2 * i + j
                if ye is not None:
                    dve.wait_ge(rows_here, n + 1)
                    for c in range(2):
                        for t in range(TPB):
                            xt = tile_of(n, t)
                            dve.scalar_tensor_tensor(out=xt, in0=back[:, bass.ds(n, 1), t, c, :].rearrange("p a d -> p (a d)"),
                                                     scalar=m["gate"][:, c, bass.ds(n * TPB + t, 1)], in1=xt, op0=ALU.mult, op1=ALU.add)
                        dve.drain()
                else:
                    dve.wait_ge(x_loaded[0], 16)
                    if not isinstance(n, int):
                        dve.wait_ge(x_loaded[1], 16)
                for t in range(TPB):
                    dve.bn_stats(stats[:, j, t, :], tile_of(n, t))
                dve.drain()
                for t in range(TPB):
                    dve.bn_aggr(mean_var[:, j, t, :], stats[:, j, t, :])
                dve.drain()
                dve.tensor_scalar(rstd[:, j], mean_var[:, j, :, 1], LN_EPS, None, ALU.add).then_inc(var_ready, 1)

            def tile_of(n, t):
                return m["xres"][:, bass.ds(n * TPB + t, 1), :].rearrange("p a d -> p (a d)")

            def norm(i, j):
                dve.wait_ge(root_ready, 2 * i + j + 1)
                dve.reciprocal(rstd[:, j], rstd[:, j])
                dve.drain()
                dve.wait_ge(turned[j], before(i))
                for t in range(TPB):
                    last = dve.tensor_scalar(h[:, j, t, :], tile_of(2 * i + j, t), mean_var[:, j, t, 0:1], rstd[:, j, t:t + 1],
                                             ALU.subtract, ALU.mult)
                last.then_inc(h_ready[j], 1)

            def split(i, j, w):
                f, r, pt = full[:, j, w], rest[:, j, w], parts[:, j, w]
                dve.wait_ge(high_ready[j][w], i + 1)
                dve.tensor_tensor(r, f, pt[:, 0], ALU.subtract)
                dve.drain()
                dve.tensor_copy(pt[:, 1], r)
                dve.drain()
                dve.tensor_tensor(pt[:, 2], r, pt[:, 1], ALU.subtract).then_inc(parts_ready[j][w], 1)

            def pair(i, more):
                for j in range(2):
                    if 0 in kinds:
                        if more or j == 0:
                            norm(*next_one(i, j))
                        if more:
                            arrive(i + 1, j)
                    if 1 in kinds:
                        split(i, j, 1)
                    if biased and 1 in kinds:
                        dve.wait_ge(v_made[j], done(i))
                        out = vals[:, bass.ds((2 * i + j) * TPB, TPB), :, :]
                        dve.tensor_tensor(out, ps[:, VB + j, :].rearrange("p (t h d) -> p t h d", t=TPB, h=H),
                                          bvb[:].rearrange("p (h d) -> p h d", h=H).unsqueeze(1).to_broadcast([P, TPB, H, DK]),
                                          ALU.add).then_inc(v_taken[j], 1)
                    if 0 in kinds:
                        split(i, j, 0)

            if 0 in kinds:
                arrive(0, 0)
                arrive(0, 1)
                norm(0, 0)
            dve.wait_ge(w_loaded, weights)
            with dve.Fori(0, B // 2 - 1) as i:
                pair(i, True)
            pair(B // 2 - 1, False)

        @block.scalar
        def _(act):
            primed(act, *k_taken, *q_taken, *hT_ready)
            if not biased:
                primed(act, *v_taken)
            def root(i, j):
                act.wait_ge(var_ready, 2 * i + j + 1)
                act.activation(rstd[:, j], rstd[:, j], ACT.Sqrt).then_inc(root_ready, 1)

            def take_turned(i, j):
                act.wait_ge(turned[j], done(i))
                act.wait_ge(q_made[j], before(i))
                act.activation(hT[:, j].rearrange("p c s -> p (c s)"), ps[:, TB + j, :], ACT.Copy).then_inc(hT_ready[j], 1)

            if 0 in kinds:
                root(0, 0)
                root(0, 1)
                take_turned(0, 0)
            if biased:
                act.wait_ge(w_loaded, weights)

            def take(i, j, w, made, taken, bank):
                act.wait_ge(made[j], done(i))
                act.wait_ge(parts_free[j], before(i))
                if biased:
                    for c in range(DC):
                        last = act.activation(full[:, j, w, c, :], ps[:, bank + j, c * S:(c + 1) * S], ACT.Identity,
                                              bias=bqk[:, w, c:c + 1])
                else:
                    last = act.activation(full[:, j, w].rearrange("p c s -> p (c s)"), ps[:, bank + j, :], ACT.Copy)
                last.then_inc(taken[j], 1)
                act.drain()
                act.activation(parts[:, j, w, 0], full[:, j, w], ACT.Copy).then_inc(high_ready[j][w], 1)

            def pair(i, more):
                for j in range(2):
                    if 1 in kinds:
                        take(i, j, 1, k_made, k_taken, KB)
                        if not biased:
                            act.wait_ge(v_made[j], done(i))
                            act.activation(vals[:, bass.ds((2 * i + j) * TPB, TPB), :, :],
                                           ps[:, VB + j, :].rearrange("p (t h d) -> p t h d", t=TPB, h=H), ACT.Copy).then_inc(v_taken[j], 1)
                    if 0 in kinds:
                        take(i, j, 0, q_made, q_taken, QB)
                        if more or j == 0:
                            take_turned(*next_one(i, j))
                        if more:
                            root(i + 1, j)

            with act.Fori(0, B // 2 - 1) as i:
                pair(i, True)
            if stacks:
                for w in kinds:
                    act.wait_ge(parts_stored[0][w], 16 * DC)
                load_stack(act, stacks, 0, parts_dram, 0, stack_loaded)
            pair(B // 2 - 1, False)
            if stacks:
                act.wait_ge(stack_loaded, 16 * 2 * len(STACK_Q))

        @block.tensor
        def _(pe):
            primed(pe, *k_made, *v_made, *q_made, *turned)
            def turn(i, j):
                pe.wait_ge(h_ready[j], done(i))
                pe.wait_ge(hT_ready[j], before(i))
                for t in range(TPB):
                    for c in range(DC):
                        last = pe.transpose(ps[:, TB + j, c * S + t * P:c * S + (t + 1) * P], h[:, j, t, c * P:(c + 1) * P], m["ident"][:])
                last.then_inc(turned[j], 1)

            def pair(i, more):
                for j in range(2):
                    if 1 in kinds:
                        pe.wait_ge(ctx_loaded[j], 16 * (i + 1))
                        pe.wait_ge(k_taken[j], before(i))
                        for dh in range(DC):
                            for c in range(DC):
                                last = pe.matmul(ps[:, KB + j, dh * S:(dh + 1) * S], wk[:, c, dh * P:(dh + 1) * P], cst[:, j, c, :],
                                                 start=c == 0, stop=c == DC - 1)
                        last.then_inc(k_made[j], 1)
                    if 1 in kinds:
                        pe.wait_ge(v_taken[j], before(i))
                        for t in range(TPB):
                            for c in range(DC):
                                last = pe.matmul(ps[:, VB + j, t * D:(t + 1) * D], cst[:, j, c, t * P:(t + 1) * P], wv[:, c, :],
                                                 start=c == 0, stop=c == DC - 1)
                        last.then_inc(v_made[j], 1)
                    if 0 in kinds:
                        pe.wait_ge(hT_ready[j], done(i))
                        pe.wait_ge(q_taken[j], before(i))
                        for dh in range(DC):
                            for c in range(DC):
                                last = pe.matmul(ps[:, QB + j, dh * S:(dh + 1) * S], wq[:, c, dh * P:(dh + 1) * P], hT[:, j, c, :],
                                                 start=c == 0, stop=c == DC - 1)
                        last.then_inc(q_made[j], 1)
                        if more or j == 0:
                            turn(*next_one(i, j))

            if 0 in kinds:
                turn(0, 0)
            pe.wait_ge(w_loaded, weights)
            with pe.Fori(0, B // 2 - 1) as i:
                pair(i, True)
            pair(B // 2 - 1, False)


def load_stack(eng, stacks, j, parts_dram, n, loaded):
    for w in range(2):
        for r, part in enumerate((STACK_Q, STACK_K)[w]):
            src = parts_dram[w, part].rearrange("(h d) t -> d h t", d=DK)[:, :, bass.ds(n * S, S)]
            eng.dma_start(stacks[w][r * DK:(r + 1) * DK, j], src).then_inc(loaded, 16)


def lead(eng, signal, n):
    eng.sem_inc(signal, n)


def free(u):
    return u + 1


def ready(u, n=0):
    return u + 1 + n


def attend_block(nc, m, layer, W, shut, parts_dram, stacks, vals, fill):
    causal = shut is not None
    ctx = ExitStack()
    with ctx:
        def sb(name, shape, dt=F32):
            return ctx.enter_context(nc.sbuf_tensor(f"{name}_{layer}", shape, dt))

        signal = ctx.enter_context(signals(nc, m["resting"]))

        def sem(name):
            return signal(f"{name}_{layer}")

        def sems(name, n=2):
            return [sem(f"{name}{j}") for j in range(n)]

        RING = 2
        wo = sb("wo", [P, NG // 2, D])
        qs, ks = stacks
        bo = sb("bo", [P, D])
        if fill:
            zeros = sb("zeros", [P, 2048])
        top = sb("top", [P, 2, TPB, G])
        top_parts = sb("top_parts", [P, 2, TPB, 2, G], BF16)
        top_row = sb("top_row", [P, 2, S], BF16)
        probs = sb("probs", [P, 2, G, TPB * S])
        v = sb("v", [P, 2, TPB, H, ROWS])
        o = sb("o", [P, 2, S])
        share = sb("share", [P, 2, TPB, G])
        wide_share = sb("wide_share", [P, 2, TPB * G, ROWS])
        oT = sb("oT", [P, 2, NG // 2, S])
        o_odd = sb("o_odd", [P, S])
        ones = sb("ones", [P, DK])
        stats = sb("stats", [P, TPB, 6])
        mv = sb("mv", [P, TPB, 2])
        ps = ctx.enter_context(nc.psum_tensor(f"att_ps_{layer}", [P, 8, 512], F32))
        SB, TB, OB, MB, XB = 0, 2, 4, 6, 7
        sums = ps[:, MB, S:S + TPB * G]

        wo_loaded = sem("wo_loaded")
        bo_loaded, bo_joined, zeros_stored = sem("bo_loaded"), sem("bo_joined"), sem("zeros_stored")
        stacks_loaded = sems("stacks_loaded")
        blank_ready, v_ready = sem("blank_ready"), sem("v_ready")
        scored, reduced = sem("scored"), sem("reduced")
        top_ready, top_turned, row_ready = sem("top_ready"), sem("top_turned"), sem("row_ready")
        scoredT, exped, valued, o_ready = sem("scoredT"), sem("exped"), sem("valued"), sem("o_ready")
        summed, share_ready, share_wide, spread, normed = sem("summed"), sem("share_ready"), sem("share_wide"), sem("spread"), sem("normed")
        out_made, out_taken = sem("out_made"), sem("out_taken")
        block = ctx.enter_context(nc.Block())

        AHEAD = 2 * H

        UNITS = [(0, 0, 4), (1, 0, 2), (1, 2, 2)] if causal else [(t, x, 2) for t in range(TPB) for x in (0, 2)]
        NU = len(UNITS)
        WIDE = S + P if causal else 2 * S

        def keys(qt):
            return (qt + 1) * P if causal else S

        def first_q(kt):
            return kt * P if causal else 0

        def after(at):
            n, j, r, g = at
            return (n, j, r, g + 1) if g + 1 < NG else (n + 1, 1 - j, r + j, 0)

        def prior(at):
            n, j, r, g = at
            return (n, j, r, g - 1) if g else (n - 1, 1 - j, None, NG - 1)

        def group(at):
            return at[0] * NG + at[3]

        def unit_bank(at, u):
            return SB + (at[3] * NU + u) % RING

        def batches(eng, batch):
            batch(0, 0, 0, True, False)
            with eng.Fori(0, B // 2 - 1) as i:
                batch(2 * i + 1, 1, i, False, False)
                batch(2 * i + 2, 0, i + 1, False, False)
            batch(B - 1, 1, B // 2 - 1, False, True)

        def of_parity(tile, j, t, h):
            return tile[:, j, t].rearrange("p (g h x) r -> p g h x r", h=2, x=G)[:, :, h]

        @block.sync
        def _(sp):
            load_stack(sp, stacks, 1, parts_dram, 1, stacks_loaded[1])
            sp.dma_start(bo[:], W["bo"].partition_broadcast(P)).then_inc(bo_loaded, 16)
            for h in range(2):
                for x in range(G):
                    src = W["Wo"].rearrange("(g h x d) n -> h x d g n", h=2, x=G, d=DK)[h, x]
                    sp.dma_start(wo[x * ROWS + h * DK:x * ROWS + (h + 1) * DK], src).then_inc(wo_loaded, 16)
            with sp.Fori(0, B // 2 - 1) as i:
                for j in range(2):
                    n = 2 * i + 2 + j
                    sp.wait_ge(scoredT, (n + 1) * H)
                    load_stack(sp, stacks, j, parts_dram, n, stacks_loaded[j])

        @block.gpsimd
        def _(pool):
            pool.memset(top_row[:], 0.0)
            pool.memset(v[:], 0.0)
            pool.drain()
            for h in range(2):
                for j in range(2):
                    for t in range(TPB):
                        pool.memset(of_parity(v, j, t, h)[:, :, :, (1 - h) * DK], 1.0)
            pool.drain()
            pool.sem_inc(blank_ready, 1)
            pool.memset(wide_share[:], 0.0)
            pool.memset(ones[:], 1.0)
            if fill:
                pool.memset(zeros[:], 0.0)
            pool.drain()
            pool.wait_ge(bo_loaded, 16)
            pool.tensor_tensor(m["xres"][:], m["xres"][:], bo[:].unsqueeze(1).to_broadcast([P, NT, D]), ALU.add).then_inc(bo_joined, 1)
            zero_parts = [buf.rearrange("r d -> (r d)").rearrange("(p f) -> p f", p=P) for buf in fill]

            def widen(n, g):
                pool.wait_ge(share_ready, ready(n * NG + g))
                h = g % 2
                pool.tensor_tensor(wide_share[:, h, :, h * DK:(h + 1) * DK],
                                   share[:, h].rearrange("p t x -> p (t x)").unsqueeze(2).to_broadcast([P, TPB * G, DK]),
                                   ones[:].unsqueeze(1).to_broadcast([P, TPB * G, DK]), ALU.mult).then_inc(share_wide, 1)

            with pool.Fori(0, B) as n:
                for g in range(NG):
                    widen(n, g)
                    if g < len(fill):
                        cols = zero_parts[g].shape[1] // B
                        pool.dma_start(zero_parts[g][:, bass.ds(n * cols, cols)], zeros[:, 0:cols]).then_inc(zeros_stored, 16)
            if fill:
                pool.wait_ge(zeros_stored, 16 * len(fill) * B)

        @block.vector
        def _(dve):
            lead(dve, reduced, RING)
            lead(dve, normed, 2)
            lead(dve, out_taken, 1)

            def reduce(at, u):
                qt, x, heads = UNITS[u]
                dve.wait_ge(scored, ready(group(at) * NU + u))
                src = ps[:, unit_bank(at, u), :].rearrange("p (h k) -> p h k", h=heads)[:, :, 0:keys(qt)]
                dve.tensor_reduce(top[:, at[3] % 2, qt, x:x + heads], src, AX.X, ALU.max).then_inc(reduced, 1)

            def tops(at):
                g = at[3]
                tp, pt = top[:, g % 2], top_parts[:, g % 2]
                dve.drain()
                if causal:
                    dve.tensor_scalar(tp, tp, FLOOR, None, ALU.max)
                    dve.drain()
                dve.tensor_copy(pt[:, :, 0], tp)
                dve.drain()
                dve.tensor_tensor(pt[:, :, 1], tp, pt[:, :, 0], ALU.subtract).then_inc(top_ready, 1)

            def values(n, j):
                for t in range(TPB):
                    src = vals[:, bass.ds(n * TPB + t, 1), :, :].rearrange("p a (g h x) d -> p (a g) h x d", h=2, x=G)
                    for h in range(2):
                        last = dve.tensor_copy(of_parity(v, j, t, h)[:, :, :, h * DK:(h + 1) * DK], src[:, :, h])
                last.then_inc(v_ready, 1)

            def invert(at):
                g = at[3]
                dve.wait_ge(summed, ready(group(at)))
                dst = share[:, g % 2].rearrange("p t x -> p (t x)")
                if causal:
                    dve.tensor_scalar(dst, sums, 1e-30, None, ALU.max)
                    dve.drain()
                    dve.reciprocal(dst, dst).then_inc(share_ready, 1)
                else:
                    dve.reciprocal(dst, sums).then_inc(share_ready, 1)

            def normalize(at):
                g = at[3]
                dve.wait_ge(spread, ready(group(at)))
                pair = oT[:, at[1], g // 2]
                if g % 2 == 0:
                    dve.tensor_tensor(pair, o[:, 0], ps[:, OB, S:2 * S], ALU.mult).then_inc(normed, 1)
                else:
                    dve.tensor_tensor(o_odd[:], o[:, 1], ps[:, OB + 1, S:2 * S], ALU.mult)
                    dve.drain()
                    dve.tensor_tensor(pair, pair, o_odd[:], ALU.add).then_inc(normed, 1)

            def residual(n):
                dve.wait_ge(out_made, ready(n))
                xt = m["xres"][:, bass.ds(n * TPB, TPB), :]
                dve.tensor_tensor(xt, xt, ps[:, XB, :].rearrange("p (t d) -> p t d", t=TPB), ALU.add).then_inc(out_taken, 1)

            def statistics(n):
                dve.drain()
                for t in range(TPB):
                    dve.bn_stats(stats[:, t, :], m["xres"][:, bass.ds(n * TPB + t, 1), :].rearrange("p a d -> p (a d)"))

            def aggregate(n):
                dve.drain()
                for t in range(TPB):
                    dve.bn_aggr(mv[:, t, :], stats[:, t, :])
                dve.drain()
                dve.tensor_copy(m["mv"][:, bass.ds(n * TPB, TPB), :], mv[:])

            def batch(n, j, r, first, last):
                for g in range(NG):
                    at = (n, j, r, g)
                    more, started = not (last and g == NG - 1), not (first and g == 0)
                    for u in range(4):
                        if u == 3 and started:
                            invert(prior(at))
                        if more and u < NU:
                            reduce(after(at), u)
                        if u == 0 and g == 3 and not first:
                            statistics(n - 1)
                    if more:
                        tops(after(at))
                    if started:
                        normalize(prior(at))
                    if g == 2 and not first:
                        residual(n - 1)
                    if g == 3 and not first:
                        aggregate(n - 1)
                    if g == 1 and not last:
                        values(n + 1, 1 - j)
                if first:
                    dve.wait_ge(bo_joined, 1)

            for u in range(NU):
                reduce((0, 0, 0, 0), u)
            tops((0, 0, 0, 0))
            dve.wait_ge(blank_ready, 1)
            values(0, 0)
            batches(dve, batch)
            invert((B - 1, 1, None, NG - 1))
            normalize((B - 1, 1, None, NG - 1))
            residual(B - 1)
            statistics(B - 1)
            aggregate(B - 1)

        @block.scalar
        def _(act):
            lead(act, exped, RING)
            act.wait_ge(blank_ready, 1)

            def take(at):
                g = at[3]
                act.wait_ge(valued, ready(group(at), 2))
                act.wait_ge(normed, free(group(at)))
                act.activation(o[:, g % 2], ps[:, OB + g % 2, 0:S], ACT.Copy).then_inc(o_ready, 1)

            def batch(n, j, r, first, last):
                for g in range(NG):
                    at = (n, j, r, g)
                    act.wait_ge(top_turned, ready(group(at)))
                    act.activation(top_row[0:2 * G, g % 2, :], ps[0:2 * G, MB, 0:S], ACT.Copy).then_inc(row_ready, 1)
                    if not (first and g == 0):
                        take(prior(at))
                    act.wait_ge(valued, free(group(at)))
                    for x in range(G):
                        act.wait_ge(scoredT, ready(n * H + g * G + x, AHEAD))
                        act.activation(probs[:, g % 2, x, 0:WIDE], ps[:, TB + x % RING, 0:WIDE], ACT.Exp, scale=DK ** -0.5).then_inc(exped, 1)

            batches(act, batch)
            take((B - 1, 1, None, NG - 1))

        @block.tensor
        def _(pe):
            lead(pe, valued, 2)
            lead(pe, scoredT, AHEAD)

            def score(at, u):
                n, j, r, g = at
                qt, x0, heads = UNITS[u]
                if g == 0 and u == 0:
                    if not (isinstance(n, int) and n == 0):
                        pe.wait_ge(stacks_loaded[j], 16 * len(STACK_Q) * 2 * (r + j))
                pe.wait_ge(reduced, free(group(at) * NU + u))
                for x in range(heads):
                    h = g * G + x0 + x
                    out = ps[:, unit_bank(at, u), x * 512 // heads:x * 512 // heads + keys(qt)]
                    last = pe.matmul(out, qs[:, j, h, qt * P:(qt + 1) * P], ks[:, j, h, 0:keys(qt)], start=True, stop=not causal)
                    if causal:
                        last = pe.matmul(out, m["identb"][:], closed(n, 0, qt, 0, keys(qt)), start=False, stop=True)
                last.then_inc(scored, 1)

            def closed(n, w, t, lo, hi):
                return shut[:, w, bass.ds(n, 1), t, lo:hi].rearrange("p a k -> p (a k)")

            def turn_tops(at):
                g = at[3]
                pe.wait_ge(top_ready, ready(group(at)))
                for t in range(TPB):
                    last = pe.matmul(ps[0:2 * G, MB, t * P:(t + 1) * P], top_parts[:, g % 2, t].rearrange("p a g -> p (a g)"),
                                     m["identb"][:], start=True, stop=True)
                last.then_inc(top_turned, 1)

            def scoreT(at, x):
                n, j, r, g = at
                h = g * G + x
                if x == 0:
                    pe.wait_ge(row_ready, ready(group(at)))
                pe.wait_ge(exped, free(n * H + h))
                col = 0
                for kt in range(TPB):
                    q0 = first_q(kt)
                    out = ps[:, TB + x % RING, col:col + S - q0]
                    col += S - q0
                    pe.matmul(out, ks[:, j, h, kt * P:(kt + 1) * P], qs[:, j, h, q0:S], start=True, stop=False)
                    if causal:
                        pe.matmul(out, m["identb"][:], closed(n, 1, kt, q0, S), start=False, stop=False)
                    last = pe.matmul(out, m["minus"][:, x, :], top_row[:, g % 2, q0:S], start=False, stop=True)
                last.then_inc(scoredT, 1)

            def value(at):
                n, j, r, g = at
                if g == 0:
                    pe.wait_ge(v_ready, n + 1)
                pe.wait_ge(normed, free(group(at)))
                pe.wait_ge(exped, ready(n * H + g * G + G - 1, RING))
                for kt in range(TPB):
                    q0 = first_q(kt)
                    for x in range(G):
                        last = pe.matmul(ps[x * ROWS:(x + 1) * ROWS, OB + g % 2, q0:S], v[:, j, kt, g * G + x, :],
                                         probs[:, g % 2, x, kt * S:kt * S + S - q0], start=kt == 0, stop=kt == TPB - 1,
                                         tile_position=(0, x * ROWS))
                last.then_inc(valued, 1)

            def turn_sums(at):
                g = at[3]
                pe.wait_ge(o_ready, ready(group(at)))
                for t in range(TPB):
                    last = pe.matmul(sums[:, t * G:(t + 1) * G], o[:, g % 2, t * P:(t + 1) * P], m["sum_row"][:, g % 2], start=True, stop=True)
                last.then_inc(summed, 1)

            def spread_shares(at):
                g = at[3]
                pe.wait_ge(share_wide, ready(group(at)))
                for t in range(TPB):
                    for x in range(G):
                        last = pe.matmul(ps[x * ROWS:(x + 1) * ROWS, OB + g % 2, S + t * P:S + (t + 1) * P],
                                         wide_share[:, g % 2, t * G + x, :], m["ident"][:], start=True, stop=True,
                                         tile_position=(0, x * ROWS))
                last.then_inc(spread, 1)

            def project(n, j):
                pe.wait_ge(normed, ready(n * NG + NG - 1, 2))
                pe.wait_ge(out_taken, free(n))
                for t in range(TPB):
                    for q in range(NG // 2):
                        last = pe.matmul(ps[:, XB, t * D:(t + 1) * D], oT[:, j, q, t * P:(t + 1) * P], wo[:, q, :],
                                         start=q == 0, stop=q == NG // 2 - 1)
                last.then_inc(out_made, 1)

            def batch(n, j, r, first, last):
                for g in range(NG):
                    at = (n, j, r, g)
                    more, started = not (last and g == NG - 1), not (first and g == 0)

                    def score_next(u):
                        if more and u < NU:
                            score(after(at), u)

                    turn_tops(at)
                    score_next(0)
                    if started:
                        value(prior(at))
                    score_next(1)
                    scoreT(at, 0)
                    score_next(2)
                    scoreT(at, 1)
                    if started:
                        turn_sums(prior(at))
                    score_next(3)
                    scoreT(at, 2)
                    scoreT(at, 3)
                    if started:
                        spread_shares(prior(at))
                    if g == 1 and not first:
                        project(n - 1, 1 - j)
                if first:
                    pe.wait_ge(wo_loaded, 16 * 2 * G)

            for u in range(NU):
                score((0, 0, 0, 0), u)
            pe.wait_ge(blank_ready, 1)
            batches(pe, batch)
            ended = (B - 1, 1, None, NG - 1)
            value(ended)
            turn_sums(ended)
            spread_shares(ended)
            project(B - 1, 1)


def route_block(nc, m, layer, E, a, hall):
    ctx = ExitStack()
    with ctx:
        def sb(name, shape, dt=F32):
            return ctx.enter_context(nc.sbuf_tensor(f"{name}_r{layer}", shape, dt))

        signal = ctx.enter_context(signals(nc, m["resting"]))

        def sem(name):
            return signal(f"{name}_r{layer}")

        def sems(name, n=2):
            return [sem(f"{name}{j}") for j in range(n)]

        capped = layer == 1
        N2 = 2 * NT
        wr = sb("wr", [P, DC, E])
        bias = sb("bias", [P, 2, E])
        lng = sb("lng", [P, 2, D])
        hs = sb("hs", [P, 2, TPB, D])
        hn = sb("hn", [P, 2, TPB, D])
        hT = sb("hT", [P, 2, DC, S])
        logits = sb("logits", [P, NT, E])
        left = sb("left", [P, NT, E])
        fall = sb("fall", [P, E])
        rise = sb("rise", [P, E])
        steps = sb("steps", [P, NT])
        upto = sb("upto", [P, E, E])
        blocks = sb("blocks", [P, NB0])
        best = sb("best", [P, 2, NT])
        key = sb("key", [P, NT, E])
        keymax = sb("keymax", [P, NT])
        pick = sb("pick", [P, 2, NT, E])
        sums = sb("sums", [P, 2, N2, E])
        work = sb("work", [P, N2, E])
        load = sb("load", [P, E])
        full = sb("full", [P, E, NT])
        nblk = sb("nblk", [P, E])
        cum = sb("cum", [P, E, E])
        last_blk = sb("last_blk", [P, E])
        base = sb("base", [P, E])
        past = sb("past", [P, NB0, E])
        owner = sb("owner", [P, NB0])
        pos = sb("pos", [P, N2])
        home = sb("home", [P, N2])
        kept = sb("kept", [P, N2])
        slotf = sb("slotf", [P, N2])
        e2 = sb("e2", [P, NT])
        ps = ctx.enter_context(nc.psum_tensor(f"route_ps_{layer}", [P, 8, 512], F32))
        TB, LB, RB, CB = 0, 2, 3, 4

        w_loaded, const_ready = sem("w_loaded"), sem("const_ready")
        var_ready, root_ready = sem("var_ready"), sem("root_ready")
        h_ready, turned, hT_ready = sems("h_ready"), sems("turned"), sems("hT_ready")
        logits_made = sems("logits_made")
        kept_copy = sems("kept_copy")
        gap_ready, gap_exp = sem("gap_ready"), sem("gap_exp")
        sums_ready, ranks_made = sem("sums_ready"), sem("ranks_made")
        block = ctx.enter_context(nc.Block())

        loads = 16 * 3

        @block.sync
        def _(sp):
            sp.dma_start(wr[:], a["Wr" if capped else "Wg"].rearrange("(c p) e -> p c e", p=P)).then_inc(w_loaded, 16)
            for x, name in enumerate(("ln_g", "ln_b") if capped else ("bg", "bias")):
                dst = lng if capped else bias
                sp.dma_start(dst[:, x, :], a[name].partition_broadcast(P)).then_inc(w_loaded, 16)

        @block.gpsimd
        def _(pool):
            def small(out, pattern, base=0, channel=0):
                return pool.iota(out, pattern=pattern, base=base, channel_multiplier=channel,
                                 allow_small_or_imprecise_dtypes=True)
            primed(pool, *kept_copy)
            small(fall[:], [[-1, E]], base=E)
            small(rise[:], [[1, E]])
            small(steps[:], [[P, NT]])
            small(blocks[:], [[1, NB0]])
            small(upto[:], [[-1, E], [1, E]])
            pool.drain()
            pool.tensor_scalar(upto[:], upto[:], 0.0, None, ALU.is_le).then_inc(const_ready, 1)
            with pool.Fori(0, B // 2) as i:
                for j in range(2):
                    pool.wait_ge(h_ready[j], done(i))
                    pool.tensor_copy(hall[:, bass.ds((2 * i + j) * TPB, TPB), :], hs[:, j]).then_inc(kept_copy[j], 1)

        @block.scalar
        def _(act):
            primed(act, *hT_ready)
            rstd_steps_scalar(act, m, var_ready, root_ready)
            with act.Fori(0, B // 2) as i:
                for j in range(2):
                    act.wait_ge(turned[j], done(i))
                    act.wait_ge(logits_made[j], before(i))
                    act.activation(hT[:, j].rearrange("p c s -> p (c s)"), ps[:, TB + j, :], ACT.Copy).then_inc(hT_ready[j], 1)
            act.wait_ge(gap_ready, 1)
            act.activation(e2[:], e2[:], ACT.Exp).then_inc(gap_exp, 1)

        @block.tensor
        def _(pe):
            primed(pe, *turned, *logits_made)
            pe.wait_ge(w_loaded, loads)
            def turn(i, j):
                pe.wait_ge(h_ready[j], done(i))
                pe.wait_ge(hT_ready[j], before(i))
                for t in range(TPB):
                    for c in range(DC):
                        last = pe.transpose(ps[:, TB + j, c * S + t * P:c * S + (t + 1) * P], hs[:, j, t, c * P:(c + 1) * P], m["ident"][:])
                last.then_inc(turned[j], 1)

            def pair(i, more):
                for j in range(2):
                    if j == 0:
                        turn(i, 1)
                    elif more:
                        turn(i + 1, 0)
                    pe.wait_ge(hT_ready[j], done(i))
                    for t in range(TPB):
                        for c in range(DC):
                            last = pe.matmul(ps[:, LB, bass.ds(((2 * i + j) * TPB + t) * E, E)], hT[:, j, c, t * P:(t + 1) * P], wr[:, c, :],
                                             start=c == 0, stop=c == DC - 1)
                    last.then_inc(logits_made[j], 1)

            turn(0, 0)
            with pe.Fori(0, B // 2 - 1) as i:
                pair(i, True)
            pair(B // 2 - 1, False)
            pe.wait_ge(sums_ready, 1)
            picks = pick[:].rearrange("p c t e -> p (c t e)")
            incl = sums[:, 0].rearrange("p n e -> p (n e)")
            pe.matmul(ps[:, RB, 0:N2 * E], m["before"][:], picks, start=True, stop=False, skip_group_check=True)
            pe.matmul(ps[:, RB, E:N2 * E], m["ones"][:], incl[:, 0:(N2 - 1) * E], start=False, stop=True, skip_group_check=True)
            pe.matmul(ps[:, CB, 0:E], m["ones"][:], incl[:, (N2 - 1) * E:N2 * E], start=True, stop=True).then_inc(ranks_made, 1)

        @block.vector
        def _(dve):
            primed(dve, *h_ready)
            rstd_steps_vector(dve, m, var_ready, root_ready)
            dve.wait_ge(w_loaded, loads)
            dve.wait_ge(const_ready, 1)
            if not capped:
                dve.tensor_tensor(bias[:, 0], bias[:, 0], bias[:, 1], ALU.add)
                dve.drain()
            with dve.Fori(0, B // 2) as i:
                for j in range(2):
                    dve.wait_ge(turned[j], before(i))
                    dve.wait_ge(kept_copy[j], before(i))
                    dst = hn if capped else hs
                    for t in range(TPB):
                        n = (2 * i + j) * TPB + t
                        last = dve.tensor_scalar(dst[:, j, t, :], m["xres"][:, bass.ds(n, 1), :].rearrange("p a d -> p (a d)"),
                                                 m["mv"][:, bass.ds(n, 1), 0], m["rstd"][:, bass.ds(n, 1)], ALU.subtract, ALU.mult)
                    if capped:
                        dve.drain()
                        dve.tensor_tensor(hn[:, j], hn[:, j], lng[:, 0].unsqueeze(1).to_broadcast([P, TPB, D]), ALU.mult)
                        dve.drain()
                        last = dve.tensor_tensor(hs[:, j], hn[:, j], lng[:, 1].unsqueeze(1).to_broadcast([P, TPB, D]), ALU.add)
                    last.then_inc(h_ready[j], 1)
            for j in range(2):
                dve.wait_ge(logits_made[j], done(B // 2 - 1))
            made = ps[:, LB, 0:NT * E].rearrange("p (t e) -> p t e", t=NT)
            if capped:
                dve.tensor_copy(logits[:], made)
            else:
                dve.tensor_tensor(logits[:], made, bias[:, 0].unsqueeze(1).to_broadcast([P, NT, E]), ALU.add)
            dve.drain()

            def then(ins):
                dve.drain()

            def over_tiles(ap):
                return ap.unsqueeze(1).to_broadcast([P, NT, E])

            src = logits
            for c in range(2):
                then(dve.tensor_reduce(best[:, c], src[:], AX.X, ALU.max))
                then(dve.tensor_tensor(key[:], src[:], best[:, c].unsqueeze(2).to_broadcast([P, NT, E]), ALU.is_equal))
                then(dve.tensor_tensor(key[:], key[:], over_tiles(fall[:]), ALU.mult))
                then(dve.tensor_reduce(keymax[:], key[:], AX.X, ALU.max))
                then(dve.tensor_tensor(pick[:, c], over_tiles(fall[:]), keymax[:].unsqueeze(2).to_broadcast([P, NT, E]), ALU.is_equal))
                if c == 0:
                    then(dve.scalar_tensor_tensor(out=left[:], in0=pick[:, 0], scalar=MASKED, in1=logits[:], op0=ALU.mult, op1=ALU.add))
                    src = left
            dve.tensor_tensor(e2[:], best[:, 1], best[:, 0], ALU.subtract).then_inc(gap_ready, 1)
            at = pick[:].rearrange("p c t e -> p (c t) e")
            reach, n = 1, 0
            while reach < N2:
                nxt = sums[:, n % 2]
                dve.tensor_copy(nxt[:, 0:reach], at[:, 0:reach])
                then(dve.tensor_tensor(nxt[:, reach:N2], at[:, reach:N2], at[:, 0:N2 - reach], ALU.add))
                at = nxt
                reach *= 2
                n += 1
            assert n % 2 == 1
            dve.sem_inc(sums_ready, 1)
            dve.wait_ge(gap_exp, 1)
            then(dve.tensor_scalar(m["gate"][:, 0], e2[:], 1.0, None, ALU.add))
            then(dve.reciprocal(m["gate"][:, 0], m["gate"][:, 0]))
            then(dve.tensor_tensor(m["gate"][:, 1], m["gate"][:, 0], e2[:], ALU.mult))

            dve.wait_ge(ranks_made, 1)
            ranks = ps[:, RB, 0:N2 * E].rearrange("p (n e) -> p n e", n=N2)
            picks = pick[:].rearrange("p c t e -> p (c t) e")

            def over_all(ap):
                return ap.unsqueeze(1).to_broadcast([P, N2, E])

            if capped:
                then(dve.tensor_tensor(work[:], ranks, picks, ALU.mult))
                then(dve.tensor_reduce(pos[:], work[:], AX.X, ALU.add))
                then(dve.tensor_tensor(work[:], over_all(rise[:]), picks, ALU.mult))
                then(dve.tensor_reduce(home[:], work[:], AX.X, ALU.add))
                then(dve.tensor_scalar(kept[:], pos[:], float(CAP), None, ALU.is_lt))
                then(dve.scalar_tensor_tensor(out=slotf[:], in0=home[:], scalar=float(CAP), in1=pos[:], op0=ALU.mult, op1=ALU.add))
                gates = m["gate"][:].rearrange("p c t -> p (c t)")
                then(dve.tensor_tensor(gates, gates, kept[:], ALU.mult))
                then(dve.tensor_tensor(home[:], slotf[:], kept[:], ALU.mult))
                dve.tensor_copy(m["slot_back"][:].rearrange("p c t -> p (c t)"), home[:])
                then(dve.tensor_scalar(kept[:], kept[:], -OUT_OF_RANGE, OUT_OF_RANGE, ALU.mult, ALU.add))
                then(dve.tensor_tensor(slotf[:], slotf[:], kept[:], ALU.add))
                dve.tensor_copy(m["slot"][:].rearrange("p c t -> p (c t)"), slotf[:])
            else:
                then(dve.tensor_copy(load[:], ps[:, CB, 0:E]))
                then(dve.tensor_tensor(full[:], load[:].unsqueeze(2).to_broadcast([P, E, NT]), steps[:].unsqueeze(1).to_broadcast([P, E, NT]), ALU.is_gt))
                then(dve.tensor_reduce(nblk[:], full[:], AX.X, ALU.add))
                then(dve.tensor_tensor(cum[:], nblk[:].unsqueeze(1).to_broadcast([P, E, E]), upto[:], ALU.mult))
                then(dve.tensor_reduce(last_blk[:], cum[:], AX.X, ALU.add))
                then(dve.tensor_tensor(base[:], last_blk[:], nblk[:], ALU.subtract))
                then(dve.tensor_scalar(base[:], base[:], float(P), None, ALU.mult))
                then(dve.tensor_tensor(work[:], ranks, over_all(base[:]), ALU.add))
                then(dve.tensor_tensor(work[:], work[:], picks, ALU.mult))
                then(dve.tensor_reduce(pos[:], work[:], AX.X, ALU.add))
                dve.tensor_copy(m["slot_back"][:].rearrange("p c t -> p (c t)"), pos[:])
                dve.tensor_copy(m["slot"][:].rearrange("p c t -> p (c t)"), pos[:])
                then(dve.tensor_tensor(past[:], last_blk[:].unsqueeze(1).to_broadcast([P, NB0, E]), blocks[:].unsqueeze(2).to_broadcast([P, NB0, E]), ALU.is_le))
                then(dve.tensor_reduce(owner[:], past[:], AX.X, ALU.add))
                then(dve.tensor_scalar(owner[:], owner[:], float(E - 1), None, ALU.min))
                dve.tensor_copy(m["block_expert"][:], owner[:])


def experts0_block(nc, m, a, xe, ye):
    ctx = ExitStack()
    with ctx:
        def sb(name, shape, dt=F32):
            return ctx.enter_context(nc.sbuf_tensor(f"{name}_e0", shape, dt))

        signal = ctx.enter_context(signals(nc, m["resting"]))

        def sem(name):
            return signal(f"{name}_e0")

        def sems(name, n):
            return [sem(f"{name}{j}") for j in range(n)]

        RING = 4
        b1 = sb("b1", [P, E0, FC0])
        b2 = sb("b2", [P, E0, D])
        w = sb("w", [P, RING, W0])
        x = sb("x", [P, RING, D])
        xT = sb("xT", [P, 2, DC, P])
        hid = sb("hid", [P, 2, FC0, P])
        y = sb("y", [P, RING, D])
        ps = ctx.enter_context(nc.psum_tensor("e0_ps", [P, 8, 512], F32))
        XB, HB, YB = 0, 2, 4

        b_loaded = sem("b_loaded")
        w_loaded, x_loaded, y_stored = sems("w_loaded", RING), sems("x_loaded", RING), sems("y_stored", RING)
        turned, xT_ready, hid_made, hid_ready = sem("turned"), sem("xT_ready"), sem("hid_made"), sem("hid_ready")
        y_made, y_ready, y_free = sem("y_made"), sem("y_ready"), sem("y_free")
        block = ctx.enter_context(nc.Block())

        TURNED, MADE, Y_MADE = RING, 2, RING

        def at(i, j):
            return (i, j) if j < RING else (i + 1, j - RING)

        def w1(j, c, f):
            return w[:, j, c * F0 + f * P:c * F0 + (f + 1) * P]

        def w2(j, f):
            return w[:, j, DC * F0 + f * D:DC * F0 + (f + 1) * D]

        @block.sync
        def _(sp):
            sp.dma_start(b1[:], a["b1"]).then_inc(b_loaded, 16)
            sp.dma_start(b2[:].rearrange("p e d -> p (e d)"), a["b2"].rearrange("e d -> (e d)").partition_broadcast(P)).then_inc(b_loaded, 16)
            with sp.Fori(0, NB0 // RING) as i:
                for j in range(RING):
                    n = RING * i + j
                    e = sp.value_load(m["block_expert"][0:1, bass.ds(n, 1)], min_val=0, max_val=E0 - 1)
                    sp.wait_ge(turned, free(n))
                    sp.dma_start(x[:, j], xe[bass.ds(n * P, P), :]).then_inc(x_loaded[j], 16)
                    sp.wait_ge(y_made, free(n))
                    sp.dma_start(w[:, j], a["W_0"][bass.ds(e, 1)].rearrange("a p f -> p (a f)")).then_inc(w_loaded[j], 16)

        @block.gpsimd
        def _(pool):
            lead(pool, y_free, RING)
            with pool.Fori(0, NB0 // RING) as i:
                for j in range(RING):
                    n = RING * i + j
                    pool.wait_ge(y_ready, ready(n, 2))
                    pool.dma_start(ye[bass.ds(n * P, P), :], y[:, j]).then_inc(y_stored[j], 16)
                    pool.wait_ge(y_stored[j], 16 * (i + 1))
                    pool.sem_inc(y_free, 1)

        @block.scalar
        def _(act):
            lead(act, hid_ready, 2)
            act.wait_ge(b_loaded, 32)
            with act.Fori(0, NB0 // RING) as i:
                for j in range(RING):
                    n = RING * i + j
                    e = act.value_load(m["block_expert"][0:1, bass.ds(n, 1)], min_val=0, max_val=E0 - 1)
                    act.wait_ge(hid_made, ready(n, MADE))
                    act.wait_ge(y_made, free(n) + Y_MADE - 2)
                    for f in range(FC0):
                        last = act.activation(hid[:, j % 2, f, :], ps[:, HB + j % 2, f * P:(f + 1) * P], ACT.Relu,
                                              bias=b1[:, bass.ds(e, 1), f])
                    last.then_inc(hid_ready, 1)

        @block.vector
        def _(dve):
            lead(dve, y_ready, 2)
            lead(dve, xT_ready, 2)
            dve.wait_ge(b_loaded, 32)

            def take_rows(i, j):
                n = RING * i + j
                dve.wait_ge(turned, ready(n, TURNED))
                dve.wait_ge(hid_made, free(n))
                dve.tensor_copy(xT[:, j % 2].rearrange("p c s -> p (c s)"), ps[:, XB + j % 2, 0:DC * P]).then_inc(xT_ready, 1)

            def take_sums(i, j):
                n = RING * i + j
                e = dve.value_load(m["block_expert"][0:1, bass.ds(n, 1)], min_val=0, max_val=E0 - 1)
                dve.wait_ge(y_made, ready(n, Y_MADE))
                dve.wait_ge(y_free, free(n))
                dve.tensor_tensor(y[:, j], ps[:, YB + j % 2, 0:D], b2[:, bass.ds(e, 1), :].rearrange("p a d -> p (a d)"),
                                  ALU.add).then_inc(y_ready, 1)

            def round_of(i, more):
                for j in range(RING):
                    if j + 2 < RING or more:
                        take_rows(*at(i, j + 2))
                    take_sums(i, j)

            take_rows(0, 0)
            take_rows(0, 1)
            with dve.Fori(0, NB0 // RING - 1) as i:
                round_of(i, True)
            round_of(NB0 // RING - 1, False)

        @block.tensor
        def _(pe):
            lead(pe, turned, TURNED)
            lead(pe, hid_made, MADE)
            lead(pe, y_made, Y_MADE)

            def turn(i, j):
                n = RING * i + j
                pe.wait_ge(x_loaded[j], 16 * (i + 1))
                pe.wait_ge(xT_ready, free(n))
                for c in range(DC):
                    last = pe.transpose(ps[:, XB + j % 2, c * P:(c + 1) * P], x[:, j, c * P:(c + 1) * P], m["ident"][:])
                last.then_inc(turned, 1)

            def first(i, j):
                n = RING * i + j
                pe.wait_ge(w_loaded[j], 16 * (i + 1))
                pe.wait_ge(xT_ready, ready(n, 2))
                pe.wait_ge(hid_ready, free(n))
                for f in range(FC0):
                    for c in range(DC):
                        last = pe.matmul(ps[:, HB + j % 2, f * P:(f + 1) * P], w1(j, c, f), xT[:, j % 2, c, :], start=c == 0, stop=c == DC - 1)
                last.then_inc(hid_made, 1)

            def second(i, j):
                n = RING * i + j
                pe.wait_ge(hid_ready, ready(n, 2))
                pe.wait_ge(y_ready, free(n))
                for f in range(FC0):
                    last = pe.matmul(ps[:, YB + j % 2, 0:D], hid[:, j % 2, f, :], w2(j, f), start=f == 0, stop=f == FC0 - 1)
                last.then_inc(y_made, 1)

            def round_of(i, more):
                for j in range(RING):
                    if j + 1 < RING or more:
                        first(*at(i, j + 1))
                    if j + 2 < RING or more:
                        turn(*at(i, j + 2))
                    second(i, j)

            turn(0, 0)
            turn(0, 1)
            first(0, 0)
            with pe.Fori(0, NB0 // RING - 1) as i:
                round_of(i, True)
            round_of(NB0 // RING - 1, False)


def experts1_block(nc, m, a, hall, xe, ye, out):
    ctx = ExitStack()
    with ctx:
        def sb(name, shape, dt=F32):
            return ctx.enter_context(nc.sbuf_tensor(f"{name}_e1", shape, dt))

        signal = ctx.enter_context(signals(nc, m["resting"]))

        def sem(name):
            return signal(f"{name}_e1")

        def sems(name, n=2):
            return [sem(f"{name}{j}") for j in range(n)]

        ROUNDS = XT // 2
        UN = 2 * FC1
        w = sb("w", [P, 2, W1C])
        wp = sb("wp", [P, 2, 2, W1C], F32R)
        x = sb("x", [P, XT, D])
        staged = sb("staged", [P, DC, XT * P])
        xT = sb("xT", [P, 2, DC, XT * P], F32R)
        act_a = sb("act_a", [P, 2, HALF])
        hid = sb("hid", [P, 2, HALF])
        hidp = sb("hidp", [P, 2, 2, HALF], F32R)
        y = sb("y", [P, XT, D])
        back = sb("back", [P, NT, 2, D])
        ps = ctx.enter_context(nc.psum_tensor("e1_ps", [P, 8, 512], F32))
        AB, BB, YB, XB = 0, 2, 4, 7
        assert XT == 6

        w_loaded = sems("w_loaded")
        w_high, w_cut = sem("w_high"), sem("w_cut")
        shared_stored, slots_filled = sem("shared_stored"), sem("slots_filled")
        x_loaded, x_turned, x_staged = sem("x_loaded"), sem("x_turned"), sem("x_staged")
        x_high, x_cut = sem("x_high"), sem("x_cut")
        first_done, silu_ready, mixed = sem("first_done"), sem("silu_ready"), sem("mixed")
        hid_high, hid_cut, second_done = sem("hid_high"), sem("hid_cut"), sem("second_done")
        y_taken = [sem("y_taken_scalar"), sem("y_taken_vector")]
        y_stored, y_free = sem("y_stored"), sem("y_free")
        back_loaded, joined, out_stored = sem("back_loaded"), sem("joined"), sem("out_stored")
        block = ctx.enter_context(nc.Block())

        chunks = a["W_1"].rearrange("e f p n -> (e f) p n")

        class Lot:
            def __init__(self, v, tiles=None):
                self.v, self.tiles = v, tiles
                self.count = XT if tiles is None else len(tiles)
                self.first_row = [0, XT // 2 * P]
                self.rows = [self.count // 2 * P, (self.count // 2 * P) if tiles else CAP - XT // 2 * P]

        SHARED = [range(0, XT), range(XT, NT - XT), range(NT - XT, NT)]
        START = Lot(0, SHARED[0])
        THEN, LAST_LOT = Lot(E1 + 1, SHARED[1]), Lot(E1 + 2, SHARED[2])

        def lots(eng, body):
            body(START, lambda c: c, Lot(1), None)
            body(Lot(1), lambda c: FC1 + c, Lot(2), START)
            with eng.Fori(2, E1 + 1) as v:
                body(Lot(v), lambda c: v * FC1 + c, Lot(v + 1), Lot(v - 1))
            shared = (E1 + 1) * FC1
            body(THEN, lambda c: shared + c % FC1, LAST_LOT, Lot(E1))
            body(LAST_LOT, lambda c: shared + c, None, THEN)

        TURN_AT = {UN // 2 - 2: 0, UN // 2: 1, UN // 2 + 2: 2}
        TURN_LATE = {UN - 5: 0, UN - 4: 1, UN - 3: 2}
        assert len(TURN_AT) == len(TURN_LATE) == ROUNDS

        def turns(lot, u, following):
            r = (TURN_LATE if lot is START else TURN_AT).get(u)
            return r if following and r in rounds_of(following) else None

        def rounds_of(lot):
            return range(lot.count // 2)

        def halves(lot, half):
            return slice(lot.first_row[half], lot.first_row[half] + lot.count // 2 * P)

        def staged_by(lot, half):
            return ((half + 1) * (lot.count // 2) - 1) // 2

        @block.sync
        def _(sp):
            def load(n, c, row):
                sp.wait_ge(w_cut, free(n + c))
                sp.dma_start(w[:, c % 2], chunks[bass.ds(row, 1)].rearrange("a p n -> p (a n)")).then_inc(w_loaded[c % 2], 16)

            load(0, 0, 0)
            for half in range(2):
                t, row = XT + half * THEN.count // 2, E1 * CAP + THEN.first_row[half]
                sp.dma_start(xe[row:row + XT // 2 * P, :].rearrange("(n p) d -> p n d", p=P),
                             hall[:, t:t + XT // 2]).then_inc(shared_stored, 16)

            def body(lot, row, following, previous):
                v = lot.v
                rows_before = FC1 - 2 if lot is START else 2
                for c in range(1, rows_before):
                    load(v * FC1, c, row(c))
                if lot is START:
                    sp.wait_ge(shared_stored, 32)
                    sp.wait_ge(slots_filled, 16 * 2 * NT)
                if lot not in (THEN, LAST_LOT):
                    sp.wait_ge(x_turned, (v + 1) * ROUNDS + 1)
                    sp.dma_start(x[:], xe[bass.ds(v * CAP, XT * P), :].rearrange("(n p) d -> p n d", p=P)).then_inc(x_loaded, 16)
                for c in range(rows_before, FC1 + (following is not None)):
                    load(v * FC1, c, row(c))

            lots(sp, body)
            dst = out.rearrange("(n p) d -> p n d", p=P)
            done_tiles = LAST_LOT.tiles[0]
            sp.wait_ge(joined, 1)
            sp.dma_start(dst[:, 0:done_tiles], m["xres"][:, 0:done_tiles]).then_inc(out_stored, 16)
            sp.wait_ge(joined, 2)
            sp.dma_start(dst[:, done_tiles:NT], m["xres"][:, done_tiles:NT]).then_inc(out_stored, 16)
            sp.wait_ge(out_stored, 32)

        @block.gpsimd
        def _(pool):
            for c in range(2):
                for t in range(NT):
                    pool.indirect_dma_start(xe, bass.IndirectOffsetOnAxis(ap=m["slot"][:, c, t:t + 1], axis=0),
                                            hall[:, t, :], None, bounds_check=xe.shape[0] - 1,
                                            oob_is_err=False).then_inc(slots_filled, 16)
            primed(pool, y_free)
            with pool.Fori(0, E1) as e:
                for taken in y_taken:
                    pool.wait_ge(taken, done(e + 1))
                full = (XT - 1) * P
                pool.dma_start(ye[bass.ds(e * CAP, full), :].rearrange("(n p) d -> p n d", p=P), y[:, 0:XT - 1]).then_inc(y_stored, 16)
                pool.dma_start(ye[bass.ds(e * CAP + full, LAST), :], y[0:LAST, XT - 1]).then_inc(y_stored, 16)
                pool.wait_ge(y_stored, 32 * (e + 1))
                pool.sem_inc(y_free, 1)
            for t in range(NT):
                for c in range(2):
                    pool.indirect_dma_start(back[:, t, c], None, ye,
                                            bass.IndirectOffsetOnAxis(ap=m["slot_back"][:, c, t:t + 1], axis=0)).then_inc(back_loaded, 16)

        @block.scalar
        def _(act):
            primed(act, y_taken[0])

            def weights_high(n, c):
                act.wait_ge(w_loaded[c % 2], 16 * ((n + c - c % 2) // 2 + 1) if isinstance(n, int) else 16 * (n // 2 + c // 2 + 1))
                act.wait_ge(second_done, (n + c) * 2 + 2)
                act.activation(wp[:, c % 2, 0], w[:, c % 2], ACT.Copy).then_inc(w_high, 1)

            weights_high(0, 0)

            def rows_high(lot, half):
                act.wait_ge(x_staged, ready(lot.v * ROUNDS + staged_by(lot, half), 1))
                act.activation(xT[:, 0, :, halves(lot, half)], staged[:, :, halves(lot, half)], ACT.Copy).then_inc(x_high, 1)

            def take_y(lot, bank):
                act.wait_ge(second_done, ready(lot.v * UN + UN - 2 + bank, 4))
                last = act.activation(y[:, 2 * bank:2 * bank + 2].rearrange("p n d -> p (n d)"), ps[:, YB + bank], ACT.Copy)
                if bank == 1:
                    last.then_inc(y_taken[0], 1)

            rows_high(START, 0)
            rows_high(START, 1)

            def body(lot, row, following, previous):
                v = lot.v
                for u in range(UN):
                    k, n = v * UN + u, lot.rows[u % 2]
                    act.wait_ge(first_done, ready(k, 1))
                    act.wait_ge(mixed, free(k))
                    act.activation(act_a[:, u % 2, 0:n], ps[:, AB + u % 2, 0:n], ACT.Silu).then_inc(silu_ready, 1)
                    act.wait_ge(mixed, ready(k, 2))
                    act.wait_ge(second_done, k + 3)
                    act.activation(hidp[:, u % 2, 0, 0:n], hid[:, u % 2, 0:n], ACT.Copy).then_inc(hid_high, 1)
                    if u == 0 and previous and not previous.tiles:
                        take_y(previous, 1)
                    if following and u == UN - 2:
                        rows_high(following, 0)
                    if u % 2 == 0 and u // 2 + 1 < FC1 + (following is not None):
                        weights_high(v * FC1, u // 2 + 1)
                    if following:
                        if u == UN - 1:
                            rows_high(following, 1)
                if lot.tiles:
                    act.sem_inc(y_taken[0], 1)
                else:
                    act.wait_ge(y_free, before(v - 1))
                    take_y(lot, 0)

            lots(act, body)

        @block.vector
        def _(dve):
            lead(dve, w_cut, 2)
            lead(dve, mixed, 2)
            lead(dve, x_staged, 1)
            primed(dve, y_taken[1])

            def weights_rest(n, c):
                dve.wait_ge(w_high, ready(n + c))
                dve.tensor_tensor(wp[:, c % 2, 1], w[:, c % 2], wp[:, c % 2, 0].bitcast(F32), ALU.subtract).then_inc(w_cut, 1)

            def stage(lot, r):
                dve.wait_ge(x_turned, ready(lot.v * ROUNDS + r, 1))
                dve.tensor_copy(staged[:, :, r * 2 * P:(r + 1) * 2 * P], ps[:, XB, :].rearrange("p (c t) -> p c t", c=DC)).then_inc(x_staged, 1)

            def rows_rest(lot, half):
                dve.drain()
                dve.wait_ge(x_high, ready(lot.v * 2 + half))
                rows = halves(lot, half)
                dve.tensor_tensor(xT[:, 1, :, rows], staged[:, :, rows], xT[:, 0, :, rows].bitcast(F32), ALU.subtract).then_inc(x_cut, 1)

            def shared_joins(lot, lo, hi):
                xt = m["xres"][:, lot.tiles[lo]:lot.tiles[lo] + hi - lo].rearrange("p n d -> p (n d)")
                return dve.tensor_tensor(xt, xt, ps[:, YB + lo // 2:YB + hi // 2].rearrange("p b f -> p (b f)"), ALU.add)

            def routed_join(tiles):
                for c in range(2):
                    for t in tiles:
                        xt = m["xres"][:, t]
                        dve.scalar_tensor_tensor(out=xt, in0=back[:, t, c], scalar=m["gate"][:, c, t:t + 1], in1=xt, op0=ALU.mult, op1=ALU.add)
                    if c == 0:
                        dve.drain()

            def finish(lot):
                v = lot.v
                if lot.tiles:
                    dve.drain()
                    dve.wait_ge(second_done, ready(v * UN + UN - 2, 4))
                    shared_joins(lot, 0, 2)
                    dve.wait_ge(second_done, ready(v * UN + UN - 1, 4))
                    shared_joins(lot, 2, lot.count).then_inc(y_taken[1], 1)
                else:
                    dve.wait_ge(second_done, ready(v * UN + UN - 1, 4))
                    dve.wait_ge(y_free, before(v - 1))
                    dve.tensor_copy(y[:, XT - 2], ps[:, YB + 2, 0:D])
                    dve.tensor_copy(y[0:LAST, XT - 1], ps[0:LAST, YB + 2, D:2 * D]).then_inc(y_taken[1], 1)

            for r in rounds_of(START):
                stage(START, r)
                if r == staged_by(START, 0):
                    weights_rest(0, 0)
                    rows_rest(START, 0)
            rows_rest(START, 1)

            def body(lot, row, following, previous):
                v = lot.v
                for u in range(UN):
                    k, n = v * UN + u, lot.rows[u % 2]
                    dve.drain()
                    dve.wait_ge(silu_ready, ready(k))
                    dve.tensor_tensor(hid[:, u % 2, 0:n], act_a[:, u % 2, 0:n], ps[:, BB + u % 2, 0:n], ALU.mult).then_inc(mixed, 1)
                    dve.wait_ge(hid_high, ready(k))
                    dve.tensor_tensor(hidp[:, u % 2, 1, 0:n], hid[:, u % 2, 0:n], hidp[:, u % 2, 0, 0:n].bitcast(F32),
                                      ALU.subtract).then_inc(hid_cut, 1)
                    if u == 0 and previous:
                        finish(previous)
                    if following and u == UN - 2:
                        rows_rest(following, 0)
                    if u % 2 == 0 and u // 2 + 1 < FC1 + (following is not None):
                        weights_rest(v * FC1, u // 2 + 1)
                    if following:
                        if turns(lot, u, following) is not None:
                            stage(following, turns(lot, u, following))
                        if u == UN - 1:
                            rows_rest(following, 1)
                    else:
                        if u == 0:
                            dve.wait_ge(back_loaded, 16 * 2 * NT)
                        if u % 2:
                            routed_join((u - 1, u))
                if not following:
                    dve.drain()
                    dve.sem_inc(joined, 1)
                    finish(lot)
                    dve.drain()
                    dve.sem_inc(joined, 1)

            lots(dve, body)

        PASSES = ((0, 0), (0, 1), (1, 0))

        @block.tensor
        def _(pe):
            lead(pe, x_turned, 1)
            lead(pe, first_done, 1)
            lead(pe, second_done, 4)

            def turn(lot, r):
                if lot in (START, LAST_LOT):
                    src = hall[:, lot.tiles[0]:lot.tiles[0] + lot.count]
                else:
                    src = x
                    if r == 0:
                        pe.wait_ge(x_loaded, 16 * lot.v)
                pe.wait_ge(x_staged, free(lot.v * ROUNDS + r))
                for c in range(DC):
                    for t in range(2):
                        last = pe.transpose(ps[:, XB, (2 * c + t) * P:(2 * c + t + 1) * P], src[:, 2 * r + t, c * P:(c + 1) * P], m["ident"][:])
                last.then_inc(x_turned, 1)

            def first(lot, u):
                v, c, half = lot.v, u // 2, u % 2
                t0, n = lot.first_row[half], lot.rows[half]
                if half == 0:
                    pe.wait_ge(w_cut, ready(v * FC1 + c, 2))
                if c == 0:
                    pe.wait_ge(x_cut, ready(v * 2 + half))
                pe.wait_ge(mixed, free(v * UN + u))
                for b, bank in enumerate((AB, BB)):
                    for d in range(DC):
                        for q, (pw, px) in enumerate(PASSES):
                            last = pe.matmul(ps[:, bank + u % 2, 0:n], wp[:, c % 2, pw, (b * DC + d) * P:(b * DC + d + 1) * P],
                                             xT[:, px, d, t0:t0 + n], start=d == 0 and q == 0, stop=d == DC - 1 and q == len(PASSES) - 1)
                last.then_inc(first_done, 1)

            def second(lot, u):
                v, c, half = lot.v, u // 2, u % 2
                pe.wait_ge(hid_cut, ready(v * UN + u))
                if u == 0:
                    for taken in y_taken:
                        pe.wait_ge(taken, before(v))
                for t in range(lot.count // 2):
                    tile = half * (lot.count // 2) + t
                    rows = min(P, lot.rows[half] - t * P)
                    out = ps[0:rows, YB + tile // 2, tile % 2 * D:(tile % 2 + 1) * D]
                    for q, (pw, px) in enumerate(PASSES):
                        last = pe.matmul(out, hidp[:, u % 2, px, t * P:t * P + rows], wp[:, c % 2, pw, 2 * DC * P:],
                                         start=c == 0 and q == 0 and tile % 2 == 0, stop=c == FC1 - 1 and q == len(PASSES) - 1,
                                         skip_group_check=True)
                last.then_inc(second_done, 1)

            for r in rounds_of(START):
                turn(START, r)

            def body(lot, row, following, previous):
                for u in range(UN):
                    first(lot, u)
                    if u:
                        second(lot, u - 1)
                    elif previous:
                        second(previous, UN - 1)
                    if turns(lot, u, following) is not None:
                        turn(following, turns(lot, u, following))
                if not following:
                    second(lot, UN - 1)

            lots(pe, body)


def two_layers(nc, a, out, stop=99):
    with ExitStack() as ctx:
        m = alloc(nc, ctx)
        xe0 = nc.dram_tensor("rows0", (ROWS0, D), F32, kind="Internal").ap()
        xe1 = nc.dram_tensor("rows1", (ROWS1, D), F32, kind="Internal").ap()
        ye0 = nc.dram_tensor("done0", (ROWS0, D), F32, kind="Internal").ap()
        ye1 = nc.dram_tensor("done1", (E1 * CAP, D), F32, kind="Internal").ap()
        W = [{n: a[f"{n}_{layer}"] for n in ("Wq", "Wk", "Wv", "Wo", "bq", "bk", "bv", "bo") if f"{n}_{layer}" in a} for layer in range(2)]
        parts = [nc.dram_tensor(f"parts_{layer}", (2, PARTS, D, T), BF16, kind="Internal").ap() for layer in range(2)]
        setup_block(nc, m)
        stack_shape = [KS, 2, H, S]
        with nc.sbuf_tensor("vals_0", [P, NT, H, DK], F32) as vals, nc.sbuf_tensor("qs_0", stack_shape, BF16) as qs, \
                nc.sbuf_tensor("ks_0", stack_shape, BF16) as ks, nc.sbuf_tensor("shut", [P, 2, B, TPB, S], BF16) as shut:
            if stop > 1:
                project_block(nc, m, 0, W[0], parts[0], q_from=(a["x"], None), kv_from=a["ctxT"], vals=vals, stacks=(qs, ks),
                              masks=(a["mask"], a["maskT"], shut))
            if stop > 2:
                attend_block(nc, m, 0, W[0], shut, parts[0], (qs, ks), vals, (xe0, xe1))
        if stop > 3:
            with nc.sbuf_tensor("vals_1", [P, NT, H, DK], F32) as vals:
                with nc.sbuf_tensor("hall_0", [P, NT, D], F32) as hall:
                    route_block(nc, m, 0, E0, a, hall)
                    project_block(nc, m, 1, W[1], parts[1], kv_from=a["ctxT"], vals=vals, scatter=(hall, xe0))
                experts0_block(nc, m, a, xe0, ye0)
                with nc.sbuf_tensor("qs_1", stack_shape, BF16) as qs, nc.sbuf_tensor("ks_1", stack_shape, BF16) as ks:
                    project_block(nc, m, 1, W[1], parts[1], q_from=(None, ye0), stacks=(qs, ks))
                    if stop > 5:
                        attend_block(nc, m, 1, W[1], None, parts[1], (qs, ks), vals, ())
        if stop > 6:
            with nc.sbuf_tensor("hall_1", [P, NT, D], F32) as hall:
                route_block(nc, m, 1, E1, a, hall)
                experts1_block(nc, m, a, hall, xe1, ye1, out)
        if stop < 8:
            store_block(nc, m, out)


def store_block(nc, m, out):
    with ExitStack() as ctx:
        out_stored = ctx.enter_context(signals(nc, m["resting"]))("out_stored")
        block = ctx.enter_context(nc.Block())

        @block.sync
        def _(sp):
            sp.dma_start(out.rearrange("(n p) d -> p n d", p=P), m["xres"][:]).then_inc(out_stored, 16)
            sp.wait_ge(out_stored, 16)


def lay_out(i):
    c = np.ascontiguousarray
    mask = i["mask_BxSxS2_bf0"]
    a = {
        "x": i["x"].reshape(T, D),
        "ctxT": c(i["ctx_1024"].reshape(T, D).T),
        "mask": mask,
        "maskT": c(mask.transpose(0, 2, 1)),
        "Wq_0": c(i["L0_xattn_Wq"].T), "Wk_0": c(i["L0_xattn_Wk"].T), "Wv_0": c(i["L0_xattn_Wv"].T),
        "Wo_0": c(i["L0_xattn_Wout"].T), "bo_0": i["L0_xattn_b_out"],
        "Wq_1": i["L1_xattn_Wq"], "Wk_1": i["L1_xattn_Wk"], "Wv_1": i["L1_xattn_Wv"], "Wo_1": i["L1_xattn_Wo"],
        "bq_1": i["L1_xattn_bq"], "bk_1": i["L1_xattn_bk"], "bv_1": i["L1_xattn_bv"], "bo_1": i["L1_xattn_bo"],
        "Wg": i["L0_ffn_Wg"], "bg": i["L0_ffn_bg"], "bias": i["L0_ffn_bias"],
        "W_0": c(np.concatenate([
            i["L0_ffn_W1"].reshape(E0, DC, P, F0).transpose(0, 2, 1, 3).reshape(E0, P, DC * F0),
            i["L0_ffn_W2"].reshape(E0, FC0, P, D).transpose(0, 2, 1, 3).reshape(E0, P, FC0 * D)], axis=2)),
        "b1": c(i["L0_ffn_b1"].reshape(E0, FC0, P).transpose(2, 0, 1)),
        "b2": i["L0_ffn_b2"],
        "ln_g": i["L1_ffn_ln_g"], "ln_b": i["L1_ffn_ln_b"], "Wr": i["L1_ffn_Wr"],
    }
    w1, w3, w2 = (np.concatenate([i[f"L1_ffn_W{n}s"][None], i[f"L1_ffn_W{n}"], i[f"L1_ffn_W{n}s"][None]]) for n in (1, 3, 2))
    w1, w3 = (w.reshape(E1 + 2, DC, P, FC1, P).transpose(0, 3, 2, 1, 4).reshape(E1 + 2, FC1, P, DC * P) for w in (w1, w3))
    a["W_1"] = c(np.concatenate([w1, w3, w2.reshape(E1 + 2, FC1, P, D)], axis=3))
    return {k: c(v) for k, v in a.items()}


def kernel(**inputs):
    from concourse import bacc
    from concourse.bass_utils import run_bass_kernel_spmd

    nc = bacc.Bacc("TRN2", target_bir_lowering=False, num_devices=1)
    arrays = lay_out({k: np.asarray(v) for k, v in inputs.items()})
    args = {k: nc.dram_tensor(f"in_{k}", v.shape, mybir.dt.from_np(v.dtype), kind="ExternalInput").ap() for k, v in arrays.items()}
    out = nc.dram_tensor("out", (T, D), F32, kind="ExternalOutput").ap()
    two_layers(nc, args, out)
    r = run_bass_kernel_spmd(nc, [{f"in_{k}": v for k, v in arrays.items()}], core_ids=[0])
    return r.results[0]["out"].reshape(B, S, D)
```
